# Optimizing a Trainium2 kernel written in Bass

```python
import numpy as np
import jax
import jax.numpy as jnp

def _softmax(x, axis=-1):
    return jax.nn.softmax(x, axis=axis)

def _gelu(x):
    return jax.nn.gelu(x, approximate=True)

def _silu(x):
    return jax.nn.silu(x)

def _sigmoid(x):
    return jax.nn.sigmoid(x)

def _layernorm(x, axis=-1, eps=1e-05):
    m = jnp.mean(x, axis=axis, keepdims=True)
    v = jnp.var(x, axis=axis, keepdims=True)
    return (x - m) / jnp.sqrt(v + eps)

def _scatter_add(tgt, idx, src, axis=0):
    return tgt.at[idx].add(src)

def _segment_sum(src, seg, n):
    return jax.ops.segment_sum(src, seg, n)
kernel_name = 'mk_seq_preln_d2_jaxref_r8_66c55d'

def setup_inputs(seed: int=0):
    np.random.seed(seed)
    _w = jnp.asarray

    def _L0_attn_setup():
        import jax, jax.numpy as jnp
        import numpy as np
        B, T, C, H = (4, 256, 128, 16)

        def _wkv(k, v, time_decay, time_first):
            b, t, c = k.shape
            h = time_decay.shape[0]
            d = c // h
            k = k.reshape(b, t, h, d).transpose(1, 0, 2, 3)
            v = v.reshape(b, t, h, d).transpose(1, 0, 2, 3)
            ew = jnp.exp(-jnp.exp(time_decay))[None, :, None]
            u = time_first[None, :, None]

            def step(carry, kv):
                sa, sb = carry
                kt, vt = kv
                eu = jnp.exp(u + kt)
                num = sa + eu * vt
                den = sb + jnp.maximum(eu.sum(-1, keepdims=True), 1e-06)
                ek = jnp.exp(kt)
                new_sa = ew * sa + ek * vt
                new_sb = ew * sb + ek.sum(-1, keepdims=True)
                return ((new_sa, new_sb), num / den)
            sa0 = jnp.zeros((b, h, d), k.dtype)
            sb0 = jnp.zeros((b, h, 1), k.dtype)
            _, out = jax.lax.scan(step, (sa0, sb0), (k, v))
            return out.transpose(1, 0, 2, 3).reshape(b, t, c)
        key = jax.random.key(seed)
        ks = jax.random.split(key, 8)
        scale = C ** (-0.5)
        return {'x': jax.random.normal(ks[0], (B, T, C), jnp.float32), 'mix_k': jnp.full((1, 1, C), 0.5, jnp.float32), 'mix_v': jnp.full((1, 1, C), 0.5, jnp.float32), 'mix_r': jnp.full((1, 1, C), 0.5, jnp.float32), 'Wk': jax.random.normal(ks[1], (C, C), jnp.float32) * scale, 'Wv': jax.random.normal(ks[2], (C, C), jnp.float32) * scale, 'Wr': jax.random.normal(ks[3], (C, C), jnp.float32) * scale, 'Wo': jax.random.normal(ks[4], (C, C), jnp.float32) * scale, 'time_decay': jax.random.normal(ks[5], (H,), jnp.float32) - 5.0, 'time_first': jax.random.normal(ks[6], (H,), jnp.float32)}
    _L0_attn_in = _L0_attn_setup()

    def _L0_ffn_setup():
        import jax, jax.numpy as jnp
        import numpy as np
        DIM = 128
        HIDDEN = 384
        SCALE = 1.0 / 127.0

        def _dequant(w_int, dtype):
            return w_int.astype(dtype) * jnp.asarray(SCALE, dtype)
        key = jax.random.key(seed)
        k_x, k_g, k_u, k_d = jax.random.split(key, 4)
        x = jax.random.normal(k_x, (4, 256, DIM), dtype=jnp.float32)
        w_gate = jax.random.randint(k_g, (HIDDEN, DIM), -127, 128, dtype=jnp.int32)
        w_up = jax.random.randint(k_u, (HIDDEN, DIM), -127, 128, dtype=jnp.int32)
        w_down = jax.random.randint(k_d, (DIM, HIDDEN), -127, 128, dtype=jnp.int32)
        return {'x': x, 'w_gate': w_gate, 'w_up': w_up, 'w_down': w_down}
    _L0_ffn_in = _L0_ffn_setup()

    def _L1_attn_setup():
        import jax, jax.numpy as jnp
        import numpy as np
        D_MODEL, N_HEADS = (128, 16)
        D_H = D_MODEL // N_HEADS
        D_HR = D_H // 2
        D_LATENT = 32
        THETA = 10000.0

        def rope(x, theta=THETA):
            S, d = (x.shape[-2], x.shape[-1])
            inv = theta ** (-jnp.arange(0, d, 2, dtype=jnp.float32) / d)
            ang = jnp.arange(S, dtype=jnp.float32)[:, None] * inv
            cos, sin = (jnp.cos(ang), jnp.sin(ang))
            x1, x2 = (x[..., 0::2], x[..., 1::2])
            r1 = x1 * cos - x2 * sin
            r2 = x1 * sin + x2 * cos
            return jnp.stack([r1, r2], axis=-1).reshape(x.shape)
        key = jax.random.key(seed)
        ks = jax.random.split(key, 9)
        s = lambda fan_in: 1.0 / np.sqrt(fan_in)
        return {'x': jax.random.normal(ks[0], (4, 256, D_MODEL), jnp.float32), 'W_DQ': jax.random.normal(ks[1], (D_MODEL, D_LATENT), jnp.float32) * s(D_MODEL), 'W_UQ': jax.random.normal(ks[2], (D_LATENT, N_HEADS * D_H), jnp.float32) * s(D_LATENT), 'W_QR': jax.random.normal(ks[3], (D_LATENT, N_HEADS * D_HR), jnp.float32) * s(D_LATENT), 'W_DKV': jax.random.normal(ks[4], (D_MODEL, D_LATENT), jnp.float32) * s(D_MODEL), 'W_UK': jax.random.normal(ks[5], (D_LATENT, N_HEADS * D_H), jnp.float32) * s(D_LATENT), 'W_UV': jax.random.normal(ks[6], (D_LATENT, N_HEADS * D_H), jnp.float32) * s(D_LATENT), 'W_KR': jax.random.normal(ks[7], (D_MODEL, D_HR), jnp.float32) * s(D_MODEL), 'W_O': jax.random.normal(ks[8], (N_HEADS * D_H, D_MODEL), jnp.float32) * s(N_HEADS * D_H)}
    _L1_attn_in = _L1_attn_setup()

    def _L1_ffn_setup():
        import jax, jax.numpy as jnp
        import numpy as np
        B, L, D = (4, 128, 128)
        E, H = (8, 512)
        CAPACITY = 6
        key = jax.random.key(seed)
        ks = jax.random.split(key, 6)
        x = jax.random.normal(ks[0], (B, L, D), dtype=jnp.float32)
        gate_weight = jax.random.normal(ks[1], (E, D), dtype=jnp.float32) * 0.006
        w1 = jax.random.normal(ks[2], (E, H, D), dtype=jnp.float32) * 0.02
        b1 = jnp.zeros((E, H), dtype=jnp.float32)
        w2 = jax.random.normal(ks[3], (E, D, H), dtype=jnp.float32) * 0.02
        b2 = jnp.zeros((E, D), dtype=jnp.float32)
        return {'x': x, 'gate_weight': gate_weight, 'w1': w1, 'b1': b1, 'w2': w2, 'b2': b2}
    _L1_ffn_in = _L1_ffn_setup()
    _d = {'L0_attn_x': _L0_attn_in['x'], 'L0_attn_mix_k': _L0_attn_in['mix_k'], 'L0_attn_mix_v': _L0_attn_in['mix_v'], 'L0_attn_mix_r': _L0_attn_in['mix_r'], 'L0_attn_Wk': _L0_attn_in['Wk'], 'L0_attn_Wv': _L0_attn_in['Wv'], 'L0_attn_Wr': _L0_attn_in['Wr'], 'L0_attn_Wo': _L0_attn_in['Wo'], 'L0_attn_time_decay': _L0_attn_in['time_decay'], 'L0_attn_time_first': _L0_attn_in['time_first'], 'L0_ffn_w_gate': _L0_ffn_in['w_gate'], 'L0_ffn_w_up': _L0_ffn_in['w_up'], 'L0_ffn_w_down': _L0_ffn_in['w_down'], 'L1_attn_W_DQ': _L1_attn_in['W_DQ'], 'L1_attn_W_UQ': _L1_attn_in['W_UQ'], 'L1_attn_W_QR': _L1_attn_in['W_QR'], 'L1_attn_W_DKV': _L1_attn_in['W_DKV'], 'L1_attn_W_UK': _L1_attn_in['W_UK'], 'L1_attn_W_UV': _L1_attn_in['W_UV'], 'L1_attn_W_KR': _L1_attn_in['W_KR'], 'L1_attn_W_O': _L1_attn_in['W_O'], 'L1_ffn_gate_weight': _L1_ffn_in['gate_weight'], 'L1_ffn_w1': _L1_ffn_in['w1'], 'L1_ffn_b1': _L1_ffn_in['b1'], 'L1_ffn_w2': _L1_ffn_in['w2'], 'L1_ffn_b2': _L1_ffn_in['b2']}
    _x0 = _d['L0_attn_x']
    _d['L0_attn_x'] = jax.random.normal(jax.random.fold_in(jax.random.key(seed), 1), (16, 256, 128), dtype=_x0.dtype)
    del _x0
    return _d

def reference(L0_attn_x, L0_attn_mix_k, L0_attn_mix_v, L0_attn_mix_r, L0_attn_Wk, L0_attn_Wv, L0_attn_Wr, L0_attn_Wo, L0_attn_time_decay, L0_attn_time_first, L0_ffn_w_gate, L0_ffn_w_up, L0_ffn_w_down, L1_attn_W_DQ, L1_attn_W_UQ, L1_attn_W_QR, L1_attn_W_DKV, L1_attn_W_UK, L1_attn_W_UV, L1_attn_W_KR, L1_attn_W_O, L1_ffn_gate_weight, L1_ffn_w1, L1_ffn_b1, L1_ffn_w2, L1_ffn_b2):

    def _L0_attn_ref(x, mix_k, mix_v, mix_r, Wk, Wv, Wr, Wo, time_decay, time_first):
        import jax, jax.numpy as jnp
        import numpy as np
        B, T, C, H = (4, 256, 128, 16)

        def _wkv(k, v, time_decay, time_first):
            b, t, c = k.shape
            h = time_decay.shape[0]
            d = c // h
            k = k.reshape(b, t, h, d).transpose(1, 0, 2, 3)
            v = v.reshape(b, t, h, d).transpose(1, 0, 2, 3)
            ew = jnp.exp(-jnp.exp(time_decay))[None, :, None]
            u = time_first[None, :, None]

            def step(carry, kv):
                sa, sb = carry
                kt, vt = kv
                eu = jnp.exp(u + kt)
                num = sa + eu * vt
                den = sb + jnp.maximum(eu.sum(-1, keepdims=True), 1e-06)
                ek = jnp.exp(kt)
                new_sa = ew * sa + ek * vt
                new_sb = ew * sb + ek.sum(-1, keepdims=True)
                return ((new_sa, new_sb), num / den)
            sa0 = jnp.zeros((b, h, d), k.dtype)
            sb0 = jnp.zeros((b, h, 1), k.dtype)
            _, out = jax.lax.scan(step, (sa0, sb0), (k, v))
            return out.transpose(1, 0, 2, 3).reshape(b, t, c)
        x_prev = jnp.pad(x, ((0, 0), (1, 0), (0, 0)))[:, :-1]
        k = (x * mix_k + x_prev * (1.0 - mix_k)) @ Wk.T
        v = (x * mix_v + x_prev * (1.0 - mix_v)) @ Wv.T
        r = jax.nn.sigmoid((x * mix_r + x_prev * (1.0 - mix_r)) @ Wr.T)
        wkv = _wkv(k, v, time_decay, time_first)
        return r * wkv @ Wo.T

    def _L0_ffn_ref(x, w_gate, w_up, w_down):
        import jax, jax.numpy as jnp
        import numpy as np
        DIM = 128
        HIDDEN = 384
        SCALE = 1.0 / 127.0

        def _dequant(w_int, dtype):
            return w_int.astype(dtype) * jnp.asarray(SCALE, dtype)
        wg = _dequant(w_gate, x.dtype)
        wu = _dequant(w_up, x.dtype)
        wd = _dequant(w_down, x.dtype)
        gate = jnp.einsum('bsd,hd->bsh', x, wg)
        up = jnp.einsum('bsd,hd->bsh', x, wu)
        h = jax.nn.silu(gate) * up
        return jnp.einsum('bsh,dh->bsd', h, wd)

    def _L1_attn_ref(x, W_DQ, W_UQ, W_QR, W_DKV, W_UK, W_UV, W_KR, W_O):
        import jax, jax.numpy as jnp
        import numpy as np
        D_MODEL, N_HEADS = (128, 16)
        D_H = D_MODEL // N_HEADS
        D_HR = D_H // 2
        D_LATENT = 32
        THETA = 10000.0

        def rope(x, theta=THETA):
            S, d = (x.shape[-2], x.shape[-1])
            inv = theta ** (-jnp.arange(0, d, 2, dtype=jnp.float32) / d)
            ang = jnp.arange(S, dtype=jnp.float32)[:, None] * inv
            cos, sin = (jnp.cos(ang), jnp.sin(ang))
            x1, x2 = (x[..., 0::2], x[..., 1::2])
            r1 = x1 * cos - x2 * sin
            r2 = x1 * sin + x2 * cos
            return jnp.stack([r1, r2], axis=-1).reshape(x.shape)
        B, S, _ = x.shape
        d_qk = D_H + D_HR
        c_q = x @ W_DQ
        Qc = (c_q @ W_UQ).reshape(B, S, N_HEADS, D_H).transpose(0, 2, 1, 3)
        Qr = (c_q @ W_QR).reshape(B, S, N_HEADS, D_HR).transpose(0, 2, 1, 3)
        Qr = rope(Qr)
        c_kv = x @ W_DKV
        Kc = (c_kv @ W_UK).reshape(B, S, N_HEADS, D_H).transpose(0, 2, 1, 3)
        Kr = rope((x @ W_KR)[:, None, :, :])
        Kr = jnp.broadcast_to(Kr, (B, N_HEADS, S, D_HR))
        V = (c_kv @ W_UV).reshape(B, S, N_HEADS, D_H).transpose(0, 2, 1, 3)
        Q = jnp.concatenate([Qc, Qr], axis=-1)
        K = jnp.concatenate([Kc, Kr], axis=-1)
        scores = jnp.einsum('bhqd,bhkd->bhqk', Q, K)
        scores = jnp.clip(scores, -80.0, 80.0)
        causal = jnp.tril(jnp.ones((S, S), dtype=bool))
        scores = jnp.where(causal, scores, -jnp.inf)
        weights = jax.nn.softmax(scores / jnp.sqrt(jnp.float32(d_qk)), axis=-1)
        attn = jnp.einsum('bhqk,bhkd->bhqd', weights, V)
        attn = attn.transpose(0, 2, 1, 3).reshape(B, S, N_HEADS * D_H)
        return attn @ W_O

    def _L1_ffn_ref(x, gate_weight, w1, b1, w2, b2):
        import jax, jax.numpy as jnp
        import numpy as np
        B, L, D = (4, 128, 128)
        E, H = (8, 512)
        CAPACITY = 6
        logits = jnp.einsum('bld,ed->ble', x, gate_weight)
        expert_k = B * L * CAPACITY
        kth_val = jnp.sort(logits.reshape(-1))[expert_k - 1]
        mask = (logits >= kth_val).astype(x.dtype)
        gates = logits * mask
        h = jax.nn.gelu(jnp.einsum('bld,ehd->bleh', x, w1) + b1, approximate=True)
        y = jnp.einsum('bleh,edh->blde', h, w2) + b2.T[None, None]
        out = jnp.einsum('blde,ble->bld', y, gates)
        return out
    x = L0_attn_x
    x = x + _L0_attn_ref(_layernorm(x, axis=-1), L0_attn_mix_k, L0_attn_mix_v, L0_attn_mix_r, L0_attn_Wk, L0_attn_Wv, L0_attn_Wr, L0_attn_Wo, L0_attn_time_decay, L0_attn_time_first)
    x = x + _L0_ffn_ref(_layernorm(x, axis=-1), L0_ffn_w_gate, L0_ffn_w_up, L0_ffn_w_down)
    x = x + _L1_attn_ref(_layernorm(x, axis=-1), L1_attn_W_DQ, L1_attn_W_UQ, L1_attn_W_QR, L1_attn_W_DKV, L1_attn_W_UK, L1_attn_W_UV, L1_attn_W_KR, L1_attn_W_O)
    x = x + _L1_ffn_ref(_layernorm(x, axis=-1), L1_ffn_gate_weight, L1_ffn_w1, L1_ffn_b1, L1_ffn_w2, L1_ffn_b2)
    return x

_drawn_inputs = setup_inputs


def setup_inputs(seed=0):
    import zlib

    import numpy as np

    out = dict(_drawn_inputs(seed))
    spreads = {'L0_attn_mix_k': (0.5, 0.6),
     'L0_attn_mix_v': (0.5, 0.6),
     'L0_attn_mix_r': (0.5, 0.6),
     'L1_ffn_b1': (0.0, 2.0),
     'L1_ffn_b2': (0.0, 2.0)}
    factors = {'L0_attn_Wk': 4.348,
     'L0_attn_Wv': 2.731,
     'L0_attn_Wr': 8.0,
     'L0_attn_Wo': 2.776,
     'L0_attn_time_decay': 8.0,
     'L0_attn_time_first': 8.0,
     'L1_attn_W_DQ': 8.0,
     'L1_attn_W_UQ': 8.0,
     'L1_attn_W_QR': 8.0,
     'L1_attn_W_DKV': 8.0,
     'L1_attn_W_UK': 8.0,
     'L1_attn_W_UV': 8.0,
     'L1_attn_W_KR': 8.0,
     'L1_attn_W_O': 8.0,
     'L1_ffn_gate_weight': 25.11,
     'L1_ffn_w1': 32.274,
     'L1_ffn_w2': 25.975}
    for name, (base, spread) in spreads.items():
        noise = np.random.default_rng([zlib.crc32(name.encode()), seed]).standard_normal(out[name].shape)
        drawn = base * np.exp(spread * noise) if base else spread * noise
        out[name] = jnp.asarray(drawn.astype(out[name].dtype))
    for name, factor in factors.items():
        out[name] = (out[name] * factor).astype(out[name].dtype)
    return out
```

```python
from contextlib import ExitStack

import concourse.bass as bass
import numpy as np
from concourse import mybir

F32 = mybir.dt.float32
R32 = mybir.dt.float32r
I32 = mybir.dt.int32
ALU = mybir.AluOpType
ACT = mybir.ActivationFunctionType

P = 128
BATCH, T, C = 16, 256, 128
N = BATCH * T
BLK = N // P
TILE = 512
NT = N // TILE
TB = TILE // P
SEQS = TILE // T
HEADS, DH, DR = 16, 8, 4
GROUPS = HEADS // 4
SLOT = 32
HIDDEN = 384
FJ = HIDDEN // P
EXPERTS, HE = 8, 512
EC = HE // P
CHUNKS = EXPERTS * EC
MT = 1024
NMT = N // MT
KTH = 4 * 128 * 6
PAIRS = N * EXPERTS
EPS = 1e-5
CLIP = 80.0
MASKED = -1.0e4
ROPE = 8
SLOT_COLS = DH + ROPE * (DR // 2)
Q_DIM = [0, 0, 1, 1, 0, 0, 1, 1]
K_DIM = [0, 1, 0, 1, 0, 1, 0, 1]
Q_SIN = [0, 0, 1, 1, 1, 1, 0, 0]
K_SIN = [0, 1, 0, 1, 1, 0, 1, 0]
SIGN = [1, -1, -1, 1, 1, 1, 1, 1]

RAW = 2048
PIECES = CHUNKS * P // RAW
ARENA = 23600

W_K, W_V, W_R, W_O0 = 0, 128, 256, 384
W_O1 = 512
W_KROPE = 640
W_COLS = W_KROPE + GROUPS * P
V_MK, V_MV, V_MR, V_DECAY, V_FIRST = range(5)
V_GATE = 5
V_B1 = V_GATE + EXPERTS
V_B2 = V_B1 + CHUNKS
V_COLS = V_B2 + EXPERTS
L_DQ, L_UQ, L_DKV, L_UK, L_UV = 0, 128, 640, 768, 1280
L_COLS = 1408
C_ID, C_ONES, C_HEAD = 0, 128, 256
C_TABQ, C_TABK = 384, 384 + T
C_LIM = 384 + 2 * T
C_COLS = C_LIM + 384


def rope_tables():
    out = np.zeros((P, C_COLS), np.float32)
    out[:, C_ID:C_ID + P] = np.eye(P)
    out[:, C_ONES:C_ONES + P] = 1.0
    for h in range(HEADS):
        out[h * DH:h * DH + DH, C_HEAD + h * DH:C_HEAD + h * DH + DH] = 1.0
    inv = np.float32(10000.0) ** (-np.arange(0, DR, 2, dtype=np.float32) / np.float32(DR))
    ang = np.arange(T, dtype=np.float32)[:, None] * inv
    trig = [np.cos(ang.astype(np.float64)), np.sin(ang.astype(np.float64))]
    for q in range(4):
        out[SLOT * q:SLOT * q + DH, C_TABQ:C_TABQ + T] = 1.0
        out[SLOT * q:SLOT * q + DH, C_TABK:C_TABK + T] = 1.0
        for p in range(DR // 2):
            for k in range(ROPE):
                row = SLOT * q + DH + ROPE * p + k
                out[row, C_TABQ:C_TABQ + T] = SIGN[k] * trig[Q_SIN[k]][:, p]
                out[row, C_TABK:C_TABK + T] = trig[K_SIN[k]][:, p]
    own = np.where(np.arange(P)[None, :] >= np.arange(P)[:, None], CLIP, MASKED)
    out[:, C_LIM:C_LIM + 384] = np.concatenate([own, np.full((P, P), CLIP), own], 1)
    return out


def build(nc, x_in, weights, vectors, latent, ints, w1_in, w2_in, consts, out):
    with ExitStack() as ctx:
        def sb(name, shape, dt=F32):
            return ctx.enter_context(nc.sbuf_tensor(name, shape, dt))

        def sem(name):
            return ctx.enter_context(nc.semaphore(name))

        ps = ctx.enter_context(nc.psum_tensor("ps", [P, 8, 512], F32))
        logits_dram = nc.dram_tensor("logits_scratch", [EXPERTS, N], F32, kind="Internal").ap()
        gates_dram = nc.dram_tensor("gates_scratch", [P, PAIRS // P], F32, kind="Internal").ap()

        x = sb("x", [P, BLK + TB, C])
        cst = sb("cst", [P, C_COLS])
        wts = sb("wts", [P, W_COLS])
        vec = sb("vec", [P, V_COLS])
        lat = sb("lat", [32, L_COLS])
        ident = cst[:, C_ID:C_ID + P]
        ones = cst[:, C_ONES:C_ONES + P]
        w1h = sb("w1h", [P, CHUNKS * P], R32)
        w1l = sb("w1l", [P, CHUNKS * P], R32)
        w2h = sb("w2h", [P, CHUNKS * P], R32)
        w2l = sb("w2l", [P, CHUNKS * P], R32)
        stats = sb("stats", [P, 2, TB, 6])
        moments = sb("moments", [P, 2, TB, 2])
        vareps = sb("vareps", [P, 2, TB])
        minus_half = sb("minus_half", [P, TB])
        rstd = sb("rstd", [P, 2, TB])
        xn = sb("xn", [P, 2, TB, C])
        wq = sb("wq", [P, GROUPS * P])
        wk = sb("wk", [P, GROUPS * P])
        wv = sb("wv", [P, P])
        gate_hi = sb("gate_hi", [P, EXPERTS], R32)
        gate_lo = sb("gate_lo", [P, EXPERTS], R32)
        raw = sb("raw", [P, RAW])
        arena_at = nc.sbuf_base
        sb("arena", [P, ARENA])
        used = [0]

        def cut(name, cols, shape=None, dt=F32):
            a = nc.alloc_sbuf_tensor_at(name, [P, cols], dt, offset=arena_at + 4 * used[0])[:, :]
            used[0] += -(-cols // 8) * 8
            assert used[0] <= ARENA, used[0]
            return a if shape is None else a.rearrange(shape[0], **shape[1])

        xT = cut("xT", 2 * SEQS * (T + 1), ("p (a b t) -> p a b t", dict(a=2, b=SEQS)))
        other = cut("other", 3)
        wmix = cut("wmix", 3 * 2 * P, ("p (m a n) -> p m a n", dict(m=3, a=2)))
        decay = cut("decay", T)
        ew = cut("ew", 2)
        ek = cut("ek", 2 * TILE, ("p (a t) -> p a t", dict(a=2)))
        eu = cut("eu", 2 * TILE, ("p (a t) -> p a t", dict(a=2)))
        th = cut("th", 2 * TILE, ("p (a t) -> p a t", dict(a=2)))
        kv = cut("kv", TILE)
        nu = cut("nu", TILE)
        sa = cut("sa", SEQS * (T + 1), ("p (b t) -> p b t", dict(b=SEQS)))
        sden = cut("sden", SEQS * (T + 1), ("p (b t) -> p b t", dict(b=SEQS)))
        num = cut("num", TILE)
        den = cut("den", TILE)
        rec = cut("rec", TILE)
        wkv = cut("wkv", TILE)
        gated = cut("gated", 2 * TILE, ("p (a t) -> p a t", dict(a=2)))
        int_raw = cut("int_raw", 3 * HIDDEN, None, I32)
        wgu = cut("wgu", 2 * HIDDEN, None, R32)
        wdn = cut("wdn", HIDDEN)
        fxh = cut("fxh", 2 * TILE, ("p (a t) -> p a t", dict(a=2)), R32)
        fxl = cut("fxl", 2 * TILE, ("p (a t) -> p a t", dict(a=2)), R32)
        ft = cut("ft", FJ * TILE, ("p (j t) -> p j t", dict(j=FJ)))
        fu = cut("fu", FJ * TILE, ("p (j t) -> p j t", dict(j=FJ)))
        fh = cut("fh", 2 * FJ * TILE, ("p (a j t) -> p a j t", dict(a=2, j=FJ)))
        used[0] = 0
        ax = cut("ax", 2 * TILE, ("p (a t) -> p a t", dict(a=2)))
        qs = cut("qs", 2 * GROUPS * TILE, ("p (a g t) -> p a g t", dict(a=2, g=GROUPS)))
        ks = cut("ks", 2 * GROUPS * TILE, ("p (a g t) -> p a g t", dict(a=2, g=GROUPS)))
        vx = cut("vx", 2 * TB * HEADS * SLOT, ("p (a n h s) -> p a n h s", dict(a=2, n=TB, h=HEADS)))
        cl = cut("cl", 2 * 2 * 384, ("p (a h t) -> p a h t", dict(a=2, h=2)))
        pr = cut("pr", 4 * 2 * 384, ("p (a h t) -> p a h t", dict(a=4, h=2)))
        ot = cut("ot", 2 * SEQS * GROUPS * T, ("p (a b g t) -> p a b g t", dict(a=2, b=SEQS, g=GROUPS)))
        otok = cut("otok", P, ("p (h d) -> p h d", dict(h=HEADS)))
        oden = cut("oden", HEADS)
        oT = cut("oT", P)
        used[0] = 0
        xh = cut("xh", N, None, R32)
        xl = cut("xl", N, None, R32)
        h32 = cut("h32", 2 * MT, ("p (a t) -> p a t", dict(a=2)))
        hh = cut("hh", 2 * MT, ("p (a t) -> p a t", dict(a=2)), R32)
        hl = cut("hl", 2 * MT, ("p (a t) -> p a t", dict(a=2)), R32)
        gbc = cut("gbc", 2 * MT, ("p (a t) -> p a t", dict(a=2)))
        gy = cut("gy", MT)
        acc = cut("acc", MT)
        yout = cut("yout", MT, ("p (n c) -> p n c", dict(n=MT // P)))
        lgT = cut("lgT", 2 * TILE, ("p (a t) -> p a t", dict(a=2)))
        lg = cut("lg", PAIRS // P)
        z = cut("z", PAIRS // P)
        zs = cut("zs", PAIRS // P)
        small = cut("small", 16)

        consts_in, weights_in, x_first_in, x_rest_in = sem("consts_in"), sem("weights_in"), sem("x_first_in"), sem("x_rest_in")
        ints_in, raw_in = sem("ints_in"), sem("expert_weights_piece_in")
        setup = sem("vector_setup_steps")
        pool_setup = sem("pool_setup_steps")
        act_setup = sem("act_setup_steps")
        w_split = sem("expert_weights_split_steps")
        m_half = sem("p4_out_half")
        passed = sem("vector_passed")
        w_gw = sem("gate_weights_split_steps")

        class Norm:

            def __init__(self, name):
                self.chain = sem(name + "_stats_steps")
                self.rstd = sem(name + "_rstd_ready")
                self.ready = sem(name + "_xn_ready")
                self.turned = sem(name + "_xn_turned")

        norms = [Norm(f"norm{i}") for i in range(1, 5)]
        CH = 2 * TB + 1

        def tile_steps(eng, body, extra):
            for s in range(extra):
                body(s, s % 2)
            with eng.Fori(0, (NT - extra) // 2) as i:
                body(2 * i + extra, extra % 2)
                body(2 * i + extra + 1, (extra + 1) % 2)
            for s in range(NT, NT + extra):
                body(s, s % 2)

        def live(t):
            return not isinstance(t, int) or 0 <= t < NT

        def blocks(t):
            return x[:, bass.ds(t * TB, TB), :] if not isinstance(t, int) else x[:, t * TB:(t + 1) * TB, :]

        def norm_stats(dve, norm, t, par, resid):
            if isinstance(t, int) and t > NT:
                return
            for wait, value in resid:
                dve.wait_ge(wait, value)
            xt = blocks(t)
            for j in range(TB):
                dve.bn_stats(stats[:, par, j, :], xt[:, j, :]).then_inc(norm.chain, 1)
            dve.wait_ge(norm.chain, t * CH + TB)
            dve.sem_inc(passed, 1)
            for j in range(TB):
                dve.bn_aggr(moments[:, par, j, :], stats[:, par, j, :]).then_inc(norm.chain, 1)
            dve.wait_ge(norm.chain, t * CH + 2 * TB)
            dve.tensor_scalar(vareps[:, par, :], moments[:, par, :, 1], EPS, None, ALU.add).then_inc(norm.chain, 1)

        def norm_rstd(pool, norm, t, par):
            if isinstance(t, int) and t > NT:
                return
            pool.wait_ge(norm.chain, (t + 1) * CH)
            pool.tensor_tensor(rstd[:, par, :], vareps[:, par, :], minus_half[:, :], ALU.pow).then_inc(norm.rstd, 1)

        def norm_apply(dve, norm, t, par):
            if not live(t):
                return
            dve.wait_ge(norm.rstd, t + 1)
            if not isinstance(t, int) or t >= 2:
                dve.wait_ge(norm.turned, t - 1)
            xt = blocks(t)
            for j in range(TB):
                dve.tensor_scalar(xn[:, par, j, :], xt[:, j, :], moments[:, par, j, 0:1], rstd[:, par, j:j + 1],
                                  ALU.subtract, ALU.mult).then_inc(norm.ready, 1)

        def norm_turn(pe, norm, t, par, bank):
            pe.wait_ge(norm.ready, t * TB + TB)
            for j in range(TB):
                mm = pe.transpose(ps[:, bank, j * P:(j + 1) * P], xn[:, par, j, :], ident)
            mm.then_inc(norm.turned, 1)

        xT_ready, mix_steps = sem("p1_xT_ready"), sem("p1_weights_mixed")
        proj_done, act1, sums_done = sem("p1_projected"), sem("p1_activated"), sem("p1_head_sums_done")
        chain1, o_done, resid1 = sem("p1_vector_steps"), sem("p1_out_projected"), sem("p1_residual_added")
        C1 = 11
        f_hi, f_lo, fg_done, f_tanh = sem("p2_hi_ready"), sem("p2_lo_ready"), sem("p2_gate_up_done"), sem("p2_tanh_ready")
        chain2, f_h, f_down, resid2 = sem("p2_vector_steps"), sem("p2_hidden_ready"), sem("p2_down_done"), sem("p2_residual_added")
        comb = sem("p3_weights_combined")
        comb_copied = sem("p3_weights_copied")
        a_x, a_proj, a_qk, a_vdone, a_vready = sem("p3_xT_ready"), sem("p3_qk_projected"), sem("p3_qk_ready"), sem("p3_v_projected"), sem("p3_v_ready")
        a_s, a_cl, a_p, a_av, a_ot = sem("p3_scores_done"), sem("p3_clipped"), sem("p3_probs_ready"), sem("p3_av_done"), sem("p3_av_copied")
        a_f1, a_fd, a_ftok, a_f2, a_oT, a_wo, resid3 = (sem("p3_out_turned"), sem("p3_denominators"), sem("p3_out_normalised"),
                                                        sem("p3_out_turned_back"), sem("p3_outT_ready"), sem("p3_out_projected"), sem("p3_residual_added"))
        g_hi, g_lo, g_mm, g_copied, g_stored = sem("p4_hi_ready"), sem("p4_lo_ready"), sem("p4_logits_done"), sem("p4_logits_copied"), [sem("p4_logits_stored0"), sem("p4_logits_stored1")]
        g_loaded, s_steps, s_counted, gates_ready, gates_stored = (sem("search_loaded"), sem("search_vector_steps"), sem("search_counted"),
                                                                   sem("gates_ready"), sem("gates_stored"))
        gb_in = [sem("gates_rows_in0"), sem("gates_rows_in1")]
        m_w1, m_gelu, m_hi, m_lo, m_w2 = sem("p4_w1_done"), sem("p4_gelu_ready"), sem("p4_hidden_hi_ready"), sem("p4_hidden_lo_ready"), sem("p4_w2_done")
        m_gy, m_acc, m_turn, m_out, stored = sem("p4_gated"), sem("p4_summed"), sem("p4_turned"), sem("p4_out_ready"), sem("p4_out_stored")

        xv = x_in.rearrange("(n p) c -> p n c", p=P)
        outv = out.rearrange("(n p) c -> p n c", p=P)
        chunks_per_tile = CHUNKS

        block = ctx.enter_context(nc.Block())

        @block.sync
        def _(sp):
            sp.dma_start(x[:, 0:TB, :], xv[:, 0:TB, :]).then_inc(x_first_in, 16)
            sp.dma_start(cst[:, :], consts).then_inc(consts_in, 16)
            sp.dma_start(wts[:, :], weights).then_inc(weights_in, 16)
            sp.dma_start(vec[:, :], vectors).then_inc(weights_in, 16)
            sp.dma_start(x[:, TB:BLK, :], xv[:, TB:BLK, :]).then_inc(x_rest_in, 16)
            sp.dma_start(int_raw, ints).then_inc(ints_in, 16)
            sp.dma_start(lat[:, :], latent).then_inc(weights_in, 16)
            for i in range(2 * PIECES):
                if i:
                    sp.wait_ge(w_split, 2 * i)
                src = (w1_in, w2_in)[i // PIECES]
                sp.dma_start(raw[:, :], src[:, (i % PIECES) * RAW:(i % PIECES + 1) * RAW]).then_inc(raw_in, 16)

            def store_logits(s, par):
                sp.wait_ge(g_copied, s + 1)
                at = bass.ds(s * TILE, TILE) if not isinstance(s, int) else slice(s * TILE, (s + 1) * TILE)
                sp.dma_start(logits_dram[:, at], lgT[0:EXPERTS, par, :]).then_inc(g_stored[par], 16)
            for s in range(2):
                store_logits(s, s)
            with sp.Fori(1, NT // 2) as i:
                store_logits(2 * i, 0)
                store_logits(2 * i + 1, 1)
            for par in range(2):
                sp.wait_ge(g_stored[par], 16 * NT // 2)
            sp.dma_start(lg, logits_dram.rearrange("e (q t) -> (e q) t", t=PAIRS // P)).then_inc(g_loaded, 16)
            sp.wait_ge(gates_ready, 1)
            sp.dma_start(gates_dram, lg).then_inc(gates_stored, 16)
            sp.wait_ge(gates_stored, 16)
            rows = gates_dram.rearrange("(e q) t -> e (q t)", e=EXPERTS)

            def expert_gates(tt, e):
                if not (isinstance(tt, int) and tt == 0 and e < 2):
                    sp.wait_ge(m_gy, tt * EXPERTS + e - 1)
                at = bass.ds(tt * MT, MT) if not isinstance(tt, int) else slice(tt * MT, (tt + 1) * MT)
                sp.dma_start(gbc[:, e % 2, :], rows[e:e + 1, at].partition_broadcast(P)).then_inc(gb_in[e % 2], 16)

            def store_out(tt):
                sp.wait_ge(m_out, tt + 1)
                at = bass.ds(tt * (MT // P), MT // P) if not isinstance(tt, int) else slice(tt * (MT // P), (tt + 1) * (MT // P))
                sp.dma_start(outv[:, at, :], yout).then_inc(stored, 16)

            for e in range(EXPERTS):
                expert_gates(0, e)
            with sp.Fori(1, NMT) as tt:
                for e in range(EXPERTS):
                    expert_gates(tt, e)
                    if e == 3:
                        store_out(tt - 1)
            store_out(NMT - 1)
            sp.wait_ge(stored, 16 * NMT)

        @block.gpsimd
        def _(pool):
            pool.memset(minus_half[:, :], -0.5).then_inc(pool_setup, 1)
            for a in range(2):
                pool.memset(xT[:, a, :, 0:1], 0.0).then_inc(pool_setup, 1)
            pool.memset(x[:, BLK:BLK + TB, :], 0.0).then_inc(pool_setup, 1)
            pool.wait_ge(pool_setup, 4)
            norm_rstd(pool, norms[0], 0, 0)
            tile_steps(pool, lambda s, par: norm_rstd(pool, norms[0], s + 1, 1 - par), 2)
            for norm in norms[1:3]:
                norm_rstd(pool, norm, 0, 0)
                tile_steps(pool, lambda s, par: norm_rstd(pool, norm, s + 1, 1 - par), 2)
                if norm is norms[1]:
                    for i in range(2 * PIECES):
                        hi, lo = ((w1h, w1l), (w2h, w2l))[i // PIECES]
                        at = slice((i % PIECES) * RAW, (i % PIECES + 1) * RAW)
                        pool.wait_ge(raw_in, 16 * (i + 1))
                        pool.tensor_copy(hi[:, at], raw[:, :]).then_inc(w_split, 1)
                        pool.wait_ge(w_split, 2 * i + 1)
                        pool.tensor_tensor(lo[:, at], raw[:, :], hi[:, at].bitcast(F32), ALU.subtract).then_inc(w_split, 1)
            norm = norms[3]
            norm_rstd(pool, norm, 0, 0)
            tile_steps(pool, lambda s, par: norm_rstd(pool, norm, s + 1, 1 - par), 2)

        @block.scalar
        def _(act):
            act.wait_ge(weights_in, 48)
            act.activation(ew[:, 0:1], vec[:, V_DECAY:V_DECAY + 1], ACT.Exp).then_inc(act_setup, 1)
            act.wait_ge(act_setup, 1)
            act.activation(ew[:, 1:2], ew[:, 0:1], ACT.Exp, scale=-1.0).then_inc(act_setup, 1)
            act.wait_ge(pool_setup, 4)

            def phase1(s, par):
                if not live(s):
                    return
                act.wait_ge(norms[0].turned, s + 1)
                if not isinstance(s, int) or s >= 2:
                    act.wait_ge(proj_done, (s - 1) * 3)
                act.activation(xT[:, par, :, 1:T + 1], ps[:, 0, :].rearrange("p (b t) -> p b t", b=SEQS),
                               ACT.Copy).then_inc(xT_ready, 1)
                if not isinstance(s, int) or s >= 2:
                    act.wait_ge(chain1, (s - 1) * C1)
                act.wait_ge(proj_done, s * 3 + 1)
                act.activation(ek[:, par, :], ps[:, 1, :], ACT.Exp).then_inc(act1, 1)
                act.activation(eu[:, par, :], ps[:, 1, :], ACT.Exp, bias=vec[:, V_FIRST:V_FIRST + 1]).then_inc(act1, 1)
                act.wait_ge(proj_done, s * 3 + 3)
                act.activation(th[:, par, :], ps[:, 3, :], ACT.Tanh, scale=0.5).then_inc(act1, 1)

            tile_steps(act, phase1, 2)

            def phase2(s, par):
                if not live(s):
                    return
                act.wait_ge(norms[1].turned, s + 1)
                if not isinstance(s, int) or s >= 2:
                    act.wait_ge(fg_done, (s - 1) * FJ)
                act.activation(fxh[:, par, :], ps[:, 0, :], ACT.Copy).then_inc(f_hi, 1)
                for j in range(FJ):
                    act.wait_ge(fg_done, s * FJ + j + 1)
                    if not isinstance(s, int) or s >= 1:
                        act.wait_ge(chain2, (s - 1) * FJ + j + 1)
                    act.activation(ft[:, j, :], ps[:, 1 + 2 * j, :], ACT.Tanh, scale=0.5 / 127.0).then_inc(f_tanh, 1)

            tile_steps(act, phase2, 2)

            def phase3(s, par):
                if live(s):
                    act.wait_ge(norms[2].turned, s + 1)
                    if not isinstance(s, int) or s >= 2:
                        act.wait_ge(a_vdone, s - 1)
                        act.wait_ge(a_proj, (s - 1) * 8)
                    act.activation(ax[:, par, :], ps[:, 0, :], ACT.Copy).then_inc(a_x, 1)
                for u in range(8):
                    if live(s - 1):
                        k = (s - 1) * 8 + u
                        for half in range(2):
                            act.wait_ge(a_cl, 2 * k + half + 1)
                            slot = (2 * u + half) % 4
                            if not (isinstance(s, int) and s == 1 and u < 2):
                                act.wait_ge(a_av, k - 1)
                            act.activation(pr[:, slot, :, :], cl[:, half, :, :], ACT.Exp, scale=12.0 ** -0.5).then_inc(a_p, 1)
                    if u == 1 and live(s):
                        act.wait_ge(a_vdone, s + 1)
                        if not isinstance(s, int) or s >= 2:
                            act.wait_ge(a_av, (s - 1) * 8)
                        act.activation(vx[:, par, :, :, 0:DH], ps[:, 0, :].rearrange("p (n h d) -> p n h d", n=TB, h=HEADS),
                                       ACT.Copy).then_inc(a_vready, 1)
                    if live(s - 1) and u >= 1:
                        copy_av(s - 1, 1 - par, u - 1)
                    if live(s - 2):
                        if u in (3, 5, 7):
                            copy_oT(s - 2, (u - 3) // 2, u)
                if live(s - 1):
                    copy_av(s - 1, 1 - par, 7)
                if live(s - 2):
                    copy_oT(s - 2, 3, 8)

            def copy_av(t, par, u):
                act.wait_ge(a_av, t * 8 + u + 1)
                if u == 0 and not (isinstance(t, int) and t < 2):
                    act.wait_ge(a_f1, (t - 1) * 4)
                act.activation(ot[:, par, u // 4, u % 4, :], ps[:, 6 + u % 2, 0:T], ACT.Copy).then_inc(a_ot, 1)

            def copy_oT(t, q, u):
                act.wait_ge(a_f2, t * 4 + q + 1)
                if not (isinstance(t, int) and t == 0 and q == 0):
                    act.wait_ge(a_wo, t * 4 + q)
                act.activation(oT, ps[:, 0, 0:P], ACT.Copy).then_inc(a_oT, 1)

            tile_steps(act, phase3, 2)

            act.wait_ge(resid3, NT * TB)

            def logits(s, par):
                if not live(s):
                    return
                act.wait_ge(norms[3].turned, s + 1)
                at = bass.ds(s * TILE, TILE) if not isinstance(s, int) else slice(s * TILE, (s + 1) * TILE)
                act.activation(xh[:, at], ps[:, par, :], ACT.Copy).then_inc(g_hi, 1)
                act.wait_ge(g_mm, s + 1)
                if not isinstance(s, int) or s >= 2:
                    act.wait_ge(g_stored[par], (s - par) * 8)
                act.activation(lgT[0:EXPERTS, par, :], ps[0:EXPERTS, 2 + par, :], ACT.Copy).then_inc(g_copied, 1)

            tile_steps(act, logits, 2)

            def experts(tt):
                for c in range(CHUNKS):
                    k = tt * CHUNKS + c
                    par = c % 2
                    act.wait_ge(m_w1, k + 1)
                    if not (isinstance(tt, int) and tt == 0 and c < 2):
                        act.wait_ge(m_lo, k - 1)
                        act.wait_ge(m_w2, k - 1)
                    act.activation(h32[:, par, :], ps[:, 2 * par:2 * par + 2, :].rearrange("p a t -> p (a t)"),
                                   ACT.Gelu_apprx_tanh, bias=vec[:, V_B1 + c:V_B1 + c + 1]).then_inc(m_gelu, 1)
                    act.wait_ge(m_gelu, k + 1)
                    act.activation(hh[:, par, :], h32[:, par, :], ACT.Copy).then_inc(m_hi, 1)

            experts(0)
            with act.Fori(1, NMT) as tt:
                experts(tt)

        @block.vector
        def _(dve):
            dve.memset(sa[:, :, 0:1], 0.0).then_inc(setup, 1)
            dve.memset(sden[:, :, 0:1], 0.0).then_inc(setup, 1)
            dve.wait_ge(x_first_in, 16)
            dve.wait_ge(pool_setup, 4)
            norm_stats(dve, norms[0], 0, 0, [])
            dve.wait_ge(act_setup, 2)
            dve.wait_ge(consts_in, 16)
            dve.tensor_scalar(decay, cst[:, C_ONES:C_ONES + 1].broadcast_to([P, T]), ew[:, 1:2], None, ALU.mult).then_inc(setup, 1)
            dve.wait_ge(weights_in, 48)
            dve.tensor_scalar(other, vec[:, V_MK:V_MK + 3], -1.0, 1.0, ALU.mult, ALU.add).then_inc(mix_steps, 1)
            dve.wait_ge(mix_steps, 1)
            for m, w in enumerate((W_K, W_V, W_R)):
                dve.tensor_scalar(wmix[:, m, 0, :], wts[:, w:w + P], vec[:, m:m + 1], None, ALU.mult).then_inc(mix_steps, 1)
                dve.tensor_scalar(wmix[:, m, 1, :], wts[:, w:w + P], other[:, m:m + 1], None, ALU.mult).then_inc(mix_steps, 1)
            dve.wait_ge(ints_in, 16)
            dve.tensor_copy(wgu, int_raw[:, 0:2 * HIDDEN]).then_inc(setup, 1)
            dve.tensor_copy(wdn, int_raw[:, 2 * HIDDEN:3 * HIDDEN]).then_inc(setup, 1)
            dve.wait_ge(weights_in, 48)
            dve.tensor_copy(gate_hi[:, :], vec[:, V_GATE:V_GATE + EXPERTS]).then_inc(w_gw, 1)
            dve.wait_ge(w_gw, 1)
            dve.tensor_tensor(gate_lo[:, :], vec[:, V_GATE:V_GATE + EXPERTS], gate_hi[:, :].bitcast(F32), ALU.subtract).then_inc(w_gw, 1)
            dve.wait_ge(setup, 5)
            dve.wait_ge(comb, 1)
            dve.tensor_copy(wq[:, :], ps[:, 7, :]).then_inc(comb_copied, 1)
            dve.wait_ge(comb, 2)
            dve.tensor_tensor(wk[:, :], ps[:, 6, :], wts[:, W_KROPE:W_KROPE + GROUPS * P], ALU.add).then_inc(comb_copied, 1)
            dve.wait_ge(comb, 3)
            dve.tensor_copy(wv[:, :], ps[:, 5, 0:P]).then_inc(comb_copied, 1)
            dve.wait_ge(x_rest_in, 16)

            def residual(t, done, scale, added, bank):
                dve.wait_ge(done, t + 1)
                xt = blocks(t)
                dve.scalar_tensor_tensor(xt, ps[:, bank, :].rearrange("p (n c) -> p n c", n=TB), scale, xt,
                                         ALU.mult, ALU.add).then_inc(added, 1)

            def phase1(s, par):
                norm_apply(dve, norms[0], s, par)
                norm_stats(dve, norms[0], s + 1, 1 - par, [])
                if live(s - 2):
                    residual(s - 2, o_done, 0.5, resid1, 6)
                t = s - 1
                if not live(t):
                    return
                q = 1 - par
                base = t * C1
                dve.wait_ge(proj_done, t * 3 + 2)
                dve.wait_ge(act1, t * 3 + 2)
                if not isinstance(t, int) or t >= 1:
                    dve.wait_ge(chain1, base)
                dve.tensor_tensor(kv, ps[:, 2, :], ek[:, q, :], ALU.mult).then_inc(chain1, 1)
                dve.tensor_tensor(nu, ps[:, 2, :], eu[:, q, :], ALU.mult).then_inc(chain1, 1)
                dve.wait_ge(chain1, base + 1)
                for b in range(SEQS):
                    dve.tensor_tensor_scan(sa[:, b, 1:T + 1], decay, kv[:, b * T:(b + 1) * T], 0.0,
                                           ALU.mult, ALU.add).then_inc(chain1, 1)
                dve.wait_ge(sums_done, t * 2 + 2)
                for b in range(SEQS):
                    dve.tensor_tensor_scan(sden[:, b, 1:T + 1], decay, ps[:, 4, b * T:(b + 1) * T], 0.0,
                                           ALU.mult, ALU.add).then_inc(chain1, 1)
                dve.wait_ge(chain1, base + 6)
                as_seqs = lambda a: a.rearrange("p (b t) -> p b t", b=SEQS)
                dve.scalar_tensor_tensor(as_seqs(den), as_seqs(ps[:, 5, :]), 1e-6, sden[:, :, 0:T], ALU.max, ALU.add).then_inc(chain1, 1)
                dve.tensor_tensor(as_seqs(num), as_seqs(nu), sa[:, :, 0:T], ALU.add).then_inc(chain1, 1)
                dve.wait_ge(chain1, base + 7)
                dve.reciprocal(rec, den).then_inc(chain1, 1)
                dve.wait_ge(chain1, base + 9)
                dve.tensor_tensor(wkv, num, rec, ALU.mult).then_inc(chain1, 1)
                dve.wait_ge(chain1, base + 10)
                dve.wait_ge(act1, t * 3 + 3)
                if not isinstance(t, int) or t >= 2:
                    dve.wait_ge(o_done, t - 1)
                dve.scalar_tensor_tensor(gated[:, q, :], th[:, q, :], 1.0, wkv, ALU.add, ALU.mult).then_inc(chain1, 1)

            tile_steps(dve, phase1, 2)

            def phase2(s, par):
                norm_apply(dve, norms[1], s, par)
                norm_stats(dve, norms[1], s + 1, 1 - par, [])
                if live(s - 2):
                    residual(s - 2, f_down, 0.5 / 127.0 ** 3, resid2, 7)
                if live(s):
                    dve.wait_ge(f_hi, s + 1)
                    if not isinstance(s, int) or s >= 2:
                        dve.wait_ge(fg_done, (s - 1) * FJ)
                    dve.tensor_tensor(fxl[:, par, :], ps[:, 0, :], fxh[:, par, :].bitcast(F32), ALU.subtract).then_inc(f_lo, 1)
                t = s - 1
                if not live(t):
                    return
                q = 1 - par
                if not isinstance(t, int) or t >= 1:
                    dve.wait_ge(f_h, t * FJ)
                for j in range(FJ):
                    dve.wait_ge(f_tanh, t * FJ + j + 1)
                    dve.scalar_tensor_tensor(fu[:, j, :], ft[:, j, :], 1.0, ps[:, 1 + 2 * j, :],
                                             ALU.add, ALU.mult).then_inc(chain2, 1)
                for j in range(FJ):
                    dve.wait_ge(chain2, t * FJ + j + 1)
                    if j == 0 and (not isinstance(t, int) or t >= 2):
                        dve.wait_ge(f_down, t - 1)
                    dve.tensor_tensor(fh[:, q, j, :], fu[:, j, :], ps[:, 2 + 2 * j, :], ALU.mult).then_inc(f_h, 1)

            norm_stats(dve, norms[1], 0, 0, [(resid1, NT), (norms[0].rstd, NT + 1)])
            tile_steps(dve, phase2, 2)

            for a in range(2):
                dve.memset(vx[:, a, :, :, DH + 1:SLOT], 0.0).then_inc(setup, 1)
                dve.memset(vx[:, a, :, :, DH:DH + 1], 1.0).then_inc(setup, 1)

            def table(col, a):
                return cst[:, col:col + T].unsqueeze(1).broadcast_to([P, SEQS, T])

            def project_done(t, par, piece):
                dve.wait_ge(a_proj, t * 8 + piece + 1)
                if piece == 0 and (not isinstance(t, int) or t >= 2):
                    dve.wait_ge(a_s, (t - 1) * 16)
                dst = (qs, ks)[piece % 2][:, par, piece // 2, :]
                dve.tensor_tensor(dst.rearrange("p (b t) -> p b t", b=SEQS), ps[:, 1, :].rearrange("p (b t) -> p b t", b=SEQS),
                                  table((C_TABQ, C_TABK)[piece % 2], 0), ALU.mult).then_inc(a_qk, 1)

            def normalise(t, q):
                dve.wait_ge(a_f1, t * 4 + q + 1)
                heads = ps[:, 0, :].rearrange("p (h s) -> p h s", h=HEADS)
                dve.reciprocal(oden, heads[:, :, DH]).then_inc(a_fd, 1)
                dve.wait_ge(a_fd, t * 4 + q + 1)
                dve.tensor_tensor(otok, heads[:, :, 0:DH], oden.unsqueeze(2).broadcast_to([P, HEADS, DH]), ALU.mult).then_inc(a_ftok, 1)

            def add_block(t, q):
                dve.wait_ge(a_wo, t * 4 + q + 1)
                xt = blocks(t)[:, q, :]
                dve.tensor_tensor(xt, ps[:, 0, 0:P], xt, ALU.add).then_inc(resid3, 1)

            lim = cst[:, C_LIM:C_LIM + 384].unsqueeze(1).broadcast_to([P, 2, 384])

            def phase3(s, par):
                norm_apply(dve, norms[2], s, par)
                norm_stats(dve, norms[2], s + 1, 1 - par, [])
                for u in range(8):
                    if live(s - 1):
                        k = (s - 1) * 8 + u
                        for half in range(2):
                            dve.wait_ge(a_s, 2 * k + half + 1)
                            if not (isinstance(s, int) and s == 1 and u == 0):
                                dve.wait_ge(a_p, 2 * k + half - 1)
                            dve.scalar_tensor_tensor(cl[:, half, :, :], ps[:, 2 + 2 * half:4 + 2 * half, 0:384], -CLIP, lim,
                                                     ALU.max, ALU.min).then_inc(a_cl, 1)
                    if live(s) and u >= 1:
                        project_done(s, par, u - 1)
                    if live(s - 2):
                        if u in (2, 4, 6):
                            normalise(s - 2, (u - 2) // 2)
                        if u in (3, 5, 7):
                            add_block(s - 2, (u - 3) // 2)
                if live(s):
                    project_done(s, par, 7)
                if live(s - 2):
                    normalise(s - 2, 3)
                    add_block(s - 2, 3)

            norm_stats(dve, norms[2], 0, 0, [(resid2, NT), (norms[1].rstd, NT + 1)])
            tile_steps(dve, phase3, 2)

            def logits(s, par):
                norm_apply(dve, norms[3], s, par)
                norm_stats(dve, norms[3], s + 1, 1 - par, [])
                if live(s):
                    dve.wait_ge(g_hi, s + 1)
                    at = bass.ds(s * TILE, TILE) if not isinstance(s, int) else slice(s * TILE, (s + 1) * TILE)
                    dve.tensor_tensor(xl[:, at], ps[:, par, :], xh[:, at].bitcast(F32), ALU.subtract).then_inc(g_lo, 1)

            norm_stats(dve, norms[3], 0, 0, [(resid3, NT * TB), (norms[2].rstd, NT + 1)])
            tile_steps(dve, logits, 2)

            steps = [0]

            def link(ins):
                ins.then_inc(s_steps, 1)
                steps[0] += 1
                dve.wait_ge(s_steps, steps[0])

            sgn, limit, part, m, cand, take, kth = (small[:, i:i + 1] for i in range(7))
            bits = small[:, 7:8]
            dve.wait_ge(g_loaded, 16)
            link(dve.tensor_scalar(zs, lg, 0.0, None, ALU.is_lt, ALU.add, accum_out=part))
            dve.wait_ge(s_counted, 1)
            link(dve.tensor_scalar(take, ps[:, 7, 0:1], float(KTH), None, ALU.is_ge))
            link(dve.tensor_scalar(sgn, take, -2.0, 1.0, ALU.mult, ALU.add))
            link(dve.tensor_scalar(limit, take, float(PAIRS - KTH - (KTH - 1)), float(KTH - 1), ALU.mult, ALU.add))
            link(dve.tensor_scalar(z, lg, sgn, None, ALU.mult))
            link(dve.memset(m, 0.0))
            for bit in range(30, -1, -1):
                link(dve.tensor_scalar(cand.bitcast(I32), m.bitcast(I32), 1 << bit, None, ALU.bitwise_or))
                link(dve.tensor_scalar(zs, z, cand, None, ALU.is_lt, ALU.add, accum_out=part))
                dve.wait_ge(s_counted, 32 - bit)
                link(dve.tensor_tensor(take.bitcast(I32), ps[:, 7, 0:1], limit, ALU.is_le))
                link(dve.copy_predicated(m, take.bitcast(I32), cand))
            link(dve.tensor_scalar(kth, m, sgn, None, ALU.mult))
            link(dve.scalar_tensor_tensor(zs, lg, kth, lg, ALU.is_ge, ALU.mult))
            dve.tensor_copy(lg, zs).then_inc(gates_ready, 1)

            def finish(tt, last):
                if not isinstance(tt, int) or tt >= 1:
                    dve.wait_ge(stored, tt * 16)
                for half in range(2):
                    dve.wait_ge(m_turn, tt * 2 + half + 1)
                    at = bass.ds(tt * 8 + 4 * half, 4) if not isinstance(tt, int) else slice(tt * 8 + 4 * half, tt * 8 + 4 * half + 4)
                    ins = dve.tensor_tensor(yout[:, 4 * half:4 * half + 4, :], ps[:, 6 + half, :].rearrange("p (n c) -> p n c", n=4),
                                            x[:, at, :], ALU.add)
                    if half:
                        dve_half = ins.then_inc(m_out, 1)
                    else:
                        ins.then_inc(m_half, 1)
                dve.wait_ge(m_half, tt + 1)
                dve.wait_ge(m_out, tt + 1)

            def experts(tt):
                for c in range(CHUNKS):
                    k = tt * CHUNKS + c
                    par = c % 2
                    dve.wait_ge(m_hi, k + 1)
                    if not (isinstance(tt, int) and tt == 0 and c < 2):
                        dve.wait_ge(m_w2, k - 1)
                    dve.tensor_tensor(hl[:, par, :], h32[:, par, :], hh[:, par, :].bitcast(F32), ALU.subtract).then_inc(m_lo, 1)
                    if c == 2 and not (isinstance(tt, int) and tt == 0):
                        finish(tt - 1, False)
                    if c % EC == 1 and c > EC:
                        gate(tt, c // EC - 1)
                gate(tt, EXPERTS - 1)

            def gate(tt, e):
                n = tt * EXPERTS + e
                dve.wait_ge(m_w2, tt * CHUNKS + (e + 1) * EC)
                dve.wait_ge(gb_in[e % 2], (tt * (EXPERTS // 2) + e // 2 + 1) * 16)
                dst = acc if e == 0 else gy
                y = ps[:, 4 + 2 * (e % 2):6 + 2 * (e % 2), :].rearrange("p a t -> p (a t)")
                if e == 0 and not (isinstance(tt, int) and tt == 0):
                    dve.wait_ge(m_turn, tt * 2)
                if not (isinstance(tt, int) and tt == 0 and e == 0):
                    dve.wait_ge(m_acc, n)
                ins = dve.scalar_tensor_tensor(dst, y, vec[:, V_B2 + e:V_B2 + e + 1], gbc[:, e % 2, :], ALU.add, ALU.mult)
                ins.then_inc(m_gy, 1)
                dve.wait_ge(m_gy, n + 1)
                if e == 0:
                    dve.sem_inc(m_acc, 1)
                else:
                    dve.tensor_tensor(acc, acc, gy, ALU.add).then_inc(m_acc, 1)

            experts(0)
            with dve.Fori(1, NMT) as tt:
                experts(tt)
            finish(NMT - 1, True)

        @block.tensor
        def _(pe):
            pe.wait_ge(weights_in, 48)
            pe.wait_ge(consts_in, 16)
            pe.matmul(ps[:, 7, :], lat[:, L_DQ:L_DQ + P], lat[:, L_UQ:L_UQ + 512], start=True, stop=True).then_inc(comb, 1)
            pe.matmul(ps[:, 6, :], lat[:, L_DKV:L_DKV + P], lat[:, L_UK:L_UK + 512], start=True, stop=True).then_inc(comb, 1)
            pe.matmul(ps[:, 5, 0:P], lat[:, L_DKV:L_DKV + P], lat[:, L_UV:L_UV + P], start=True, stop=True).then_inc(comb, 1)
            pe.wait_ge(comb_copied, 3)
            pe.wait_ge(mix_steps, 7)

            def phase1(s, par):
                if live(s):
                    if not isinstance(s, int) or s >= 1:
                        pe.wait_ge(xT_ready, s)
                    norm_turn(pe, norms[0], s, par, 0)
                    pe.wait_ge(xT_ready, s + 1)
                    if not isinstance(s, int) or s >= 1:
                        pe.wait_ge(act1, s * 3)
                    for m in range(3):
                        if m == 1 and (not isinstance(s, int) or s >= 1):
                            pe.wait_ge(chain1, (s - 1) * C1 + 2)
                        dst = ps[:, 1 + m, :].rearrange("p (b t) -> p b t", b=SEQS)
                        pe.matmul(dst, wmix[:, m, 0, :], xT[:, par, :, 1:T + 1], start=True, stop=False)
                        pe.matmul(dst, wmix[:, m, 1, :], xT[:, par, :, 0:T], start=False, stop=True).then_inc(proj_done, 1)
                    for i, e in enumerate((ek, eu)):
                        pe.wait_ge(act1, s * 3 + 1 + i)
                        if not isinstance(s, int) or s >= 1:
                            pe.wait_ge(chain1, (s - 1) * C1 + 7)
                        pe.matmul(ps[:, 4 + i, :], cst[:, C_HEAD:C_HEAD + P], e[:, par, :], start=True, stop=True).then_inc(sums_done, 1)
                t = s - 1
                if live(t):
                    pe.wait_ge(chain1, (t + 1) * C1)
                    if not isinstance(t, int) or t >= 1:
                        pe.wait_ge(resid1, t)
                    for j in range(TB):
                        mm = pe.matmul(ps[:, 6, j * P:(j + 1) * P], gated[:, 1 - par, j * P:(j + 1) * P],
                                       wts[:, W_O0:W_O0 + P], start=True, stop=True)
                    mm.then_inc(o_done, 1)

            tile_steps(pe, phase1, 2)
            pe.wait_ge(resid1, NT)

            def phase2(s, par):
                if live(s):
                    if not isinstance(s, int) or s >= 1:
                        pe.wait_ge(f_lo, s)
                    norm_turn(pe, norms[1], s, par, 0)
                    pe.wait_ge(f_lo, s + 1)
                    for j in range(FJ):
                        if not isinstance(s, int) or s >= 1:
                            pe.wait_ge(f_h, (s - 1) * FJ + j + 1)
                        for i in range(2):
                            w = wgu[:, (i * FJ + j) * P:(i * FJ + j + 1) * P]
                            pe.matmul(ps[:, 1 + 2 * j + i, :], w, fxh[:, par, :], start=True, stop=False)
                            mm = pe.matmul(ps[:, 1 + 2 * j + i, :], w, fxl[:, par, :], start=False, stop=True)
                        mm.then_inc(fg_done, 1)
                t = s - 1
                if live(t):
                    pe.wait_ge(f_h, (t + 1) * FJ)
                    if not isinstance(t, int) or t >= 1:
                        pe.wait_ge(resid2, t)
                    for b in range(TB):
                        for j in range(FJ):
                            mm = pe.matmul(ps[:, 7, b * P:(b + 1) * P], fh[:, 1 - par, j, b * P:(b + 1) * P],
                                           wdn[:, j * P:(j + 1) * P], start=(j == 0), stop=(j == FJ - 1))
                    mm.then_inc(f_down, 1)

            tile_steps(pe, phase2, 2)
            pe.wait_ge(resid2, NT)
            pe.wait_ge(setup, 9)

            def project(t, par, piece):
                if not (isinstance(t, int) and t == 0 and piece == 0):
                    pe.wait_ge(a_qk, t * 8 + piece)
                w = (wq, wk)[piece % 2]
                g = piece // 2
                pe.matmul(ps[:, 1, :], w[:, g * P:(g + 1) * P], ax[:, par, :], start=True, stop=True).then_inc(a_proj, 1)

            def weigh(t, par, u):
                k = t * 8 + u
                b, g = u // 4, u % 4
                pe.wait_ge(a_p, 2 * k + 2)
                if not (isinstance(t, int) and t == 0 and u < 2):
                    pe.wait_ge(a_ot, k - 1)
                for h in range(4):
                    probs = pr[:, (2 * u + h // 2) % 4, h % 2, :]
                    dst = ps[SLOT * h:SLOT * h + SLOT, 6 + u % 2, :]
                    pe.matmul(dst[:, 0:T], vx[:, par, 2 * b, 4 * g + h, :], probs[:, 0:T], start=True, stop=False)
                    mm = pe.matmul(dst[:, P:T], vx[:, par, 2 * b + 1, 4 * g + h, :], probs[:, T:T + P], start=False, stop=True)
                mm.then_inc(a_av, 1)

            def turn_out(t, par, q):
                if not (isinstance(t, int) and t == 0 and q == 0):
                    pe.wait_ge(resid3, t * 4 + q)
                b, half = q // 2, q % 2
                pe.wait_ge(a_ot, t * 8 + 4 * b + 4)
                for g in range(GROUPS):
                    mm = pe.transpose(ps[:, 0, g * P:(g + 1) * P], ot[:, par, b, g, half * P:(half + 1) * P], ident)
                mm.then_inc(a_f1, 1)

            def turn_back(t, q):
                pe.wait_ge(a_ftok, t * 4 + q + 1)
                pe.transpose(ps[:, 0, 0:P], otok.rearrange("p h d -> p (h d)"), ident).then_inc(a_f2, 1)

            def out_project(t, q):
                pe.wait_ge(a_oT, t * 4 + q + 1)
                pe.matmul(ps[:, 0, 0:P], oT, wts[:, W_O1:W_O1 + P], start=True, stop=True).then_inc(a_wo, 1)

            def phase3(s, par):
                for u in range(8):
                    if u == 0 and live(s):
                        if live(s - 1):
                            pe.wait_ge(a_vready, s)
                        if live(s - 3):
                            pe.wait_ge(resid3, (s - 2) * 4)
                        norm_turn(pe, norms[2], s, par, 0)
                    if live(s - 1):
                        k = (s - 1) * 8 + u
                        b, g = u // 4, u % 4
                        if u == 0:
                            pe.wait_ge(a_qk, s * 8)
                        for half in range(2):
                            if not (isinstance(s, int) and s == 1 and u == 0):
                                pe.wait_ge(a_cl, 2 * k + half - 1)
                            for i in range(2):
                                h = 2 * half + i
                                rows = slice(SLOT * h, SLOT * h + SLOT)
                                kk = ks[rows, 1 - par, g, :]
                                qq = qs[rows, 1 - par, g, :]
                                o = b * T
                                pe.matmul(ps[:, 2 + h, 0:T], kk[:, o:o + P], qq[:, o:o + T], start=True, stop=True)
                            for i in range(2):
                                h = 2 * half + i
                                rows = slice(SLOT * h, SLOT * h + SLOT)
                                kk = ks[rows, 1 - par, g, :]
                                qq = qs[rows, 1 - par, g, :]
                                mm = pe.matmul(ps[:, 2 + h, T:T + P], kk[:, o + P:o + T], qq[:, o + P:o + T], start=True, stop=True)
                            mm.then_inc(a_s, 1)
                    if live(s):
                        if u == 1:
                            pe.wait_ge(a_x, s + 1)
                            for j in range(TB):
                                mm = pe.matmul(ps[:, 0, j * P:(j + 1) * P], ax[:, par, j * P:(j + 1) * P], wv[:, :], start=True, stop=True)
                            mm.then_inc(a_vdone, 1)
                        if u >= 1:
                            project(s, par, u - 1)
                    if live(s - 1) and u >= 1:
                        if u == 1:
                            pe.wait_ge(a_vready, s)
                        weigh(s - 1, 1 - par, u - 1)
                    if live(s - 2):
                        if u == 2 and live(s):
                            pe.wait_ge(a_vready, s + 1)
                        if u in (2, 4, 6):
                            turn_out(s - 2, par, (u - 2) // 2)
                            turn_back(s - 2, (u - 2) // 2)
                        if u in (3, 5, 7):
                            out_project(s - 2, (u - 3) // 2)
                if live(s):
                    project(s, par, 7)
                if live(s - 1):
                    weigh(s - 1, 1 - par, 7)
                if live(s - 2):
                    turn_out(s - 2, par, 3)
                    turn_back(s - 2, 3)
                    out_project(s - 2, 3)

            tile_steps(pe, phase3, 2)
            pe.wait_ge(resid3, NT * TB)
            pe.wait_ge(w_gw, 2)

            def logits(s, par):
                if not live(s):
                    return
                if not isinstance(s, int) or s >= 2:
                    pe.wait_ge(g_lo, s - 1)
                norm_turn(pe, norms[3], s, par, par)
                pe.wait_ge(g_lo, s + 1)
                if not isinstance(s, int) or s >= 2:
                    pe.wait_ge(g_copied, s - 1)
                at = bass.ds(s * TILE, TILE) if not isinstance(s, int) else slice(s * TILE, (s + 1) * TILE)
                dst = ps[0:EXPERTS, 2 + par, :]
                pe.matmul(dst, gate_hi[:, :], xh[:, at], start=True, stop=False)
                pe.matmul(dst, gate_hi[:, :], xl[:, at], start=False, stop=False)
                pe.matmul(dst, gate_lo[:, :], xh[:, at], start=False, stop=True).then_inc(g_mm, 1)

            tile_steps(pe, logits, 2)
            for i in range(32):
                pe.wait_ge(s_steps, 1 if i == 0 else 6 + 4 * (i - 1) + 2)
                pe.matmul(ps[:, 7, 0:1], ones, small[:, 2:3], start=True, stop=True).then_inc(s_counted, 1)
            pe.wait_ge(w_split, 4 * PIECES)
            pe.wait_ge(g_copied, NT)

            def first(tt, c):
                k = tt * CHUNKS + c
                par = c % 2
                if not (isinstance(tt, int) and tt == 0 and c < 2):
                    pe.wait_ge(m_gelu, k - 1)
                w = slice(c * P, (c + 1) * P)
                for i, (wt, xs) in enumerate(((w1h, xh), (w1h, xl), (w1l, xh))):
                    for half in range(2):
                        o = tt * MT + half * 512
                        at = bass.ds(o, 512) if not isinstance(tt, int) else slice(o, o + 512)
                        mm = pe.matmul(ps[:, 2 * par + half, :], wt[:, w], xs[:, at], start=(i == 0), stop=(i == 2))
                mm.then_inc(m_w1, 1)

            def second(tt, c):
                k = tt * CHUNKS + c
                par = c % 2
                e, j = c // EC, c % EC
                if j == 0:
                    if not (isinstance(tt, int) and tt == 0 and e < 2):
                        pe.wait_ge(m_gy, tt * EXPERTS + e - 1)
                    if e == 1 and not (isinstance(tt, int) and tt == 0):
                        pe.wait_ge(m_out, tt)
                w = slice(c * P, (c + 1) * P)
                pe.wait_ge(m_hi, k + 1)
                for i, (wt, hs) in enumerate(((w2h, hh), (w2l, hh), (w2h, hl))):
                    if i == 2:
                        pe.wait_ge(m_lo, k + 1)
                    for half in range(2):
                        mm = pe.matmul(ps[:, 4 + 2 * (e % 2) + half, :], wt[:, w], hs[:, par, half * 512:half * 512 + 512],
                                       start=(j == 0 and i == 0), stop=(j == EC - 1 and i == 2))
                mm.then_inc(m_w2, 1)

            def turn_sum(tt):
                pe.wait_ge(m_acc, (tt + 1) * EXPERTS)
                for half in range(2):
                    for j in range(4):
                        mm = pe.transpose(ps[:, 6 + half, j * P:(j + 1) * P],
                                          acc[:, half * 512 + j * P:half * 512 + (j + 1) * P], ident)
                    mm.then_inc(m_turn, 1)

            def experts(tt):
                for c in range(CHUNKS + 1):
                    if c < CHUNKS:
                        first(tt, c)
                    if c == 2 and not (isinstance(tt, int) and tt == 0):
                        turn_sum(tt - 1)
                    if c:
                        second(tt, c - 1)

            experts(0)
            with pe.Fori(1, NMT) as tt:
                experts(tt)
            turn_sum(NMT - 1)


def kernel(**inputs):
    import concourse.bacc as _bacc
    from concourse.bass_utils import run_bass_kernel_spmd as _run

    a = {k: np.ascontiguousarray(v) for k, v in inputs.items()}
    f = np.float32
    weights = np.zeros((P, W_COLS), f)
    for at, name in ((W_K, "Wk"), (W_V, "Wv"), (W_R, "Wr"), (W_O0, "Wo")):
        weights[:, at:at + P] = a["L0_attn_" + name].T
    weights[:, W_O1:W_O1 + P] = a["L1_attn_W_O"]
    latent = np.zeros((32, L_COLS), f)
    latent[:, L_DQ:L_DQ + P] = a["L1_attn_W_DQ"].T
    latent[:, L_DKV:L_DKV + P] = a["L1_attn_W_DKV"].T
    latent[:, L_UV:L_UV + P] = a["L1_attn_W_UV"]
    for h in range(HEADS):
        o = h * SLOT
        latent[:, L_UQ + o:L_UQ + o + DH] = a["L1_attn_W_UQ"][:, h * DH:(h + 1) * DH]
        latent[:, L_UK + o:L_UK + o + DH] = a["L1_attn_W_UK"][:, h * DH:(h + 1) * DH]
        for p in range(DR // 2):
            for k in range(ROPE):
                col = o + DH + ROPE * p + k
                latent[:, L_UQ + col] = a["L1_attn_W_QR"][:, h * DR + 2 * p + Q_DIM[k]]
                weights[:, W_KROPE + col] = a["L1_attn_W_KR"][:, 2 * p + K_DIM[k]]
    vectors = np.zeros((P, V_COLS), f)
    for at, name in ((V_MK, "mix_k"), (V_MV, "mix_v"), (V_MR, "mix_r")):
        vectors[:, at] = a["L0_attn_" + name].reshape(C)
    vectors[:, V_DECAY] = np.repeat(a["L0_attn_time_decay"], DH)
    vectors[:, V_FIRST] = np.repeat(a["L0_attn_time_first"], DH)
    vectors[:, V_GATE:V_GATE + EXPERTS] = a["L1_ffn_gate_weight"].T
    vectors[:, V_B1:V_B1 + CHUNKS] = a["L1_ffn_b1"].reshape(CHUNKS, P).T
    vectors[:, V_B2:V_B2 + EXPERTS] = a["L1_ffn_b2"].T
    ints = np.concatenate([a["L0_ffn_w_gate"].T, a["L0_ffn_w_up"].T,
                           a["L0_ffn_w_down"].T.reshape(FJ, P, C).transpose(1, 0, 2).reshape(P, HIDDEN)], 1)
    w1 = a["L1_ffn_w1"].reshape(EXPERTS * HE, C).T
    w2 = a["L1_ffn_w2"].transpose(0, 2, 1).reshape(CHUNKS, P, C).transpose(1, 0, 2).reshape(P, CHUNKS * C)
    arrays = {"x_in": a["L0_attn_x"].reshape(N, C), "weights_in_dram": weights, "vectors_dram": vectors,
              "latent_dram": latent, "ints_dram": ints, "w1_dram": w1, "w2_dram": w2, "consts_dram": rope_tables()}
    arrays = {k: np.ascontiguousarray(v) for k, v in arrays.items()}
    nc = _bacc.Bacc("TRN2", target_bir_lowering=False, num_devices=1)
    args = [nc.dram_tensor(k, v.shape, mybir.dt.from_np(v.dtype), kind="ExternalInput").ap() for k, v in arrays.items()]
    args.append(nc.dram_tensor("out_dram", (N, C), F32, kind="ExternalOutput").ap())
    build(nc, *args)
    r = _run(nc, [arrays], core_ids=[0])
    return r.results[0]["out_dram"].reshape(BATCH, T, C)
```

```python
from contextlib import ExitStack

import concourse.bass as bass
import numpy as np
from concourse import mybir

F32 = mybir.dt.float32
R32 = mybir.dt.float32r
I32 = mybir.dt.int32
ALU = mybir.AluOpType
ACT = mybir.ActivationFunctionType

P = 128
BATCH, T, C = 16, 256, 128
N = BATCH * T
BLK = N // P
TILE = 512
NT = N // TILE
TB = TILE // P
SEQS = TILE // T
HEADS, DH, DR = 16, 8, 4
GROUPS = HEADS // 4
SLOT = 32
HIDDEN = 384
FJ = HIDDEN // P
EXPERTS, HE = 8, 512
EC = HE // P
CHUNKS = EXPERTS * EC
MT = 1024
NMT = N // MT
KTH = 4 * 128 * 6
PAIRS = N * EXPERTS
EPS = 1e-5
CLIP = 80.0
MASKED = -1.0e4
ROPE = 8
SLOT_COLS = DH + ROPE * (DR // 2)
Q_DIM = [0, 0, 1, 1, 0, 0, 1, 1]
K_DIM = [0, 1, 0, 1, 0, 1, 0, 1]
Q_SIN = [0, 0, 1, 1, 1, 1, 0, 0]
K_SIN = [0, 1, 0, 1, 1, 0, 1, 0]
SIGN = [1, -1, -1, 1, 1, 1, 1, 1]

SPLIT = CHUNKS * P // (N // 512)
ARENA = 25500

W_K, W_V, W_R, W_O0 = 0, 128, 256, 384
W_O1 = 512
W_KROPE = 640
W_COLS = W_KROPE + GROUPS * P
V_MK, V_MV, V_MR, V_DECAY, V_FIRST = range(5)
V_GATE = 5
V_B1 = V_GATE + EXPERTS
V_B2 = V_B1 + CHUNKS
V_COLS = V_B2 + EXPERTS
L_DQ, L_UQ, L_DKV, L_UK, L_UV = 0, 128, 640, 768, 1280
L_COLS = 1408
C_ID, C_ONES, C_HEAD = 0, 128, 256
C_TABQ, C_TABK = 384, 384 + T
C_LIM = 384 + 2 * T
KB = T // 4
S_AT = [0, T, 0, P]
C_SLOT = C_LIM + 2 * T - KB + P + KB
C_COLS = C_SLOT + 4
XY = 2 * T - KB
ZC = P + KB


def rope_tables():
    out = np.zeros((P, C_COLS), np.float32)
    out[:, C_ID:C_ID + P] = np.eye(P)
    out[:, C_ONES:C_ONES + P] = 1.0
    for h in range(HEADS):
        out[h * DH:h * DH + DH, C_HEAD + h * DH:C_HEAD + h * DH + DH] = 1.0
    inv = np.float32(10000.0) ** (-np.arange(0, DR, 2, dtype=np.float32) / np.float32(DR))
    ang = np.arange(T, dtype=np.float32)[:, None] * inv
    trig = [np.cos(ang.astype(np.float64)), np.sin(ang.astype(np.float64))]
    for q in range(4):
        out[SLOT * q:SLOT * q + DH, C_TABQ:C_TABQ + T] = 1.0
        out[SLOT * q:SLOT * q + DH, C_TABK:C_TABK + T] = 1.0
        for p in range(DR // 2):
            for k in range(ROPE):
                row = SLOT * q + DH + ROPE * p + k
                out[row, C_TABQ:C_TABQ + T] = SIGN[k] * trig[Q_SIN[k]][:, p]
                out[row, C_TABK:C_TABK + T] = trig[K_SIN[k]][:, p]
    for q in range(4):
        out[SLOT * q:SLOT * q + SLOT, C_SLOT + q] = 1.0
    own = np.where(np.arange(KB)[None, :] >= np.arange(P)[:, None] % KB, CLIP, MASKED)
    out[:, C_LIM:C_SLOT] = CLIP
    for at in (0, T, XY, XY + P):
        out[:, C_LIM + at:C_LIM + at + KB] = own
    return out


def build(nc, x_in, weights, vectors, latent, ints, w1_in, w2_in, consts, out):
    with ExitStack() as ctx:
        def sb(name, shape, dt=F32):
            return ctx.enter_context(nc.sbuf_tensor(name, shape, dt))

        def sem(name):
            return ctx.enter_context(nc.semaphore(name))

        ps = ctx.enter_context(nc.psum_tensor("ps", [P, 8, 512], F32))
        logits_dram = nc.dram_tensor("logits_scratch", [EXPERTS, N], F32, kind="Internal").ap()
        gates_dram = nc.dram_tensor("gates_scratch", [P, PAIRS // P], F32, kind="Internal").ap()

        x = sb("x", [P, BLK + TB, C])
        cst = sb("cst", [P, C_COLS])
        wts = sb("wts", [P, W_COLS])
        vec = sb("vec", [P, V_COLS])
        ident = cst[:, C_ID:C_ID + P]
        ones = cst[:, C_ONES:C_ONES + P]
        w1h = sb("w1h", [P, CHUNKS * P], R32)
        w1l = sb("w1l", [P, CHUNKS * P], R32)
        w2h = sb("w2h", [P, CHUNKS * P], R32)
        w2l = sb("w2l", [P, CHUNKS * P], R32)
        stats = sb("stats", [P, 2, TB, 6])
        moments = sb("moments", [P, 2, TB, 2])
        vareps = sb("vareps", [P, 2, TB])
        minus_half = sb("minus_half", [P, TB])
        rstd = sb("rstd", [P, 2, TB])
        xn = sb("xn", [P, 2, TB, C])
        wqkv_hi = sb("wqkv_hi", [P, 2 * GROUPS * P + P], R32)
        wqkv_lo = sb("wqkv_lo", [P, 2 * GROUPS * P + P], R32)
        gate_hi = sb("gate_hi", [P, EXPERTS], R32)
        gate_lo = sb("gate_lo", [P, EXPERTS], R32)
        arena_at = nc.sbuf_base
        sb("arena", [P, ARENA])
        used = [0]

        def cut(name, cols, shape=None, dt=F32):
            a = nc.alloc_sbuf_tensor_at(name, [P, cols], dt, offset=arena_at + 4 * used[0])[:, :]
            used[0] += -(-cols // 8) * 8
            assert used[0] <= ARENA, used[0]
            return a if shape is None else a.rearrange(shape[0], **shape[1])

        xT = cut("xT", 2 * SEQS * (T + 1), ("p (a b t) -> p a b t", dict(a=2, b=SEQS)))
        other = cut("other", 3)
        wmix = cut("wmix", 3 * 2 * P, ("p (m a n) -> p m a n", dict(m=3, a=2)))
        decay = cut("decay", T)
        ew = cut("ew", 2)
        ek = cut("ek", 2 * TILE, ("p (a t) -> p a t", dict(a=2)))
        eu = cut("eu", 2 * TILE, ("p (a t) -> p a t", dict(a=2)))
        th = cut("th", 2 * TILE, ("p (a t) -> p a t", dict(a=2)))
        kv = cut("kv", TILE)
        nu = cut("nu", TILE)
        sa = cut("sa", SEQS * (T + 1), ("p (b t) -> p b t", dict(b=SEQS)))
        sden = cut("sden", SEQS * (T + 1), ("p (b t) -> p b t", dict(b=SEQS)))
        num = cut("num", TILE)
        den = cut("den", TILE)
        rec = cut("rec", TILE)
        wkv = cut("wkv", TILE)
        gated = cut("gated", 2 * TILE, ("p (a t) -> p a t", dict(a=2)))
        lat = cut("lat", L_COLS)[0:32, :]
        raw = cut("raw", CHUNKS * P)
        int_raw = raw[:, 0:3 * HIDDEN].bitcast(I32)
        wgu = cut("wgu", 2 * HIDDEN, None, R32)
        wdn = cut("wdn", HIDDEN)
        fxh = cut("fxh", 2 * TILE, ("p (a t) -> p a t", dict(a=2)), R32)
        fxl = cut("fxl", 2 * TILE, ("p (a t) -> p a t", dict(a=2)), R32)
        ft = cut("ft", FJ * TILE, ("p (j t) -> p j t", dict(j=FJ)))
        fu = cut("fu", FJ * TILE, ("p (j t) -> p j t", dict(j=FJ)))
        fh = cut("fh", 2 * FJ * TILE, ("p (a j t) -> p a j t", dict(a=2, j=FJ)))
        used[0] = 0
        axh = cut("axh", 2 * TILE, ("p (a t) -> p a t", dict(a=2)), R32)
        axl = cut("axl", 2 * TILE, ("p (a t) -> p a t", dict(a=2)), R32)
        qs = cut("qs", 2 * GROUPS * TILE, ("p (a g t) -> p a g t", dict(a=2, g=GROUPS)))
        ks = cut("ks", 2 * GROUPS * TILE, ("p (a g t) -> p a g t", dict(a=2, g=GROUPS)))
        kbd = cut("kbd", 2 * 2 * 4 * P, ("p (a q j i k) -> p a q j i k", dict(a=2, q=2, j=4, i=2)))
        vx = cut("vx", 2 * 8 * 8 * SLOT, ("p (a j q i s) -> p a j q i s", dict(a=2, j=8, q=8, i=2)))
        clxy = cut("clxy", 2 * XY, ("p (q t) -> p q t", dict(q=2)))
        clz = cut("clz", 2 * ZC, ("p (q t) -> p q t", dict(q=2)))
        prxy = cut("prxy", 4 * 2 * XY, ("p (a q t) -> p a q t", dict(a=4, q=2)))
        prz = cut("prz", 4 * 2 * ZC, ("p (a q t) -> p a q t", dict(a=4, q=2)))
        ot = cut("ot", 2 * SEQS * 2 * T, ("p (a b w t) -> p a b w t", dict(a=2, b=SEQS, w=2)))
        otok = cut("otok", P, ("p (h d) -> p h d", dict(h=HEADS)))
        oden = cut("oden", HEADS)
        oT = cut("oT", P)
        used[0] = 0
        xh = cut("xh", N, None, R32)
        xl = cut("xl", N, None, R32)
        h32 = cut("h32", 2 * MT, ("p (a t) -> p a t", dict(a=2)))
        hh = cut("hh", 2 * MT, ("p (a t) -> p a t", dict(a=2)), R32)
        hl = cut("hl", 2 * MT, ("p (a t) -> p a t", dict(a=2)), R32)
        gbc = cut("gbc", 2 * MT, ("p (a t) -> p a t", dict(a=2)))
        gy = cut("gy", MT)
        acc = cut("acc", MT)
        yout = cut("yout", MT, ("p (n c) -> p n c", dict(n=MT // P)))
        lgT = cut("lgT", 2 * TILE, ("p (a t) -> p a t", dict(a=2)))
        lg = cut("lg", PAIRS // P)
        z = cut("z", PAIRS // P)
        zs = cut("zs", PAIRS // P)
        small = cut("small", 16)

        consts_in, weights_in, x_first_in, x_rest_in = sem("consts_in"), sem("weights_in"), sem("x_first_in"), sem("x_rest_in")
        ints_in, raw_in = sem("ints_in"), sem("expert_weights_piece_in")
        setup = sem("vector_setup_steps")
        pool_setup = sem("pool_setup_steps")
        act_setup = sem("act_setup_steps")
        w_split = sem("expert_weights_split_steps")
        m_half = sem("p4_out_half")
        a_kb = sem("p3_key_blocks_ready")
        axl_ready, wsteps = sem("p3_lo_ready"), sem("p3_weights_split_steps")
        pool_passed = sem("pool_passed")
        passed = sem("vector_passed")
        w_gw = sem("gate_weights_split_steps")

        class Norm:

            def __init__(self, name):
                self.chain = sem(name + "_stats_steps")
                self.rstd = sem(name + "_rstd_ready")
                self.ready = sem(name + "_xn_ready")
                self.turned = sem(name + "_xn_turned")

        norms = [Norm(f"norm{i}") for i in range(1, 5)]
        CH = 2 * TB + 1

        def tile_steps(eng, body, extra):
            for s in range(extra):
                body(s, s % 2)
            with eng.Fori(0, (NT - extra) // 2) as i:
                body(2 * i + extra, extra % 2)
                body(2 * i + extra + 1, (extra + 1) % 2)
            for s in range(NT, NT + extra):
                body(s, s % 2)

        def live(t):
            return not isinstance(t, int) or 0 <= t < NT

        def blocks(t):
            return x[:, bass.ds(t * TB, TB), :] if not isinstance(t, int) else x[:, t * TB:(t + 1) * TB, :]

        def norm_stats(dve, norm, t, par, resid):
            if isinstance(t, int) and t > NT:
                return
            for wait, value in resid:
                dve.wait_ge(wait, value)
            xt = blocks(t)
            for j in range(TB):
                dve.bn_stats(stats[:, par, j, :], xt[:, j, :]).then_inc(norm.chain, 1)
            dve.wait_ge(norm.chain, t * CH + TB)
            dve.sem_inc(passed, 1)
            for j in range(TB):
                dve.bn_aggr(moments[:, par, j, :], stats[:, par, j, :]).then_inc(norm.chain, 1)
            dve.wait_ge(norm.chain, t * CH + 2 * TB)
            dve.tensor_scalar(vareps[:, par, :], moments[:, par, :, 1], EPS, None, ALU.add).then_inc(norm.chain, 1)

        def norm_rstd(pool, norm, t, par):
            if isinstance(t, int) and t > NT:
                return
            pool.wait_ge(norm.chain, (t + 1) * CH)
            pool.tensor_tensor(rstd[:, par, :], vareps[:, par, :], minus_half[:, :], ALU.pow).then_inc(norm.rstd, 1)

        def norm_apply(dve, norm, t, par):
            if not live(t):
                return
            dve.wait_ge(norm.rstd, t + 1)
            if not isinstance(t, int) or t >= 2:
                dve.wait_ge(norm.turned, t - 1)
            xt = blocks(t)
            for j in range(TB):
                dve.tensor_scalar(xn[:, par, j, :], xt[:, j, :], moments[:, par, j, 0:1], rstd[:, par, j:j + 1],
                                  ALU.subtract, ALU.mult).then_inc(norm.ready, 1)

        def norm_turn(pe, norm, t, par, bank):
            pe.wait_ge(norm.ready, t * TB + TB)
            for j in range(TB):
                mm = pe.transpose(ps[:, bank, j * P:(j + 1) * P], xn[:, par, j, :], ident)
            mm.then_inc(norm.turned, 1)

        xT_ready, mix_steps = sem("p1_xT_ready"), sem("p1_weights_mixed")
        proj_done, act1, sums_done = sem("p1_projected"), sem("p1_activated"), sem("p1_head_sums_done")
        chain1, o_done, resid1 = sem("p1_vector_steps"), sem("p1_out_projected"), sem("p1_residual_added")
        C1 = 11
        f_hi, f_lo, fg_done, f_tanh = sem("p2_hi_ready"), sem("p2_lo_ready"), sem("p2_gate_up_done"), sem("p2_tanh_ready")
        chain2, f_h, f_down, resid2 = sem("p2_vector_steps"), sem("p2_hidden_ready"), sem("p2_down_done"), sem("p2_residual_added")
        comb = sem("p3_weights_combined")
        comb_copied = sem("p3_weights_copied")
        a_x, a_proj, a_qk, a_vdone, a_vready = sem("p3_xT_ready"), sem("p3_qk_projected"), sem("p3_qk_ready"), sem("p3_v_projected"), sem("p3_v_ready")
        a_s, a_cl, a_p, a_av, a_ot = sem("p3_scores_done"), sem("p3_clipped"), sem("p3_probs_ready"), sem("p3_av_done"), sem("p3_av_copied")
        a_f1, a_fd, a_ftok, a_f2, a_oT, a_wo, resid3 = (sem("p3_out_turned"), sem("p3_denominators"), sem("p3_out_normalised"),
                                                        sem("p3_out_turned_back"), sem("p3_outT_ready"), sem("p3_out_projected"), sem("p3_residual_added"))
        g_hi, g_lo, g_mm, g_copied, g_stored = sem("p4_hi_ready"), sem("p4_lo_ready"), sem("p4_logits_done"), sem("p4_logits_copied"), [sem("p4_logits_stored0"), sem("p4_logits_stored1")]
        g_loaded, s_steps, s_counted, gates_ready, gates_stored = (sem("search_loaded"), sem("search_vector_steps"), sem("search_counted"),
                                                                   sem("gates_ready"), sem("gates_stored"))
        gb_in = [sem("gates_rows_in0"), sem("gates_rows_in1")]
        m_w1, m_gelu, m_hi, m_lo, m_w2 = sem("p4_w1_done"), sem("p4_gelu_ready"), sem("p4_hidden_hi_ready"), sem("p4_hidden_lo_ready"), sem("p4_w2_done")
        m_gy, m_acc, m_turn, m_out, stored = sem("p4_gated"), sem("p4_summed"), sem("p4_turned"), sem("p4_out_ready"), sem("p4_out_stored")

        xv = x_in.rearrange("(n p) c -> p n c", p=P)
        outv = out.rearrange("(n p) c -> p n c", p=P)
        chunks_per_tile = CHUNKS

        block = ctx.enter_context(nc.Block())

        @block.sync
        def _(sp):
            sp.dma_start(x[:, 0:TB, :], xv[:, 0:TB, :]).then_inc(x_first_in, 16)
            sp.dma_start(cst[:, :], consts).then_inc(consts_in, 16)
            sp.dma_start(wts[:, :], weights).then_inc(weights_in, 16)
            sp.dma_start(vec[:, :], vectors).then_inc(weights_in, 16)
            sp.dma_start(x[:, TB:BLK, :], xv[:, TB:BLK, :]).then_inc(x_rest_in, 16)
            sp.dma_start(int_raw, ints).then_inc(ints_in, 16)
            sp.dma_start(lat, latent).then_inc(weights_in, 16)
            sp.wait_ge(setup, 5)
            sp.dma_start(raw, w1_in).then_inc(raw_in, 16)
            sp.wait_ge(w_split, 2 * NT)
            sp.dma_start(raw, w2_in).then_inc(raw_in, 16)

            def store_logits(s, par):
                sp.wait_ge(g_copied, s + 1)
                at = bass.ds(s * TILE, TILE) if not isinstance(s, int) else slice(s * TILE, (s + 1) * TILE)
                sp.dma_start(logits_dram[:, at], lgT[0:EXPERTS, par, :]).then_inc(g_stored[par], 16)
            for s in range(2):
                store_logits(s, s)
            with sp.Fori(1, NT // 2) as i:
                store_logits(2 * i, 0)
                store_logits(2 * i + 1, 1)
            for par in range(2):
                sp.wait_ge(g_stored[par], 16 * NT // 2)
            sp.dma_start(lg, logits_dram.rearrange("e (q t) -> (e q) t", t=PAIRS // P)).then_inc(g_loaded, 16)
            sp.wait_ge(gates_ready, 1)
            sp.dma_start(gates_dram, lg).then_inc(gates_stored, 16)
            sp.wait_ge(gates_stored, 16)
            rows = gates_dram.rearrange("(e q) t -> e (q t)", e=EXPERTS)

            def expert_gates(tt, e):
                if not (isinstance(tt, int) and tt == 0 and e < 2):
                    sp.wait_ge(m_gy, tt * EXPERTS + e - 1)
                at = bass.ds(tt * MT, MT) if not isinstance(tt, int) else slice(tt * MT, (tt + 1) * MT)
                sp.dma_start(gbc[:, e % 2, :], rows[e:e + 1, at].partition_broadcast(P)).then_inc(gb_in[e % 2], 16)

            def store_out(tt):
                sp.wait_ge(m_out, tt + 1)
                at = bass.ds(tt * (MT // P), MT // P) if not isinstance(tt, int) else slice(tt * (MT // P), (tt + 1) * (MT // P))
                sp.dma_start(outv[:, at, :], yout).then_inc(stored, 16)

            for e in range(EXPERTS):
                expert_gates(0, e)
            with sp.Fori(1, NMT) as tt:
                for e in range(EXPERTS):
                    expert_gates(tt, e)
                    if e == 3:
                        store_out(tt - 1)
            store_out(NMT - 1)
            sp.wait_ge(stored, 16 * NMT)

        @block.gpsimd
        def _(pool):
            pool.memset(minus_half[:, :], -0.5).then_inc(pool_setup, 1)
            for a in range(2):
                pool.memset(xT[:, a, :, 0:1], 0.0).then_inc(pool_setup, 1)
            pool.memset(x[:, BLK:BLK + TB, :], 0.0).then_inc(pool_setup, 1)
            pool.wait_ge(pool_setup, 4)
            norm_rstd(pool, norms[0], 0, 0)

            def split(s, hi, lo, base):
                if not live(s):
                    return
                at = bass.ds(s * SPLIT, SPLIT) if not isinstance(s, int) else slice(s * SPLIT, (s + 1) * SPLIT)
                pool.tensor_copy(hi[:, at], raw[:, at]).then_inc(w_split, 1)
                pool.wait_ge(w_split, base + 2 * s + 1)
                pool.sem_inc(pool_passed, 1)
                pool.tensor_tensor(lo[:, at], raw[:, at], hi[:, at].bitcast(F32), ALU.subtract).then_inc(w_split, 1)

            pool.wait_ge(raw_in, 16)

            def phase1(s, par):
                norm_rstd(pool, norms[0], s + 1, 1 - par)
                split(s, w1h, w1l, 0)

            tile_steps(pool, phase1, 2)
            norm_rstd(pool, norms[1], 0, 0)
            pool.wait_ge(raw_in, 32)

            def phase2(s, par):
                norm_rstd(pool, norms[1], s + 1, 1 - par)
                split(s, w2h, w2l, 2 * NT)

            tile_steps(pool, phase2, 2)
            norm_rstd(pool, norms[2], 0, 0)

            def phase3(s, par):
                t = s - 1
                if live(t):
                    for u in range(8):
                        k = t * 8 + u
                        b, g = u // 4, u % 4
                        if u == 0:
                            pool.wait_ge(a_qk, t * 8 + 4)
                        if not (isinstance(t, int) and t == 0 and u < 2):
                            pool.wait_ge(a_s, 2 * k - 2)
                        pool.sem_inc(pool_passed, 1)
                        for h in range(4):
                            pool.tensor_scalar(kbd[:, u % 2, h // 2, :, h % 2, :],
                                               ks[:, 1 - par, g, b * T:(b + 1) * T].rearrange("p (j k) -> p j k", j=4),
                                               cst[:, C_SLOT + h:C_SLOT + h + 1], 0.0, ALU.mult, ALU.add).then_inc(a_kb, 1)
                norm_rstd(pool, norms[2], s + 1, 1 - par)

            tile_steps(pool, phase3, 2)
            norm_rstd(pool, norms[3], 0, 0)
            tile_steps(pool, lambda s, par: norm_rstd(pool, norms[3], s + 1, 1 - par), 2)

        @block.scalar
        def _(act):
            act.wait_ge(weights_in, 48)
            act.activation(ew[:, 0:1], vec[:, V_DECAY:V_DECAY + 1], ACT.Exp).then_inc(act_setup, 1)
            act.wait_ge(act_setup, 1)
            act.activation(ew[:, 1:2], ew[:, 0:1], ACT.Exp, scale=-1.0).then_inc(act_setup, 1)
            act.wait_ge(pool_setup, 4)

            def phase1(s, par):
                if not live(s):
                    return
                act.wait_ge(norms[0].turned, s + 1)
                if not isinstance(s, int) or s >= 2:
                    act.wait_ge(proj_done, (s - 1) * 3)
                act.activation(xT[:, par, :, 1:T + 1], ps[:, 0, :].rearrange("p (b t) -> p b t", b=SEQS),
                               ACT.Copy).then_inc(xT_ready, 1)
                if not isinstance(s, int) or s >= 2:
                    act.wait_ge(chain1, (s - 1) * C1)
                act.wait_ge(proj_done, s * 3 + 1)
                act.activation(ek[:, par, :], ps[:, 1, :], ACT.Exp).then_inc(act1, 1)
                act.activation(eu[:, par, :], ps[:, 1, :], ACT.Exp, bias=vec[:, V_FIRST:V_FIRST + 1]).then_inc(act1, 1)
                act.wait_ge(proj_done, s * 3 + 3)
                act.activation(th[:, par, :], ps[:, 3, :], ACT.Tanh, scale=0.5).then_inc(act1, 1)

            tile_steps(act, phase1, 2)

            def phase2(s, par):
                if not live(s):
                    return
                act.wait_ge(norms[1].turned, s + 1)
                if not isinstance(s, int) or s >= 2:
                    act.wait_ge(fg_done, (s - 1) * FJ)
                act.activation(fxh[:, par, :], ps[:, 0, :], ACT.Copy).then_inc(f_hi, 1)
                for j in range(FJ):
                    act.wait_ge(fg_done, s * FJ + j + 1)
                    if not isinstance(s, int) or s >= 1:
                        act.wait_ge(chain2, (s - 1) * FJ + j + 1)
                    act.activation(ft[:, j, :], ps[:, 1 + 2 * j, :], ACT.Tanh, scale=0.5 / 127.0).then_inc(f_tanh, 1)

            tile_steps(act, phase2, 2)

            def phase3(s, par):
                if live(s):
                    act.wait_ge(norms[2].turned, s + 1)
                    if not isinstance(s, int) or s >= 2:
                        act.wait_ge(a_vdone, s - 1)
                        act.wait_ge(a_proj, (s - 1) * 8)
                    act.activation(axh[:, par, :], ps[:, 0, :], ACT.Copy).then_inc(a_x, 1)
                for u in range(8):
                    if live(s - 1):
                        k = (s - 1) * 8 + u
                        if not (isinstance(s, int) and s == 1 and u < 4):
                            act.wait_ge(a_av, (s - 1) * 4 + u // 2 - 1)
                        act.wait_ge(a_cl, 2 * k + 1)
                        act.activation(prxy[:, u % 4, :, :], clxy, ACT.Exp, scale=12.0 ** -0.5).then_inc(a_p, 1)
                        act.wait_ge(a_cl, 2 * k + 2)
                        act.activation(prz[:, u % 4, :, :], clz, ACT.Exp, scale=12.0 ** -0.5).then_inc(a_p, 1)
                    if u == 1 and live(s):
                        copy_v(s, par)
                    if live(s - 1) and u in (2, 4, 6):
                        copy_av(s - 1, 1 - par, u // 2 - 1)
                    if live(s - 2) and u in (3, 5, 7):
                        copy_oT(s - 2, (u - 3) // 2)
                if live(s - 1):
                    copy_av(s - 1, 1 - par, 3)
                if live(s - 2):
                    copy_oT(s - 2, 3)

            def copy_v(t, par):
                act.wait_ge(a_vdone, t + 1)
                if not isinstance(t, int) or t >= 2:
                    act.wait_ge(a_av, (t - 1) * 4)
                for i in range(2):
                    for odd in range(2):
                        src = ps[odd * 64:odd * 64 + 64, 0, :].rearrange("p (n q i d) -> p n q i d", n=TB, q=8, i=2)
                        dst = vx[i * 64:i * 64 + 64, par, :, :, i, 0:DH].rearrange("p (n o) q d -> p n o q d", o=2)
                        act.activation(dst[:, :, odd, :, :], src[:, :, :, i, :], ACT.Copy).then_inc(a_vready, 1)

            def copy_av(t, par, w):
                act.wait_ge(a_av, t * 4 + w + 1)
                if w == 0 and not (isinstance(t, int) and t < 2):
                    act.wait_ge(a_f1, (t - 1) * 4)
                act.activation(ot[:, par, w // 2, w % 2, :], ps[:, 5 + w % 2, 0:T], ACT.Copy).then_inc(a_ot, 1)

            def copy_oT(t, q):
                act.wait_ge(a_f2, t * 4 + q + 1)
                if not (isinstance(t, int) and t == 0 and q == 0):
                    act.wait_ge(a_wo, t * 4 + q)
                act.activation(oT, ps[:, 7, 256:384], ACT.Copy).then_inc(a_oT, 1)

            tile_steps(act, phase3, 2)

            act.wait_ge(resid3, NT * TB)

            def logits(s, par):
                if not live(s):
                    return
                act.wait_ge(norms[3].turned, s + 1)
                at = bass.ds(s * TILE, TILE) if not isinstance(s, int) else slice(s * TILE, (s + 1) * TILE)
                act.activation(xh[:, at], ps[:, par, :], ACT.Copy).then_inc(g_hi, 1)
                act.wait_ge(g_mm, s + 1)
                if not isinstance(s, int) or s >= 2:
                    act.wait_ge(g_stored[par], (s - par) * 8)
                act.activation(lgT[0:EXPERTS, par, :], ps[0:EXPERTS, 2 + par, :], ACT.Copy).then_inc(g_copied, 1)

            tile_steps(act, logits, 2)

            def experts(tt):
                for c in range(CHUNKS):
                    k = tt * CHUNKS + c
                    par = c % 2
                    act.wait_ge(m_w1, k + 1)
                    if not (isinstance(tt, int) and tt == 0 and c < 2):
                        act.wait_ge(m_lo, k - 1)
                        act.wait_ge(m_w2, k - 1)
                    act.activation(h32[:, par, :], ps[:, 2 * par:2 * par + 2, :].rearrange("p a t -> p (a t)"),
                                   ACT.Gelu_apprx_tanh, bias=vec[:, V_B1 + c:V_B1 + c + 1]).then_inc(m_gelu, 1)
                    act.wait_ge(m_gelu, k + 1)
                    act.activation(hh[:, par, :], h32[:, par, :], ACT.Copy).then_inc(m_hi, 1)

            experts(0)
            with act.Fori(1, NMT) as tt:
                experts(tt)

        @block.vector
        def _(dve):
            dve.memset(sa[:, :, 0:1], 0.0).then_inc(setup, 1)
            dve.memset(sden[:, :, 0:1], 0.0).then_inc(setup, 1)
            dve.wait_ge(x_first_in, 16)
            dve.wait_ge(pool_setup, 4)
            norm_stats(dve, norms[0], 0, 0, [])
            dve.wait_ge(act_setup, 2)
            dve.wait_ge(consts_in, 16)
            dve.tensor_scalar(decay, cst[:, C_ONES:C_ONES + 1].broadcast_to([P, T]), ew[:, 1:2], None, ALU.mult).then_inc(setup, 1)
            dve.wait_ge(weights_in, 48)
            dve.tensor_scalar(other, vec[:, V_MK:V_MK + 3], -1.0, 1.0, ALU.mult, ALU.add).then_inc(mix_steps, 1)
            dve.wait_ge(mix_steps, 1)
            for m, w in enumerate((W_K, W_V, W_R)):
                dve.tensor_scalar(wmix[:, m, 0, :], wts[:, w:w + P], vec[:, m:m + 1], None, ALU.mult).then_inc(mix_steps, 1)
                dve.tensor_scalar(wmix[:, m, 1, :], wts[:, w:w + P], other[:, m:m + 1], None, ALU.mult).then_inc(mix_steps, 1)
            dve.wait_ge(ints_in, 16)
            dve.tensor_copy(wgu, int_raw[:, 0:2 * HIDDEN]).then_inc(setup, 1)
            dve.tensor_copy(wdn, int_raw[:, 2 * HIDDEN:3 * HIDDEN]).then_inc(setup, 1)
            dve.wait_ge(weights_in, 48)
            dve.tensor_copy(gate_hi[:, :], vec[:, V_GATE:V_GATE + EXPERTS]).then_inc(w_gw, 1)
            dve.wait_ge(w_gw, 1)
            dve.tensor_tensor(gate_lo[:, :], vec[:, V_GATE:V_GATE + EXPERTS], gate_hi[:, :].bitcast(F32), ALU.subtract).then_inc(w_gw, 1)
            dve.wait_ge(setup, 5)
            dve.wait_ge(comb, 1)
            gp = GROUPS * P
            dve.tensor_copy(wqkv_hi[:, 0:gp], ps[:, 7, :]).then_inc(wsteps, 1)
            dve.wait_ge(comb, 2)
            wk = wts[:, W_KROPE:W_KROPE + gp]
            dve.tensor_tensor(wk, ps[:, 6, :], wk, ALU.add).then_inc(wsteps, 1)
            dve.wait_ge(comb, 3)
            dve.tensor_copy(wqkv_hi[:, 2 * gp:2 * gp + P], ps[:, 5, 0:P]).then_inc(wsteps, 1)
            dve.wait_ge(wsteps, 2)
            dve.tensor_copy(wqkv_hi[:, gp:2 * gp], wk).then_inc(wsteps, 1)
            dve.wait_ge(wsteps, 4)
            dve.tensor_tensor(wqkv_lo[:, 0:gp], ps[:, 7, :], wqkv_hi[:, 0:gp].bitcast(F32), ALU.subtract).then_inc(comb_copied, 1)
            dve.tensor_tensor(wqkv_lo[:, gp:2 * gp], wk, wqkv_hi[:, gp:2 * gp].bitcast(F32), ALU.subtract).then_inc(comb_copied, 1)
            dve.tensor_tensor(wqkv_lo[:, 2 * gp:2 * gp + P], ps[:, 5, 0:P], wqkv_hi[:, 2 * gp:2 * gp + P].bitcast(F32),
                              ALU.subtract).then_inc(comb_copied, 1)
            dve.wait_ge(x_rest_in, 16)

            def residual(t, done, scale, added, bank):
                dve.wait_ge(done, t + 1)
                xt = blocks(t)
                dve.scalar_tensor_tensor(xt, ps[:, bank, :].rearrange("p (n c) -> p n c", n=TB), scale, xt,
                                         ALU.mult, ALU.add).then_inc(added, 1)

            def phase1(s, par):
                norm_apply(dve, norms[0], s, par)
                norm_stats(dve, norms[0], s + 1, 1 - par, [])
                if live(s - 2):
                    residual(s - 2, o_done, 0.5, resid1, 6)
                t = s - 1
                if not live(t):
                    return
                q = 1 - par
                base = t * C1
                dve.wait_ge(proj_done, t * 3 + 2)
                dve.wait_ge(act1, t * 3 + 2)
                if not isinstance(t, int) or t >= 1:
                    dve.wait_ge(chain1, base)
                dve.tensor_tensor(kv, ps[:, 2, :], ek[:, q, :], ALU.mult).then_inc(chain1, 1)
                dve.tensor_tensor(nu, ps[:, 2, :], eu[:, q, :], ALU.mult).then_inc(chain1, 1)
                dve.wait_ge(chain1, base + 1)
                for b in range(SEQS):
                    dve.tensor_tensor_scan(sa[:, b, 1:T + 1], decay, kv[:, b * T:(b + 1) * T], 0.0,
                                           ALU.mult, ALU.add).then_inc(chain1, 1)
                dve.wait_ge(sums_done, t * 2 + 2)
                for b in range(SEQS):
                    dve.tensor_tensor_scan(sden[:, b, 1:T + 1], decay, ps[:, 4, b * T:(b + 1) * T], 0.0,
                                           ALU.mult, ALU.add).then_inc(chain1, 1)
                dve.wait_ge(chain1, base + 6)
                as_seqs = lambda a: a.rearrange("p (b t) -> p b t", b=SEQS)
                dve.scalar_tensor_tensor(as_seqs(den), as_seqs(ps[:, 5, :]), 1e-6, sden[:, :, 0:T], ALU.max, ALU.add).then_inc(chain1, 1)
                dve.tensor_tensor(as_seqs(num), as_seqs(nu), sa[:, :, 0:T], ALU.add).then_inc(chain1, 1)
                dve.wait_ge(chain1, base + 7)
                dve.reciprocal(rec, den).then_inc(chain1, 1)
                dve.wait_ge(chain1, base + 9)
                dve.tensor_tensor(wkv, num, rec, ALU.mult).then_inc(chain1, 1)
                dve.wait_ge(chain1, base + 10)
                dve.wait_ge(act1, t * 3 + 3)
                if not isinstance(t, int) or t >= 2:
                    dve.wait_ge(o_done, t - 1)
                dve.scalar_tensor_tensor(gated[:, q, :], th[:, q, :], 1.0, wkv, ALU.add, ALU.mult).then_inc(chain1, 1)

            tile_steps(dve, phase1, 2)

            def phase2(s, par):
                norm_apply(dve, norms[1], s, par)
                norm_stats(dve, norms[1], s + 1, 1 - par, [])
                if live(s - 2):
                    residual(s - 2, f_down, 0.5 / 127.0 ** 3, resid2, 7)
                if live(s):
                    dve.wait_ge(f_hi, s + 1)
                    if not isinstance(s, int) or s >= 2:
                        dve.wait_ge(fg_done, (s - 1) * FJ)
                    dve.tensor_tensor(fxl[:, par, :], ps[:, 0, :], fxh[:, par, :].bitcast(F32), ALU.subtract).then_inc(f_lo, 1)
                t = s - 1
                if not live(t):
                    return
                q = 1 - par
                if not isinstance(t, int) or t >= 1:
                    dve.wait_ge(f_h, t * FJ)
                for j in range(FJ):
                    dve.wait_ge(f_tanh, t * FJ + j + 1)
                    dve.scalar_tensor_tensor(fu[:, j, :], ft[:, j, :], 1.0, ps[:, 1 + 2 * j, :],
                                             ALU.add, ALU.mult).then_inc(chain2, 1)
                for j in range(FJ):
                    dve.wait_ge(chain2, t * FJ + j + 1)
                    if j == 0 and (not isinstance(t, int) or t >= 2):
                        dve.wait_ge(f_down, t - 1)
                    dve.tensor_tensor(fh[:, q, j, :], fu[:, j, :], ps[:, 2 + 2 * j, :], ALU.mult).then_inc(f_h, 1)

            norm_stats(dve, norms[1], 0, 0, [(resid1, NT), (norms[0].rstd, NT + 1)])
            tile_steps(dve, phase2, 2)

            dve.wait_ge(o_done, NT)
            dve.wait_ge(f_down, NT)
            dve.wait_ge(w_split, 4 * NT)
            for a in range(2):
                dve.memset(vx[:, a, :, :, :, :].rearrange("p j q i s -> p (j q i s)"), 0.0).then_inc(setup, 1)
            dve.wait_ge(setup, 7)
            for a in range(2):
                for i in range(2):
                    dve.memset(vx[i * 64:i * 64 + 64, a, :, :, i, DH:DH + 1], 1.0).then_inc(setup, 1)

            def table(col, a):
                return cst[:, col:col + T].unsqueeze(1).broadcast_to([P, SEQS, T])

            def project_done(t, par, piece):
                dve.wait_ge(a_proj, t * 8 + piece + 1)
                if piece == 0 and (not isinstance(t, int) or t >= 2):
                    dve.wait_ge(a_kb, (t - 1) * 32)
                if piece == 4 and (not isinstance(t, int) or t >= 2):
                    dve.wait_ge(a_s, (t - 1) * 16)
                dst = (ks, qs)[piece // 4][:, par, piece % 4, :]
                dve.tensor_tensor(dst.rearrange("p (b t) -> p b t", b=SEQS), ps[:, 1, :].rearrange("p (b t) -> p b t", b=SEQS),
                                  table((C_TABK, C_TABQ)[piece // 4], 0), ALU.mult).then_inc(a_qk, 1)

            def normalise(t, q):
                dve.wait_ge(a_f1, t * 4 + q + 1)
                heads = ps[:, 7, 0:256].rearrange("p (h s) -> p h s", h=HEADS)
                dve.reciprocal(oden, heads[:, :, DH]).then_inc(a_fd, 1)
                dve.wait_ge(a_fd, t * 4 + q + 1)
                dve.tensor_tensor(otok, heads[:, :, 0:DH], oden.unsqueeze(2).broadcast_to([P, HEADS, DH]), ALU.mult).then_inc(a_ftok, 1)

            def add_block(t, q):
                dve.wait_ge(a_wo, t * 4 + q + 1)
                xt = blocks(t)[:, q, :]
                dve.tensor_tensor(xt, ps[:, 7, 384:512], xt, ALU.add).then_inc(resid3, 1)

            limxy = cst[:, C_LIM:C_LIM + XY].unsqueeze(1).broadcast_to([P, 2, XY])
            limz = cst[:, C_LIM + XY:C_LIM + XY + ZC].unsqueeze(1).broadcast_to([P, 2, ZC])

            def phase3(s, par):
                norm_apply(dve, norms[2], s, par)
                norm_stats(dve, norms[2], s + 1, 1 - par, [])
                if live(s):
                    dve.wait_ge(a_x, s + 1)
                    if not isinstance(s, int) or s >= 2:
                        dve.wait_ge(a_proj, (s - 1) * 8)
                        dve.wait_ge(a_vdone, s - 1)
                    dve.tensor_tensor(axl[:, par, :], ps[:, 0, :], axh[:, par, :].bitcast(F32), ALU.subtract).then_inc(axl_ready, 1)
                for u in range(8):
                    if live(s - 1):
                        k = (s - 1) * 8 + u
                        first = isinstance(s, int) and s == 1 and u == 0
                        dve.wait_ge(a_s, 2 * k + 1)
                        if not first:
                            dve.wait_ge(a_p, 2 * k - 1)
                        dve.scalar_tensor_tensor(clxy, ps[:, 2:4, 0:XY], -CLIP, limxy, ALU.max, ALU.min).then_inc(a_cl, 1)
                        dve.wait_ge(a_s, 2 * k + 2)
                        if not first:
                            dve.wait_ge(a_p, 2 * k)
                        dve.scalar_tensor_tensor(clz, ps[:, 4, 0:2 * ZC].rearrange("p (q t) -> p q t", q=2), -CLIP, limz,
                                                 ALU.max, ALU.min).then_inc(a_cl, 1)
                    if live(s) and u >= 1:
                        project_done(s, par, u - 1)
                    if live(s - 2):
                        if u in (2, 4, 6):
                            normalise(s - 2, (u - 2) // 2)
                        if u in (3, 5, 7):
                            add_block(s - 2, (u - 3) // 2)
                if live(s):
                    project_done(s, par, 7)
                if live(s - 2):
                    normalise(s - 2, 3)
                    add_block(s - 2, 3)

            norm_stats(dve, norms[2], 0, 0, [(resid2, NT), (norms[1].rstd, NT + 1)])
            tile_steps(dve, phase3, 2)

            def logits(s, par):
                norm_apply(dve, norms[3], s, par)
                norm_stats(dve, norms[3], s + 1, 1 - par, [])
                if live(s):
                    dve.wait_ge(g_hi, s + 1)
                    at = bass.ds(s * TILE, TILE) if not isinstance(s, int) else slice(s * TILE, (s + 1) * TILE)
                    dve.tensor_tensor(xl[:, at], ps[:, par, :], xh[:, at].bitcast(F32), ALU.subtract).then_inc(g_lo, 1)

            norm_stats(dve, norms[3], 0, 0, [(resid3, NT * TB), (norms[2].rstd, NT + 1)])
            tile_steps(dve, logits, 2)

            steps = [0]

            def link(ins):
                ins.then_inc(s_steps, 1)
                steps[0] += 1
                dve.wait_ge(s_steps, steps[0])

            sgn, limit, part, m, cand, take, kth = (small[:, i:i + 1] for i in range(7))
            bits = small[:, 7:8]
            dve.wait_ge(g_loaded, 16)
            link(dve.tensor_scalar(zs, lg, 0.0, None, ALU.is_lt, ALU.add, accum_out=part))
            dve.wait_ge(s_counted, 1)
            link(dve.tensor_scalar(take, ps[:, 7, 0:1], float(KTH), None, ALU.is_ge))
            link(dve.tensor_scalar(sgn, take, -2.0, 1.0, ALU.mult, ALU.add))
            link(dve.tensor_scalar(limit, take, float(PAIRS - KTH - (KTH - 1)), float(KTH - 1), ALU.mult, ALU.add))
            link(dve.tensor_scalar(z, lg, sgn, None, ALU.mult))
            link(dve.memset(m, 0.0))
            for bit in range(30, -1, -1):
                link(dve.tensor_scalar(cand.bitcast(I32), m.bitcast(I32), 1 << bit, None, ALU.bitwise_or))
                link(dve.tensor_scalar(zs, z, cand, None, ALU.is_lt, ALU.add, accum_out=part))
                dve.wait_ge(s_counted, 32 - bit)
                link(dve.tensor_tensor(take.bitcast(I32), ps[:, 7, 0:1], limit, ALU.is_le))
                link(dve.copy_predicated(m, take.bitcast(I32), cand))
            link(dve.tensor_scalar(kth, m, sgn, None, ALU.mult))
            link(dve.scalar_tensor_tensor(zs, lg, kth, lg, ALU.is_ge, ALU.mult))
            dve.tensor_copy(lg, zs).then_inc(gates_ready, 1)

            def finish(tt, last):
                if not isinstance(tt, int) or tt >= 1:
                    dve.wait_ge(stored, tt * 16)
                for half in range(2):
                    dve.wait_ge(m_turn, tt * 2 + half + 1)
                    at = bass.ds(tt * 8 + 4 * half, 4) if not isinstance(tt, int) else slice(tt * 8 + 4 * half, tt * 8 + 4 * half + 4)
                    ins = dve.tensor_tensor(yout[:, 4 * half:4 * half + 4, :], ps[:, 6 + half, :].rearrange("p (n c) -> p n c", n=4),
                                            x[:, at, :], ALU.add)
                    if half:
                        dve_half = ins.then_inc(m_out, 1)
                    else:
                        ins.then_inc(m_half, 1)
                dve.wait_ge(m_half, tt + 1)
                dve.wait_ge(m_out, tt + 1)

            def experts(tt):
                for c in range(CHUNKS):
                    k = tt * CHUNKS + c
                    par = c % 2
                    dve.wait_ge(m_hi, k + 1)
                    if not (isinstance(tt, int) and tt == 0 and c < 2):
                        dve.wait_ge(m_w2, k - 1)
                    dve.tensor_tensor(hl[:, par, :], h32[:, par, :], hh[:, par, :].bitcast(F32), ALU.subtract).then_inc(m_lo, 1)
                    if c == 2 and not (isinstance(tt, int) and tt == 0):
                        finish(tt - 1, False)
                    if c % EC == 1 and c > EC:
                        gate(tt, c // EC - 1)
                gate(tt, EXPERTS - 1)

            def gate(tt, e):
                n = tt * EXPERTS + e
                dve.wait_ge(m_w2, tt * CHUNKS + (e + 1) * EC)
                dve.wait_ge(gb_in[e % 2], (tt * (EXPERTS // 2) + e // 2 + 1) * 16)
                dst = acc if e == 0 else gy
                y = ps[:, 4 + 2 * (e % 2):6 + 2 * (e % 2), :].rearrange("p a t -> p (a t)")
                if e == 0 and not (isinstance(tt, int) and tt == 0):
                    dve.wait_ge(m_turn, tt * 2)
                if not (isinstance(tt, int) and tt == 0 and e == 0):
                    dve.wait_ge(m_acc, n)
                ins = dve.scalar_tensor_tensor(dst, y, vec[:, V_B2 + e:V_B2 + e + 1], gbc[:, e % 2, :], ALU.add, ALU.mult)
                ins.then_inc(m_gy, 1)
                dve.wait_ge(m_gy, n + 1)
                if e == 0:
                    dve.sem_inc(m_acc, 1)
                else:
                    dve.tensor_tensor(acc, acc, gy, ALU.add).then_inc(m_acc, 1)

            experts(0)
            with dve.Fori(1, NMT) as tt:
                experts(tt)
            finish(NMT - 1, True)

        @block.tensor
        def _(pe):
            pe.wait_ge(weights_in, 48)
            pe.wait_ge(consts_in, 16)
            pe.matmul(ps[:, 7, :], lat[:, L_DQ:L_DQ + P], lat[:, L_UQ:L_UQ + 512], start=True, stop=True).then_inc(comb, 1)
            pe.matmul(ps[:, 6, :], lat[:, L_DKV:L_DKV + P], lat[:, L_UK:L_UK + 512], start=True, stop=True).then_inc(comb, 1)
            pe.matmul(ps[:, 5, 0:P], lat[:, L_DKV:L_DKV + P], lat[:, L_UV:L_UV + P], start=True, stop=True).then_inc(comb, 1)
            pe.wait_ge(comb_copied, 3)
            pe.wait_ge(mix_steps, 7)

            def phase1(s, par):
                if live(s):
                    if not isinstance(s, int) or s >= 1:
                        pe.wait_ge(xT_ready, s)
                    norm_turn(pe, norms[0], s, par, 0)
                    pe.wait_ge(xT_ready, s + 1)
                    if not isinstance(s, int) or s >= 1:
                        pe.wait_ge(act1, s * 3)
                    for m in range(3):
                        if m == 1 and (not isinstance(s, int) or s >= 1):
                            pe.wait_ge(chain1, (s - 1) * C1 + 2)
                        dst = ps[:, 1 + m, :].rearrange("p (b t) -> p b t", b=SEQS)
                        pe.matmul(dst, wmix[:, m, 0, :], xT[:, par, :, 1:T + 1], start=True, stop=False)
                        pe.matmul(dst, wmix[:, m, 1, :], xT[:, par, :, 0:T], start=False, stop=True).then_inc(proj_done, 1)
                    for i, e in enumerate((ek, eu)):
                        pe.wait_ge(act1, s * 3 + 1 + i)
                        if not isinstance(s, int) or s >= 1:
                            pe.wait_ge(chain1, (s - 1) * C1 + 7)
                        pe.matmul(ps[:, 4 + i, :], cst[:, C_HEAD:C_HEAD + P], e[:, par, :], start=True, stop=True).then_inc(sums_done, 1)
                t = s - 1
                if live(t):
                    pe.wait_ge(chain1, (t + 1) * C1)
                    if not isinstance(t, int) or t >= 1:
                        pe.wait_ge(resid1, t)
                    for j in range(TB):
                        mm = pe.matmul(ps[:, 6, j * P:(j + 1) * P], gated[:, 1 - par, j * P:(j + 1) * P],
                                       wts[:, W_O0:W_O0 + P], start=True, stop=True)
                    mm.then_inc(o_done, 1)

            tile_steps(pe, phase1, 2)
            pe.wait_ge(resid1, NT)

            def phase2(s, par):
                if live(s):
                    if not isinstance(s, int) or s >= 1:
                        pe.wait_ge(f_lo, s)
                    norm_turn(pe, norms[1], s, par, 0)
                    pe.wait_ge(f_lo, s + 1)
                    for j in range(FJ):
                        if not isinstance(s, int) or s >= 1:
                            pe.wait_ge(f_h, (s - 1) * FJ + j + 1)
                        for i in range(2):
                            w = wgu[:, (i * FJ + j) * P:(i * FJ + j + 1) * P]
                            pe.matmul(ps[:, 1 + 2 * j + i, :], w, fxh[:, par, :], start=True, stop=False)
                            mm = pe.matmul(ps[:, 1 + 2 * j + i, :], w, fxl[:, par, :], start=False, stop=True)
                        mm.then_inc(fg_done, 1)
                t = s - 1
                if live(t):
                    pe.wait_ge(f_h, (t + 1) * FJ)
                    if not isinstance(t, int) or t >= 1:
                        pe.wait_ge(resid2, t)
                    for b in range(TB):
                        for j in range(FJ):
                            mm = pe.matmul(ps[:, 7, b * P:(b + 1) * P], fh[:, 1 - par, j, b * P:(b + 1) * P],
                                           wdn[:, j * P:(j + 1) * P], start=(j == 0), stop=(j == FJ - 1))
                    mm.then_inc(f_down, 1)

            tile_steps(pe, phase2, 2)
            pe.wait_ge(resid2, NT)
            pe.wait_ge(setup, 11)

            def project(t, par, piece):
                if not (isinstance(t, int) and t == 0 and piece == 0):
                    pe.wait_ge(a_qk, t * 8 + piece)
                o = ((piece + 4) % 8) * P
                for i, (w, xs) in enumerate(((wqkv_hi, axh), (wqkv_lo, axh), (wqkv_hi, axl))):
                    if i == 2 and piece == 0:
                        pe.wait_ge(axl_ready, t + 1)
                    mm = pe.matmul(ps[:, 1, :], w[:, o:o + P], xs[:, par, :], start=(i == 0), stop=(i == 2))
                mm.then_inc(a_proj, 1)

            def values(t, par):
                pe.wait_ge(a_x, t + 1)
                pe.wait_ge(axl_ready, t + 1)
                o = 2 * GROUPS * P
                for n in range(TB):
                    toks = slice(n * P, (n + 1) * P)
                    for i, (xs, w) in enumerate(((axh, wqkv_hi), (axl, wqkv_hi), (axh, wqkv_lo))):
                        mm = pe.matmul(ps[:, 0, toks], xs[:, par, toks], w[:, o:o + P], start=(i == 0), stop=(i == 2))
                mm.then_inc(a_vdone, 1)

            def scores(t, par, u):
                k = t * 8 + u
                b, g = u // 4, u % 4
                first = isinstance(t, int) and t == 0 and u == 0
                if u == 0:
                    pe.wait_ge(a_qk, t * 8 + 8)
                pe.wait_ge(a_kb, 4 * k + 4)
                for part in range(2):
                    if not first:
                        pe.wait_ge(a_cl, 2 * k - 1 + part)
                    for pair in range(2):
                        for j in (2 * part, 2 * part + 1):
                            n = T - j * KB
                            at = (S_AT[j], pair * ZC + S_AT[j])[part]
                            mm = pe.matmul(ps[:, (2 + pair, 4)[part], at:at + n],
                                           kbd[:, u % 2, pair, j, :, :].rearrange("p i k -> p (i k)"),
                                           qs[:, par, g, b * T + j * KB:(b + 1) * T], start=True, stop=True)
                    mm.then_inc(a_s, 1)

            def weigh(t, par, w):
                b = w // 2
                pe.wait_ge(a_p, 2 * (t * 8 + 2 * w) + 4)
                if not (isinstance(t, int) and t == 0 and w < 2):
                    pe.wait_ge(a_ot, t * 4 + w - 1)
                for j in range(4):
                    n = T - j * KB
                    for q in range(4):
                        slot = (2 * w + q // 2) % 4
                        probs = (prxy, prz)[j // 2][:, slot, q % 2, S_AT[j]:S_AT[j] + n]
                        mm = pe.matmul(ps[SLOT * q:SLOT * q + SLOT, 5 + w % 2, T - n:T],
                                       vx[:, par, 4 * b + j, 4 * (w % 2) + q, :, :].rearrange("p i s -> p (i s)"),
                                       probs, start=(j == 0), stop=(j == 3))
                mm.then_inc(a_av, 1)

            def turn_out(t, par, q):
                if not (isinstance(t, int) and t == 0 and q == 0):
                    pe.wait_ge(resid3, t * 4 + q)
                b, half = q // 2, q % 2
                pe.wait_ge(a_ot, t * 4 + 2 * b + 2)
                for w in range(2):
                    mm = pe.transpose(ps[:, 7, w * P:(w + 1) * P], ot[:, par, b, w, half * P:(half + 1) * P], ident)
                mm.then_inc(a_f1, 1)

            def turn_back(t, q):
                pe.wait_ge(a_ftok, t * 4 + q + 1)
                pe.transpose(ps[:, 7, 256:384], otok.rearrange("p h d -> p (h d)"), ident).then_inc(a_f2, 1)

            def out_project(t, q):
                pe.wait_ge(a_oT, t * 4 + q + 1)
                pe.matmul(ps[:, 7, 384:512], oT, wts[:, W_O1:W_O1 + P], start=True, stop=True).then_inc(a_wo, 1)

            def phase3(s, par):
                if live(s):
                    if not isinstance(s, int) or s >= 1:
                        pe.wait_ge(a_vready, s * 4)
                    norm_turn(pe, norms[2], s, par, 0)
                for u in range(8):
                    if live(s - 1):
                        scores(s - 1, 1 - par, u)
                    if live(s):
                        if u == 1:
                            values(s, par)
                        if u >= 1:
                            project(s, par, u - 1)
                    if live(s - 1) and u in (2, 4, 6):
                        if u == 2:
                            pe.wait_ge(a_vready, s * 4)
                        weigh(s - 1, 1 - par, u // 2 - 1)
                    if live(s - 2):
                        if u in (2, 4, 6):
                            turn_out(s - 2, par, (u - 2) // 2)
                            turn_back(s - 2, (u - 2) // 2)
                        if u in (3, 5, 7):
                            out_project(s - 2, (u - 3) // 2)
                if live(s):
                    project(s, par, 7)
                if live(s - 1):
                    weigh(s - 1, 1 - par, 3)
                if live(s - 2):
                    turn_out(s - 2, par, 3)
                    turn_back(s - 2, 3)
                    out_project(s - 2, 3)

            tile_steps(pe, phase3, 2)
            pe.wait_ge(resid3, NT * TB)
            pe.wait_ge(w_gw, 2)

            def logits(s, par):
                if not live(s):
                    return
                if not isinstance(s, int) or s >= 2:
                    pe.wait_ge(g_lo, s - 1)
                norm_turn(pe, norms[3], s, par, par)
                pe.wait_ge(g_lo, s + 1)
                if not isinstance(s, int) or s >= 2:
                    pe.wait_ge(g_copied, s - 1)
                at = bass.ds(s * TILE, TILE) if not isinstance(s, int) else slice(s * TILE, (s + 1) * TILE)
                dst = ps[0:EXPERTS, 2 + par, :]
                pe.matmul(dst, gate_hi[:, :], xh[:, at], start=True, stop=False)
                pe.matmul(dst, gate_hi[:, :], xl[:, at], start=False, stop=False)
                pe.matmul(dst, gate_lo[:, :], xh[:, at], start=False, stop=True).then_inc(g_mm, 1)

            tile_steps(pe, logits, 2)
            for i in range(32):
                pe.wait_ge(s_steps, 1 if i == 0 else 6 + 4 * (i - 1) + 2)
                pe.matmul(ps[:, 7, 0:1], ones, small[:, 2:3], start=True, stop=True).then_inc(s_counted, 1)
            pe.wait_ge(w_split, 4 * NT)
            pe.wait_ge(g_copied, NT)

            def first(tt, c):
                k = tt * CHUNKS + c
                par = c % 2
                if not (isinstance(tt, int) and tt == 0 and c < 2):
                    pe.wait_ge(m_gelu, k - 1)
                w = slice(c * P, (c + 1) * P)
                for i, (wt, xs) in enumerate(((w1h, xh), (w1h, xl), (w1l, xh))):
                    for half in range(2):
                        o = tt * MT + half * 512
                        at = bass.ds(o, 512) if not isinstance(tt, int) else slice(o, o + 512)
                        mm = pe.matmul(ps[:, 2 * par + half, :], wt[:, w], xs[:, at], start=(i == 0), stop=(i == 2))
                mm.then_inc(m_w1, 1)

            def second(tt, c):
                k = tt * CHUNKS + c
                par = c % 2
                e, j = c // EC, c % EC
                if j == 0:
                    if not (isinstance(tt, int) and tt == 0 and e < 2):
                        pe.wait_ge(m_gy, tt * EXPERTS + e - 1)
                    if e == 1 and not (isinstance(tt, int) and tt == 0):
                        pe.wait_ge(m_out, tt)
                w = slice(c * P, (c + 1) * P)
                pe.wait_ge(m_hi, k + 1)
                for i, (wt, hs) in enumerate(((w2h, hh), (w2l, hh), (w2h, hl))):
                    if i == 2:
                        pe.wait_ge(m_lo, k + 1)
                    for half in range(2):
                        mm = pe.matmul(ps[:, 4 + 2 * (e % 2) + half, :], wt[:, w], hs[:, par, half * 512:half * 512 + 512],
                                       start=(j == 0 and i == 0), stop=(j == EC - 1 and i == 2))
                mm.then_inc(m_w2, 1)

            def turn_sum(tt):
                pe.wait_ge(m_acc, (tt + 1) * EXPERTS)
                for half in range(2):
                    for j in range(4):
                        mm = pe.transpose(ps[:, 6 + half, j * P:(j + 1) * P],
                                          acc[:, half * 512 + j * P:half * 512 + (j + 1) * P], ident)
                    mm.then_inc(m_turn, 1)

            def experts(tt):
                for c in range(CHUNKS + 1):
                    if c < CHUNKS:
                        first(tt, c)
                    if c == 2 and not (isinstance(tt, int) and tt == 0):
                        turn_sum(tt - 1)
                    if c:
                        second(tt, c - 1)

            experts(0)
            with pe.Fori(1, NMT) as tt:
                experts(tt)
            turn_sum(NMT - 1)


def kernel(**inputs):
    import concourse.bacc as _bacc
    from concourse.bass_utils import run_bass_kernel_spmd as _run

    a = {k: np.ascontiguousarray(v) for k, v in inputs.items()}
    f = np.float32
    weights = np.zeros((P, W_COLS), f)
    for at, name in ((W_K, "Wk"), (W_V, "Wv"), (W_R, "Wr"), (W_O0, "Wo")):
        weights[:, at:at + P] = a["L0_attn_" + name].T
    weights[:, W_O1:W_O1 + P] = a["L1_attn_W_O"]
    latent = np.zeros((32, L_COLS), f)
    latent[:, L_DQ:L_DQ + P] = a["L1_attn_W_DQ"].T
    latent[:, L_DKV:L_DKV + P] = a["L1_attn_W_DKV"].T
    latent[:, L_UV:L_UV + P] = a["L1_attn_W_UV"]
    for h in range(HEADS):
        o = h * SLOT
        latent[:, L_UQ + o:L_UQ + o + DH] = a["L1_attn_W_UQ"][:, h * DH:(h + 1) * DH]
        latent[:, L_UK + o:L_UK + o + DH] = a["L1_attn_W_UK"][:, h * DH:(h + 1) * DH]
        for p in range(DR // 2):
            for k in range(ROPE):
                col = o + DH + ROPE * p + k
                latent[:, L_UQ + col] = a["L1_attn_W_QR"][:, h * DR + 2 * p + Q_DIM[k]]
                weights[:, W_KROPE + col] = a["L1_attn_W_KR"][:, 2 * p + K_DIM[k]]
    vectors = np.zeros((P, V_COLS), f)
    for at, name in ((V_MK, "mix_k"), (V_MV, "mix_v"), (V_MR, "mix_r")):
        vectors[:, at] = a["L0_attn_" + name].reshape(C)
    vectors[:, V_DECAY] = np.repeat(a["L0_attn_time_decay"], DH)
    vectors[:, V_FIRST] = np.repeat(a["L0_attn_time_first"], DH)
    vectors[:, V_GATE:V_GATE + EXPERTS] = a["L1_ffn_gate_weight"].T
    vectors[:, V_B1:V_B1 + CHUNKS] = a["L1_ffn_b1"].reshape(CHUNKS, P).T
    vectors[:, V_B2:V_B2 + EXPERTS] = a["L1_ffn_b2"].T
    ints = np.concatenate([a["L0_ffn_w_gate"].T, a["L0_ffn_w_up"].T,
                           a["L0_ffn_w_down"].T.reshape(FJ, P, C).transpose(1, 0, 2).reshape(P, HIDDEN)], 1)
    w1 = a["L1_ffn_w1"].reshape(EXPERTS * HE, C).T
    w2 = a["L1_ffn_w2"].transpose(0, 2, 1).reshape(CHUNKS, P, C).transpose(1, 0, 2).reshape(P, CHUNKS * C)
    arrays = {"x_in": a["L0_attn_x"].reshape(N, C), "weights_in_dram": weights, "vectors_dram": vectors,
              "latent_dram": latent, "ints_dram": ints, "w1_dram": w1, "w2_dram": w2, "consts_dram": rope_tables()}
    arrays = {k: np.ascontiguousarray(v) for k, v in arrays.items()}
    nc = _bacc.Bacc("TRN2", target_bir_lowering=False, num_devices=1)
    args = [nc.dram_tensor(k, v.shape, mybir.dt.from_np(v.dtype), kind="ExternalInput").ap() for k, v in arrays.items()]
    args.append(nc.dram_tensor("out_dram", (N, C), F32, kind="ExternalOutput").ap())
    build(nc, *args)
    r = _run(nc, [arrays], core_ids=[0])
    return r.results[0]["out_dram"].reshape(BATCH, T, C)
```

```python
from contextlib import ExitStack

import concourse.bass as bass
import numpy as np
from concourse import mybir

F32 = mybir.dt.float32
R32 = mybir.dt.float32r
I32 = mybir.dt.int32
I16 = mybir.dt.int16
ALU = mybir.AluOpType
ACT = mybir.ActivationFunctionType

P = 128
BATCH, T, C = 16, 256, 128
N = BATCH * T
BLK = N // P
TILE = 512
NT = N // TILE
TB = TILE // P
SEQS = TILE // T
HEADS, DH, DR = 16, 8, 4
GROUPS = HEADS // 4
SLOT = 32
HIDDEN = 384
FJ = HIDDEN // P
EXPERTS, HE = 8, 512
EC = HE // P
CHUNKS = EXPERTS * EC
MT = 1024
NMT = N // MT
KTH = 4 * 128 * 6
PAIRS = N * EXPERTS
EPS = 1e-5
CLIP = 80.0
MASKED = -1.0e4
ROPE = 8
SLOT_COLS = DH + ROPE * (DR // 2)
Q_DIM = [0, 0, 1, 1, 0, 0, 1, 1]
K_DIM = [0, 1, 0, 1, 0, 1, 0, 1]
Q_SIN = [0, 0, 1, 1, 1, 1, 0, 0]
K_SIN = [0, 1, 0, 1, 1, 0, 1, 0]
SIGN = [1, -1, -1, 1, 1, 1, 1, 1]

SPLIT = CHUNKS * P // (N // 512)
ARENA = 25456

W_K, W_V, W_R, W_O0 = 0, 128, 256, 384
W_O1 = 512
W_KROPE = 640
W_COLS = W_KROPE + GROUPS * P
V_MK, V_MV, V_MR, V_DECAY, V_HDECAY, V_FIRST = range(6)
V_GATE = 6
V_B1 = V_GATE + EXPERTS
V_B2 = V_B1 + CHUNKS
V_COLS = V_B2 + EXPERTS
L_DQ, L_UQ, L_DKV, L_UK, L_UV = 0, 128, 640, 768, 1280
L_COLS = 1408
C_ID, C_ONES = 0, 128
C_SUM, C_SPREAD = 256, 512
LOW = 16
ROUNDS = LOW // 2
EARLY = 4
GATES_AT = 2 * (PAIRS // P)
AHEAD = 8
C_TABQ, C_TABK = 768, 768 + T
C_LIM = 768 + 2 * T
KB = T // 4
S_AT = [0, T, 0, P]
C_SLOT = C_LIM + 2 * T - KB + P + KB
C_STEP = C_SLOT + 4
C_COLS = C_STEP + 3
XY = 2 * T - KB
ZC = P + KB


def rope_tables():
    out = np.zeros((P, C_COLS), np.float32)
    out[:, C_ID:C_ID + P] = np.eye(P)
    out[:, C_ONES:C_ONES + P] = 1.0
    for h in range(HEADS):
        for b in range(SEQS):
            out[h * DH:h * DH + DH, C_SUM + b * P + b * HEADS + h] = 1.0
            out[b * HEADS + h, C_SPREAD + b * P + h * DH:C_SPREAD + b * P + h * DH + DH] = 1.0
    inv = np.float32(10000.0) ** (-np.arange(0, DR, 2, dtype=np.float32) / np.float32(DR))
    ang = np.arange(T, dtype=np.float32)[:, None] * inv
    trig = [np.cos(ang.astype(np.float64)), np.sin(ang.astype(np.float64))]
    for q in range(4):
        out[SLOT * q:SLOT * q + DH, C_TABQ:C_TABQ + T] = 1.0
        out[SLOT * q:SLOT * q + DH, C_TABK:C_TABK + T] = 1.0
        for p in range(DR // 2):
            for k in range(ROPE):
                row = SLOT * q + DH + ROPE * p + k
                out[row, C_TABQ:C_TABQ + T] = SIGN[k] * trig[Q_SIN[k]][:, p]
                out[row, C_TABK:C_TABK + T] = trig[K_SIN[k]][:, p]
    for q in range(4):
        out[SLOT * q:SLOT * q + SLOT, C_SLOT + q] = 1.0
    out[:, C_STEP:C_STEP + 3] = (1.0, 2.0, 3.0)
    own = np.where(np.arange(KB)[None, :] >= np.arange(P)[:, None] % KB, CLIP, MASKED)
    out[:, C_LIM:C_SLOT] = CLIP
    for at in (0, T, XY, XY + P):
        out[:, C_LIM + at:C_LIM + at + KB] = own
    return out


def build(nc, x_in, weights, vectors, latent, ints, w1_in, w2_in, consts, out):
    with ExitStack() as ctx:
        def sb(name, shape, dt=F32):
            return ctx.enter_context(nc.sbuf_tensor(name, shape, dt))

        def sem(name):
            return ctx.enter_context(nc.semaphore(name))

        ps = ctx.enter_context(nc.psum_tensor("ps", [P, 8, 512], F32))
        gates_dram = nc.dram_tensor("gates_scratch", [BLK * EXPERTS, P], F32, kind="Internal").ap()

        x = sb("x", [P, BLK + TB, C])
        cst = sb("cst", [P, C_COLS])
        wts = sb("wts", [P, W_COLS])
        vec = sb("vec", [P, V_COLS])
        ident = cst[:, C_ID:C_ID + P]
        ones = cst[:, C_ONES:C_ONES + P]
        w1h = sb("w1h", [P, CHUNKS * P], R32)
        w1l = sb("w1l", [P, CHUNKS * P], R32)
        w2h = sb("w2h", [P, CHUNKS * P], R32)
        w2l = sb("w2l", [P, CHUNKS * P], R32)
        stats = sb("stats", [P, 2, TB, 6])
        moments = sb("moments", [P, 2, TB, 2])
        vareps = sb("vareps", [P, 2, TB])
        minus_half = sb("minus_half", [P, TB])
        rstd = sb("rstd", [P, 2, TB])
        xn = sb("xn", [P, 2, TB, C])
        wqkv_hi = sb("wqkv_hi", [P, 2 * GROUPS * P + P], R32)
        wqkv_lo = sb("wqkv_lo", [P, 2 * GROUPS * P + P], R32)
        stats4 = sb("stats4", [P, TB, 6])
        stage4 = sb("stage4", [P, TB * 2])
        moments4 = sb("moments4", [P, BLK * 2])
        vareps4 = sb("vareps4", [P, BLK])
        rstd4 = sb("rstd4", [P, BLK])
        gate_hi = sb("gate_hi", [P, EXPERTS], R32)
        gate_lo = sb("gate_lo", [P, EXPERTS], R32)
        arena_at = nc.sbuf_base
        sb("arena", [P, ARENA])
        used = [0]

        def cut(name, cols, shape=None, dt=F32):
            a = nc.alloc_sbuf_tensor_at(name, [P, cols], dt, offset=arena_at + 4 * used[0])[:, :]
            used[0] += -(-cols // 8) * 8
            assert used[0] <= ARENA, used[0]
            return a if shape is None else a.rearrange(shape[0], **shape[1])

        xT = cut("xT", 2 * SEQS * (T + 1), ("p (a b t) -> p a b t", dict(a=2, b=SEQS)))
        other = cut("other", 3)
        wmix = cut("wmix", 3 * 2 * P, ("p (m a n) -> p m a n", dict(m=3, a=2)))
        decay = cut("decay", T)
        hdecay = cut("hdecay", T)
        ew = cut("ew", 4)
        ek = cut("ek", 2 * TILE, ("p (a t) -> p a t", dict(a=2)))
        eu = cut("eu", 2 * TILE, ("p (a t) -> p a t", dict(a=2)))
        th = cut("th", 2 * TILE, ("p (a t) -> p a t", dict(a=2)))
        kv = cut("kv", TILE)
        nu = cut("nu", TILE)
        sa = cut("sa", SEQS * (T + 1), ("p (b t) -> p b t", dict(b=SEQS)))
        sden = cut("sden", T + 1)
        num = cut("num", TILE)
        den = cut("den", T)
        rec = cut("rec", T)
        wkv = cut("wkv", TILE)
        gated = cut("gated", 2 * TILE, ("p (a t) -> p a t", dict(a=2)))
        lat = cut("lat", L_COLS)[0:32, :]
        raw = cut("raw", CHUNKS * P)
        wgu = cut("wgu", 2 * HIDDEN, None, R32)
        wdn = cut("wdn", HIDDEN)
        fxh = cut("fxh", 2 * TILE, ("p (a t) -> p a t", dict(a=2)), R32)
        fxl = cut("fxl", 2 * TILE, ("p (a t) -> p a t", dict(a=2)), R32)
        ft = cut("ft", FJ * TILE, ("p (j t) -> p j t", dict(j=FJ)))
        hidden_buffer = cut("fh", 2 * FJ * TILE)
        fh = hidden_buffer.rearrange("p (a j t) -> p a j t", a=2, j=FJ)
        int_raw = hidden_buffer[:, 0:3 * HIDDEN].bitcast(I32)
        used[0] = 0
        axh = cut("axh", 2 * TILE, ("p (a t) -> p a t", dict(a=2)), R32)
        axl = cut("axl", 2 * TILE, ("p (a t) -> p a t", dict(a=2)), R32)
        vx = cut("vx", 2 * 8 * 8 * SLOT, ("p (a j q i s) -> p a j q i s", dict(a=2, j=8, q=8, i=2)))
        qs = cut("qs", 2 * GROUPS * TILE, ("p (a g t) -> p a g t", dict(a=2, g=GROUPS)))
        ks = cut("ks", 2 * GROUPS * TILE, ("p (a g t) -> p a g t", dict(a=2, g=GROUPS)))
        kbd = cut("kbd", 2 * 2 * 4 * P, ("p (a q j i k) -> p a q j i k", dict(a=2, q=2, j=4, i=2)))
        clxy = cut("clxy", 2 * XY, ("p (q t) -> p q t", dict(q=2)))
        clz = cut("clz", 2 * ZC, ("p (q t) -> p q t", dict(q=2)))
        prxy = cut("prxy", 4 * 2 * XY, ("p (a q t) -> p a q t", dict(a=4, q=2)))
        prz = cut("prz", 4 * 2 * ZC, ("p (a q t) -> p a q t", dict(a=4, q=2)))
        ot = cut("ot", 2 * SEQS * 2 * T, ("p (a b w t) -> p a b w t", dict(a=2, b=SEQS, w=2)))
        otok = cut("otok", P, ("p (h d) -> p h d", dict(h=HEADS)))
        oden = cut("oden", HEADS)
        oT = cut("oT", P)
        used[0] = 0
        xh = cut("xh", N, None, R32)
        xl = cut("xl", N, None, R32)
        lgT = cut("lgT", 2 * TILE, ("p (a t) -> p a t", dict(a=2)))
        h32 = cut("h32", 2 * MT, ("p (a t) -> p a t", dict(a=2)))
        hh = cut("hh", 4 * MT, ("p (a t) -> p a t", dict(a=4)), R32)
        hl = cut("hl", 4 * MT, ("p (a t) -> p a t", dict(a=4)), R32)
        gbc = cut("gbc", 2 * MT, ("p (a t) -> p a t", dict(a=2)))
        gy = cut("gy", MT)
        acc = cut("acc", MT)
        yout = cut("yout", MT, ("p (n c) -> p n c", dict(n=MT // P)))
        lg = cut("lg", PAIRS // P)
        gT = cut("gT", PAIRS // P)
        small = cut("small", 24)

        consts_in, weights_in, x_first_in, x_rest_in = sem("consts_in"), sem("weights_in"), sem("x_first_in"), sem("x_rest_in")
        ints_in, raw_in = sem("ints_in"), sem("expert_weights_piece_in")
        setup = sem("vector_setup_steps")
        pool_setup = sem("pool_setup_steps")
        act_setup = sem("act_setup_steps")
        v_setup = sem("p3_v_zeros_and_ones")
        w_split = sem("expert_weights_split_steps")
        m_half = sem("p4_out_half")
        a_kb = sem("p3_key_blocks_ready")
        axl_ready, wsteps = sem("p3_lo_ready"), sem("p3_weights_split_steps")
        pool_passed = sem("pool_passed")
        passed = sem("vector_passed")
        w_gw = sem("gate_weights_split_steps")

        class Norm:

            def __init__(self, name):
                self.chain = sem(name + "_stats_steps")
                self.rstd = sem(name + "_rstd_ready")
                self.ready = sem(name + "_xn_ready")
                self.turned = sem(name + "_xn_turned")

        norms = [Norm(f"norm{i}") for i in range(1, 4)]
        CH = 2 * TB + 1

        def tile_steps(eng, body, extra, last=NT):
            for s in range(extra):
                body(s, s % 2)
            with eng.Fori(0, (last - extra) // 2) as i:
                body(2 * i + extra, extra % 2)
                body(2 * i + extra + 1, (extra + 1) % 2)
            for s in range(last, NT + extra):
                body(s, s % 2)

        def piece_bank(t, piece):
            return 1 + piece % 3 if isinstance(t, int) and t == 0 and piece < 7 else 1

        def at_tile(t, size):
            return bass.ds(t * size, size) if not isinstance(t, int) else slice(t * size, (t + 1) * size)

        def live(t):
            return not isinstance(t, int) or 0 <= t < NT

        def blocks(t):
            return x[:, bass.ds(t * TB, TB), :] if not isinstance(t, int) else x[:, t * TB:(t + 1) * TB, :]

        def norm_stats(dve, norm, t, par, resid):
            if isinstance(t, int) and t > NT:
                return
            for wait, value in resid:
                dve.wait_ge(wait, value)
            xt = blocks(t)
            for j in range(TB):
                dve.bn_stats(stats[:, par, j, :], xt[:, j, :]).then_inc(norm.chain, 1)
            dve.wait_ge(norm.chain, t * CH + TB)
            dve.sem_inc(passed, 1)
            for j in range(TB):
                dve.bn_aggr(moments[:, par, j, :], stats[:, par, j, :]).then_inc(norm.chain, 1)
            dve.wait_ge(norm.chain, t * CH + 2 * TB)
            dve.tensor_scalar(vareps[:, par, :], moments[:, par, :, 1], EPS, None, ALU.add).then_inc(norm.chain, 1)

        def norm_rstd(pool, norm, t, par):
            if isinstance(t, int) and t > NT:
                return
            pool.wait_ge(norm.chain, (t + 1) * CH)
            pool.tensor_tensor(rstd[:, par, :], vareps[:, par, :], minus_half[:, :], ALU.pow).then_inc(norm.rstd, 1)

        def norm_apply(dve, norm, t, par):
            if isinstance(t, int) and t > NT:
                return
            dve.wait_ge(norm.rstd, t + 1)
            if not isinstance(t, int) or t >= 2:
                dve.wait_ge(norm.turned, t - 1)
            xt = blocks(t)
            for j in range(TB):
                dve.tensor_scalar(xn[:, par, j, :], xt[:, j, :], moments[:, par, j, 0:1], rstd[:, par, j:j + 1],
                                  ALU.subtract, ALU.mult).then_inc(norm.ready, 1)

        def norm_turn(pe, norm, t, par, bank):
            pe.wait_ge(norm.ready, t * TB + TB)
            for j in range(TB):
                mm = pe.transpose(ps[:, bank, j * P:(j + 1) * P], xn[:, par, j, :], ident)
            mm.then_inc(norm.turned, 1)

        xT_ready, mix_steps = sem("p1_xT_ready"), sem("p1_weights_mixed")
        proj_done, act1, sums_done = sem("p1_projected"), sem("p1_activated"), sem("p1_head_sums_done")
        c_kv, c_sa, c_den, c_num = sem("p1_times_v"), sem("p1_decayed_sums"), sem("p1_denominator_steps"), sem("p1_numerators")
        c_spread, c_wkv, c_gated = sem("p1_reciprocals_spread"), sem("p1_quotients"), sem("p1_gated")
        o_done, resid1 = sem("p1_out_projected"), sem("p1_residual_added")
        f_hi, f_lo, fg_done, f_silu = sem("p2_hi_ready"), sem("p2_lo_ready"), sem("p2_gate_up_done"), sem("p2_silu_ready")
        f_h, f_down, resid2 = sem("p2_hidden_ready"), sem("p2_down_done"), sem("p2_residual_added")
        comb = sem("p3_weights_combined")
        comb_copied = sem("p3_weights_copied")
        a_x, a_proj, a_qk, a_vdone, a_vready = sem("p3_xT_ready"), sem("p3_qk_projected"), sem("p3_qk_ready"), sem("p3_v_projected"), sem("p3_v_ready")
        a_s, a_cl, a_p, a_av, a_ot = sem("p3_scores_done"), sem("p3_clipped"), sem("p3_probs_ready"), sem("p3_av_done"), sem("p3_av_copied")
        a_f1, a_fd, a_ftok, a_f2, a_oT, a_wo, resid3 = (sem("p3_out_turned"), sem("p3_denominators"), sem("p3_out_normalised"),
                                                        sem("p3_out_turned_back"), sem("p3_outT_ready"), sem("p3_out_projected"), sem("p3_residual_added"))
        x4_stats, x4_moments, x4_staged, x4_var = sem("norm4_block_stats"), sem("norm4_moments"), sem("norm4_moments_kept"), sem("norm4_variances_kept")
        x4_rstd, x4_ready, x4_turned = sem("norm4_rstd_ready"), sem("norm4_xn_ready"), sem("norm4_xn_turned")
        g_hi, g_lo, g_mm = sem("p4_hi_ready"), sem("p4_lo_ready"), sem("p4_logits_done")
        g_copied, g_placed = sem("p4_logits_copied"), sem("p4_logits_placed")
        g_masked, g_turned = sem("gates_masked"), sem("gates_turned")
        g_loaded, s_steps, s_counted, gates_ready, gates_stored = (sem("search_logits_copied"), sem("search_vector_steps"), sem("search_counted"),
                                                                   sem("gates_ready"), sem("gates_stored"))
        s_parts = sem("search_partition_counts")
        gb_in = [sem("gates_rows_in0"), sem("gates_rows_in1")]
        m_w1, m_gelu, m_hi, m_lo, m_w2 = sem("p4_w1_done"), sem("p4_gelu_ready"), sem("p4_hidden_hi_ready"), sem("p4_hidden_lo_ready"), sem("p4_w2_done")
        m_gy, m_acc, m_turn, m_out, stored = sem("p4_gated"), sem("p4_summed"), sem("p4_turned"), sem("p4_out_ready"), sem("p4_out_stored")

        xv = x_in.rearrange("(n p) c -> p n c", p=P)
        outv = out.rearrange("(n p) c -> p n c", p=P)

        block = ctx.enter_context(nc.Block())

        @block.sync
        def _(sp):
            sp.dma_start(x[:, 0:TB, :], xv[:, 0:TB, :]).then_inc(x_first_in, 16)
            sp.dma_start(vec[:, :], vectors).then_inc(weights_in, 16)
            sp.dma_start(wts[:, :], weights).then_inc(weights_in, 16)
            sp.dma_start(lat, latent).then_inc(weights_in, 16)
            sp.dma_start(cst[:, :], consts).then_inc(consts_in, 16)
            sp.dma_start(x[:, TB:BLK, :], xv[:, TB:BLK, :]).then_inc(x_rest_in, 16)
            sp.dma_start(int_raw, ints).then_inc(ints_in, 16)
            sp.dma_start(raw, w1_in).then_inc(raw_in, 16)
            sp.wait_ge(w_split, 2 * NT)
            sp.dma_start(raw, w2_in).then_inc(raw_in, 16)

            sp.wait_ge(gates_ready, 1)
            sp.dma_start(gates_dram.rearrange("(h r) t -> r h t", r=P), gT.rearrange("p (h t) -> p h t", t=P)).then_inc(gates_stored, 16)
            sp.wait_ge(gates_stored, 16)
            rows = gates_dram.rearrange("(b e) t -> e b t", e=EXPERTS)

            def expert_gates(tt, e):
                if not (isinstance(tt, int) and tt == 0 and e < 2):
                    sp.wait_ge(m_gy, tt * EXPERTS + e - 1)
                at = at_tile(tt, MT // P)
                sp.dma_start(gbc[:, e % 2, :].rearrange("p (b t) -> p b t", t=P),
                             rows[e:e + 1, at, :].partition_broadcast(P)).then_inc(gb_in[e % 2], 16)

            def store_out(tt):
                sp.wait_ge(m_out, tt + 1)
                at = bass.ds(tt * (MT // P), MT // P) if not isinstance(tt, int) else slice(tt * (MT // P), (tt + 1) * (MT // P))
                sp.dma_start(outv[:, at, :], yout).then_inc(stored, 16)

            for e in range(EXPERTS):
                expert_gates(0, e)
            with sp.Fori(1, NMT) as tt:
                for e in range(EXPERTS):
                    expert_gates(tt, e)
                    if e == 3:
                        store_out(tt - 1)
            store_out(NMT - 1)
            sp.wait_ge(stored, 16 * NMT)

        @block.gpsimd
        def _(pool):
            pool.memset(minus_half[:, :], -0.5).then_inc(pool_setup, 1)
            for a in range(2):
                pool.memset(xT[:, a, :, 0:1], 0.0).then_inc(pool_setup, 1)
            pool.memset(x[:, BLK:BLK + TB, :], 0.0).then_inc(pool_setup, 1)
            pool.wait_ge(pool_setup, 4)
            norm_rstd(pool, norms[0], 0, 0)

            def split(s, hi, lo, base):
                if not live(s):
                    return
                at = bass.ds(s * SPLIT, SPLIT) if not isinstance(s, int) else slice(s * SPLIT, (s + 1) * SPLIT)
                pool.tensor_copy(hi[:, at], raw[:, at]).then_inc(w_split, 1)
                pool.wait_ge(w_split, base + 2 * s + 1)
                pool.sem_inc(pool_passed, 1)
                pool.tensor_tensor(lo[:, at], raw[:, at], hi[:, at].bitcast(F32), ALU.subtract).then_inc(w_split, 1)

            pool.wait_ge(raw_in, 16)

            def phase1(s, par):
                t = s - 1
                if live(t):
                    pool.wait_ge(c_sa, t * 2 + 2)
                    if not isinstance(t, int) or t >= 1:
                        pool.wait_ge(c_wkv, t)
                    pool.tensor_tensor(num.rearrange("p (b t) -> p b t", b=SEQS), nu.rearrange("p (b t) -> p b t", b=SEQS),
                                       sa[:, :, 0:T], ALU.add).then_inc(c_num, 1)
                if isinstance(s, int) and s in (NT - 1, NT):
                    norm_rstd(pool, norms[1], s - NT + 1, 1 - par)
                elif not isinstance(s, int) or s < NT:
                    norm_rstd(pool, norms[0], s + 1, 1 - par)
                split(s, w1h, w1l, 0)

            tile_steps(pool, phase1, 2, NT - 2)
            pool.wait_ge(raw_in, 32)

            def phase2(s, par):
                if not isinstance(s, int) or s >= 1:
                    norm_rstd(pool, norms[1], s + 1, 1 - par)
                if isinstance(s, int) and s == NT:
                    norm_rstd(pool, norms[2], 0, 0)
                split(s, w2h, w2l, 2 * NT)
                if isinstance(s, int) and s == NT:
                    pool.wait_ge(o_done, NT)
                    pool.wait_ge(w_split, 4 * NT)
                    for a in range(2):
                        pool.memset(vx[:, a, :, :, :, :].rearrange("p j q i s -> p (j q i s)"), 0.0).then_inc(v_setup, 1)
                    pool.wait_ge(v_setup, 2)
                    for a in range(2):
                        for i in range(2):
                            pool.memset(vx[i * 64:i * 64 + 64, a, :, :, i, DH:DH + 1], 1.0).then_inc(v_setup, 1)
                            pool.wait_ge(v_setup, 3 + 2 * a + i)

            tile_steps(pool, phase2, 2)

            def last_rstd(t):
                pool.wait_ge(x4_var, t + 1)
                at = at_tile(t, TB)
                pool.tensor_tensor(rstd4[:, at], vareps4[:, at], minus_half[:, :], ALU.pow).then_inc(x4_rstd, 1)

            def phase3(s, par):
                t = s - 1
                if live(t):
                    for u in range(8):
                        k = t * 8 + u
                        b, g = u // 4, u % 4
                        if b == 0:
                            pool.wait_ge(a_qk, t * 8 + 2 * g + 1)
                        if not (isinstance(t, int) and t == 0 and u < 2):
                            pool.wait_ge(a_s, 3 * k - 3)
                        pool.sem_inc(pool_passed, 1)
                        for h in range(4):
                            pool.tensor_scalar(kbd[:, u % 2, h // 2, :, h % 2, :],
                                               ks[:, 1 - par, g, b * T:(b + 1) * T].rearrange("p (j k) -> p j k", j=4),
                                               cst[:, C_SLOT + h:C_SLOT + h + 1], 0.0, ALU.mult, ALU.add).then_inc(a_kb, 1)
                        if isinstance(s, int) and s == NT and u < NT - 2:
                            last_rstd(u)
                norm_rstd(pool, norms[2], s + 1, 1 - par)

            tile_steps(pool, phase3, 2)
            last_rstd(NT - 2)
            last_rstd(NT - 1)
            for c in range(AHEAD):
                pool.wait_ge(m_hi, c + 1)
                if c >= 4:
                    pool.wait_ge(m_w2, c - 3)
                pool.tensor_tensor(hl[:, c % 4, :], h32[:, c % 2, :], hh[:, c % 4, :].bitcast(F32), ALU.subtract).then_inc(m_lo, 1)

        @block.scalar
        def _(act):
            act.wait_ge(weights_in, 48)
            act.activation(ew[:, 0:2], vec[:, V_DECAY:V_DECAY + 2], ACT.Exp).then_inc(act_setup, 1)
            act.wait_ge(act_setup, 1)
            act.activation(ew[:, 2:4], ew[:, 0:2], ACT.Exp, scale=-1.0).then_inc(act_setup, 1)
            act.wait_ge(pool_setup, 4)

            def copy_xT(t, par):
                act.wait_ge(norms[0].turned, t + 1)
                if not isinstance(t, int) or t >= 2:
                    act.wait_ge(proj_done, (t - 1) * 3)
                act.activation(xT[:, par, :, 1:T + 1], ps[:, 0, :].rearrange("p (b t) -> p b t", b=SEQS),
                               ACT.Copy).then_inc(xT_ready, 1)

            def phase1(s, par):
                if not live(s):
                    return
                if not isinstance(s, int) or s >= 2:
                    act.wait_ge(c_gated, s - 1)
                act.wait_ge(proj_done, s * 3 + 1)
                act.activation(ek[:, par, :], ps[:, 1, :], ACT.Exp).then_inc(act1, 1)
                act.activation(eu[:, par, :], ps[:, 1, :], ACT.Exp, bias=vec[:, V_FIRST:V_FIRST + 1]).then_inc(act1, 1)
                act.wait_ge(proj_done, s * 3 + 3)
                act.activation(th[:, par, :], ps[:, 3, :], ACT.Tanh, scale=0.5).then_inc(act1, 1)
                if isinstance(s, int) and s == NT - 1:
                    gated_high_part(0, 0)
                else:
                    copy_xT(s + 1, 1 - par)

            def gated_high_part(t, par):
                act.wait_ge(norms[1].turned, t + 1)
                if not isinstance(t, int) or t >= 2:
                    act.wait_ge(fg_done, (t - 1) * FJ)
                act.activation(fxh[:, par, :], ps[:, 0, :], ACT.Copy).then_inc(f_hi, 1)

            copy_xT(0, 0)
            tile_steps(act, phase1, 2, NT - 2)

            def phase2(s, par):
                t = s - 1
                if live(t):
                    for j in range(FJ):
                        act.wait_ge(fg_done, t * FJ + j + 1)
                        if not isinstance(t, int) or t >= 1:
                            act.wait_ge(f_h, (t - 1) * FJ + j + 1)
                        act.activation(ft[:, j, :], ps[:, 1 + 2 * j, :], ACT.Silu, scale=1.0 / 127.0).then_inc(f_silu, 1)
                if not isinstance(s, int) or 1 <= s < NT:
                    gated_high_part(s, par)

            tile_steps(act, phase2, 2)

            def high_part(t, par):
                act.wait_ge(x4_turned, t + 1)
                act.activation(xh[:, at_tile(t, TILE)], ps[:, par, :], ACT.Copy).then_inc(g_hi, 1)

            def exp_pair(k, u, pair):
                act.wait_ge(a_cl, 3 * k + pair + 1)
                act.activation(prxy[:, u % 4, pair, :], clxy[:, pair, :], ACT.Exp, scale=12.0 ** -0.5).then_inc(a_p, 1)

            def copy_logits(t, par):
                act.wait_ge(g_mm, t + 1)
                if not isinstance(t, int) or t >= 2:
                    act.wait_ge(g_placed, t - 1)
                act.activation(lgT[0:EXPERTS, par, :], ps[0:EXPERTS, 2 + par, :], ACT.Copy).then_inc(g_copied, 1)

            def phase3(s, par):
                for u in range(8):
                    k = (s - 1) * 8 + u
                    if live(s) and u == 2:
                        copy_v(s, par)
                    if live(s - 1):
                        if not (isinstance(s, int) and s == 1 and u < 4):
                            act.wait_ge(a_av, (s - 1) * 4 + u // 2 - 1)
                        exp_pair(k, u, 0)
                    if live(s - 2) and u % 2:
                        copy_oT(s - 2, u // 2)
                    if live(s - 1):
                        exp_pair(k, u, 1)
                    if isinstance(s, int) and s == NT + 1 and u % 2:
                        high_part(u // 2, u // 2 % 2)
                        if u > 1:
                            copy_logits(u // 2 - 1, (u // 2 - 1) % 2)
                    if live(s - 1):
                        act.wait_ge(a_cl, 3 * k + 3)
                        act.activation(prz[:, u % 4, :, :], clz, ACT.Exp, scale=12.0 ** -0.5).then_inc(a_p, 1)
                    if u == 0 and live(s - 2):
                        copy_av(s - 2, par, 3)
                    if u == 0 and live(s):
                        act.wait_ge(norms[2].turned, s + 1)
                        if not isinstance(s, int) or s >= 2:
                            act.wait_ge(a_vdone, s - 1)
                            act.wait_ge(a_proj, (s - 1) * 8)
                        act.activation(axh[:, par, :], ps[:, 0, :], ACT.Copy).then_inc(a_x, 1)
                    if live(s - 1) and u in (2, 4, 6):
                        copy_av(s - 1, 1 - par, u // 2 - 1)

            def copy_v(t, par):
                act.wait_ge(a_vdone, t + 1)
                if isinstance(t, int) and t == 0:
                    act.wait_ge(v_setup, 6)
                if not isinstance(t, int) or t >= 2:
                    act.wait_ge(a_av, (t - 1) * 4)
                for i in range(2):
                    for odd in range(2):
                        src = ps[odd * 64:odd * 64 + 64, 0, :].rearrange("p (n q i d) -> p n q i d", n=TB, q=8, i=2)
                        dst = vx[i * 64:i * 64 + 64, par, :, :, i, 0:DH].rearrange("p (n o) q d -> p n o q d", o=2)
                        act.activation(dst[:, :, odd, :, :], src[:, :, :, i, :], ACT.Copy).then_inc(a_vready, 1)

            def copy_av(t, par, w):
                act.wait_ge(a_av, t * 4 + w + 1)
                if w == 0 and not (isinstance(t, int) and t < 2):
                    act.wait_ge(a_f1, (t - 1) * 4)
                act.activation(ot[:, par, w // 2, w % 2, :], ps[:, 5 + w % 2, 0:T], ACT.Copy).then_inc(a_ot, 1)

            def copy_oT(t, q):
                act.wait_ge(a_f2, t * 4 + q + 1)
                if not (isinstance(t, int) and t == 0 and q == 0):
                    act.wait_ge(a_wo, t * 4 + q)
                act.activation(oT, ps[:, 7, 256:384], ACT.Copy).then_inc(a_oT, 1)

            tile_steps(act, phase3, 2)

            with act.Fori(EARLY // 2, NT // 2) as i:
                for par in range(2):
                    high_part(2 * i + par, par)
                    copy_logits(2 * i + par - 1, 1 - par)
            copy_logits(NT - 1, 1)
            act.wait_ge(resid3, NT * TB)

            def experts(tt):
                for c in range(CHUNKS):
                    k = tt * CHUNKS + c
                    par = c % 2
                    act.wait_ge(m_w1, k + 1)
                    if not (isinstance(tt, int) and tt == 0 and c < 2):
                        act.wait_ge(m_lo, k - 1)
                    act.activation(h32[:, par, :], ps[:, 2 * par:2 * par + 2, :].rearrange("p a t -> p (a t)"),
                                   ACT.Gelu_apprx_tanh, bias=vec[:, V_B1 + c:V_B1 + c + 1]).then_inc(m_gelu, 1)
                    act.wait_ge(m_gelu, k + 1)
                    if not (isinstance(tt, int) and tt == 0 and c < 4):
                        act.wait_ge(m_w2, k - 3)
                    act.activation(hh[:, c % 4, :], h32[:, par, :], ACT.Copy).then_inc(m_hi, 1)

            experts(0)
            with act.Fori(1, NMT) as tt:
                experts(tt)

        @block.vector
        def _(dve):
            dve.memset(sa[:, :, 0:1], 0.0).then_inc(setup, 1)
            dve.memset(sden[:, 0:1], 0.0).then_inc(setup, 1)
            dve.wait_ge(x_first_in, 16)
            dve.wait_ge(pool_setup, 4)
            norm_stats(dve, norms[0], 0, 0, [])
            dve.wait_ge(act_setup, 2)
            dve.wait_ge(consts_in, 16)
            one = cst[:, C_ONES:C_ONES + 1].broadcast_to([P, T])
            dve.tensor_scalar(decay, one, ew[:, 2:3], None, ALU.mult).then_inc(setup, 1)
            dve.tensor_scalar(hdecay, one, ew[:, 3:4], None, ALU.mult).then_inc(mix_steps, 1)
            dve.wait_ge(weights_in, 48)
            dve.tensor_scalar(other, vec[:, V_MK:V_MK + 3], -1.0, 1.0, ALU.mult, ALU.add).then_inc(mix_steps, 1)
            dve.wait_ge(mix_steps, 2)
            for m, w in enumerate((W_K, W_V, W_R)):
                dve.tensor_scalar(wmix[:, m, 0, :], wts[:, w:w + P], vec[:, m:m + 1], None, ALU.mult).then_inc(mix_steps, 1)
                dve.tensor_scalar(wmix[:, m, 1, :], wts[:, w:w + P], other[:, m:m + 1], None, ALU.mult).then_inc(mix_steps, 1)
            dve.wait_ge(x_rest_in, 16)

            def residual(t, done, scale, added, bank):
                dve.wait_ge(done, t + 1)
                xt = blocks(t)
                dve.scalar_tensor_tensor(xt, ps[:, bank, :].rearrange("p (n c) -> p n c", n=TB), scale, xt,
                                         ALU.mult, ALU.add).then_inc(added, 1)

            def decayed_sums(t, par):
                dve.wait_ge(proj_done, t * 3 + 2)
                dve.wait_ge(act1, t * 3 + 2)
                if not isinstance(t, int) or t >= 1:
                    dve.wait_ge(c_num, t)
                dve.tensor_tensor(kv, ps[:, 2, :], ek[:, par, :], ALU.mult).then_inc(c_kv, 1)
                dve.tensor_tensor(nu, ps[:, 2, :], eu[:, par, :], ALU.mult).then_inc(c_kv, 1)
                dve.wait_ge(sums_done, t * 2 + 2)
                dve.tensor_tensor_scan(sden[:, 1:T + 1], hdecay, ps[:, 4, 0:T], 0.0, ALU.mult, ALU.add).then_inc(c_den, 1)
                dve.wait_ge(c_den, t * 3 + 1)
                if not isinstance(t, int) or t >= 1:
                    dve.wait_ge(c_spread, t)
                dve.scalar_tensor_tensor(den, ps[:, 4, T:2 * T], 1e-6, sden[:, 0:T], ALU.max, ALU.add).then_inc(c_den, 1)
                dve.wait_ge(c_kv, t * 2 + 1)
                for b in range(SEQS):
                    dve.tensor_tensor_scan(sa[:, b, 1:T + 1], decay, kv[:, b * T:(b + 1) * T], 0.0,
                                           ALU.mult, ALU.add).then_inc(c_sa, 1)
                dve.wait_ge(c_den, t * 3 + 2)
                dve.reciprocal(rec, den).then_inc(c_den, 1)

            def gate_sums(t, par):
                dve.wait_ge(c_num, t + 1)
                dve.wait_ge(c_spread, t + 1)
                dve.tensor_tensor(wkv, ps[:, 5, :], num, ALU.mult).then_inc(c_wkv, 1)
                dve.wait_ge(c_wkv, t + 1)
                dve.wait_ge(act1, t * 3 + 3)
                if not isinstance(t, int) or t >= 2:
                    dve.wait_ge(o_done, t - 1)
                dve.scalar_tensor_tensor(gated[:, par, :], th[:, par, :], 1.0, wkv, ALU.add, ALU.mult).then_inc(c_gated, 1)

            def gated_low_part(t, par):
                dve.wait_ge(f_hi, t + 1)
                if not isinstance(t, int) or t >= 2:
                    dve.wait_ge(fg_done, (t - 1) * FJ)
                dve.tensor_tensor(fxl[:, par, :], ps[:, 0, :], fxh[:, par, :].bitcast(F32), ALU.subtract).then_inc(f_lo, 1)

            def phase1(s, par):
                handover = isinstance(s, int) and s in (NT - 1, NT)
                if isinstance(s, int) and s == NT:
                    gated_low_part(0, 0)
                if live(s - 1):
                    decayed_sums(s - 1, 1 - par)
                if live(s - 2):
                    residual(s - 2, o_done, 0.5, resid1, 6)
                if handover:
                    norm_stats(dve, norms[1], s - NT + 1, 1 - par, [(resid1, s - NT + 2), (norms[0].rstd, NT)])
                elif not isinstance(s, int) or s < NT:
                    norm_stats(dve, norms[0], s + 1, 1 - par, [])
                if live(s - 1):
                    gate_sums(s - 1, 1 - par)
                if handover:
                    dve.wait_ge(norms[0].turned, s)
                    norm_apply(dve, norms[1], s - NT + 1, 1 - par)
                elif not isinstance(s, int) or s < NT:
                    norm_apply(dve, norms[0], s + 1, 1 - par)
                if isinstance(s, int) and s == 0:
                    later_weights()

            def later_weights():
                dve.wait_ge(ints_in, 16)
                dve.tensor_copy(wgu, int_raw[:, 0:2 * HIDDEN]).then_inc(setup, 1)
                dve.tensor_copy(wdn, int_raw[:, 2 * HIDDEN:3 * HIDDEN]).then_inc(setup, 1)
                dve.wait_ge(weights_in, 48)
                dve.tensor_copy(gate_hi[:, :], vec[:, V_GATE:V_GATE + EXPERTS]).then_inc(w_gw, 1)
                dve.wait_ge(w_gw, 1)
                dve.tensor_tensor(gate_lo[:, :], vec[:, V_GATE:V_GATE + EXPERTS], gate_hi[:, :].bitcast(F32), ALU.subtract).then_inc(w_gw, 1)
                dve.wait_ge(setup, 5)
                dve.wait_ge(comb, 1)
                gp = GROUPS * P
                dve.tensor_copy(wqkv_hi[:, 0:gp], ps[:, 7, :]).then_inc(wsteps, 1)
                dve.wait_ge(comb, 2)
                wk = wts[:, W_KROPE:W_KROPE + gp]
                dve.tensor_tensor(wk, ps[:, 6, :], wk, ALU.add).then_inc(wsteps, 1)
                dve.wait_ge(comb, 3)
                dve.tensor_copy(wqkv_hi[:, 2 * gp:2 * gp + P], ps[:, 5, 0:P]).then_inc(wsteps, 1)
                dve.wait_ge(wsteps, 2)
                dve.tensor_copy(wqkv_hi[:, gp:2 * gp], wk).then_inc(wsteps, 1)
                dve.wait_ge(wsteps, 4)
                dve.tensor_tensor(wqkv_lo[:, 0:gp], ps[:, 7, :], wqkv_hi[:, 0:gp].bitcast(F32), ALU.subtract).then_inc(comb_copied, 1)
                dve.tensor_tensor(wqkv_lo[:, gp:2 * gp], wk, wqkv_hi[:, gp:2 * gp].bitcast(F32), ALU.subtract).then_inc(comb_copied, 1)
                dve.tensor_tensor(wqkv_lo[:, 2 * gp:2 * gp + P], ps[:, 5, 0:P], wqkv_hi[:, 2 * gp:2 * gp + P].bitcast(F32),
                                  ALU.subtract).then_inc(comb_copied, 1)

            norm_apply(dve, norms[0], 0, 0)
            tile_steps(dve, phase1, 2, NT - 2)

            def hidden(t, par):
                if not isinstance(t, int) or t >= 2:
                    dve.wait_ge(f_down, t - 1)
                for j in range(FJ):
                    dve.wait_ge(f_silu, t * FJ + j + 1)
                    dve.tensor_tensor(fh[:, par, j, :], ft[:, j, :], ps[:, 2 + 2 * j, :], ALU.mult).then_inc(f_h, 1)

            def phase2(s, par):
                if not isinstance(s, int) or 2 <= s < NT:
                    norm_apply(dve, norms[1], s, par)
                if live(s - 1):
                    hidden(s - 1, 1 - par)
                if not isinstance(s, int) or 1 <= s < NT:
                    gated_low_part(s, par)
                if not isinstance(s, int) or s >= 1:
                    norm_stats(dve, norms[1], s + 1, 1 - par, [])
                if isinstance(s, int) and s == NT:
                    norm_stats(dve, norms[2], 0, 0, [(resid2, 1), (norms[1].rstd, NT + 1)])
                if live(s - 2):
                    residual(s - 2, f_down, 1.0 / 127.0 ** 2, resid2, 7)
                if isinstance(s, int) and s == NT:
                    norm_apply(dve, norms[2], 0, 0)

            tile_steps(dve, phase2, 2)

            def table(col, a):
                return cst[:, col:col + T].unsqueeze(1).broadcast_to([P, SEQS, T])

            def project_done(t, par, piece):
                dve.wait_ge(a_proj, t * 8 + piece + 1)
                if piece == 0 and (not isinstance(t, int) or t >= 2):
                    dve.wait_ge(a_kb, (t - 1) * 32)
                if piece == 1 and (not isinstance(t, int) or t >= 2):
                    dve.wait_ge(a_s, (t - 1) * 24)
                dst = (ks, qs)[piece % 2][:, par, piece // 2, :]
                dve.tensor_tensor(dst.rearrange("p (b t) -> p b t", b=SEQS), ps[:, piece_bank(t, piece), :].rearrange("p (b t) -> p b t", b=SEQS),
                                  table((C_TABK, C_TABQ)[piece % 2], 0), ALU.mult).then_inc(a_qk, 1)

            def normalise(t, q):
                dve.wait_ge(a_f1, t * 4 + q + 1)
                heads = ps[:, 7, 0:256].rearrange("p (h s) -> p h s", h=HEADS)
                dve.reciprocal(oden, heads[:, :, DH]).then_inc(a_fd, 1)
                dve.wait_ge(a_fd, t * 4 + q + 1)
                dve.tensor_tensor(otok, heads[:, :, 0:DH], oden.unsqueeze(2).broadcast_to([P, HEADS, DH]), ALU.mult).then_inc(a_ftok, 1)

            def add_block(t, q):
                dve.wait_ge(a_wo, t * 4 + q + 1)
                xt = blocks(t)[:, q, :]
                dve.tensor_tensor(xt, ps[:, 7, 384:512], xt, ALU.add).then_inc(resid3, 1)

            limz = cst[:, C_LIM + XY:C_LIM + XY + ZC].unsqueeze(1).broadcast_to([P, 2, ZC])

            def clip(k, part):
                dve.wait_ge(a_s, 3 * k + part + 1)
                if not (isinstance(k, int) and k == 0):
                    dve.wait_ge(a_p, 3 * k - 2 + part)
                if part < 2:
                    dve.scalar_tensor_tensor(clxy[:, part, :], ps[:, 2 + part, 0:XY], -CLIP, cst[:, C_LIM:C_LIM + XY],
                                             ALU.max, ALU.min).then_inc(a_cl, 1)
                else:
                    dve.scalar_tensor_tensor(clz, ps[:, 4, 0:2 * ZC].rearrange("p (q t) -> p q t", q=2), -CLIP, limz,
                                             ALU.max, ALU.min).then_inc(a_cl, 1)

            def block_stats(t, q):
                dve.wait_ge(resid3, t * TB + q + 1)
                if q == 0 and (not isinstance(t, int) or t >= 1):
                    dve.wait_ge(x4_moments, t * TB)
                dve.sem_inc(passed, 1)
                dve.bn_stats(stats4[:, q, :], blocks(t)[:, q, :]).then_inc(x4_stats, 1)

            def keep_moments(t):
                dve.wait_ge(x4_stats, t * TB + TB)
                if not isinstance(t, int) or t >= 1:
                    dve.wait_ge(x4_var, t)
                dve.sem_inc(passed, 1)
                for j in range(TB):
                    dve.bn_aggr(stage4[:, 2 * j:2 * j + 2], stats4[:, j, :]).then_inc(x4_moments, 1)
                dve.wait_ge(x4_moments, t * TB + TB)
                dve.tensor_copy(moments4[:, at_tile(t, 2 * TB)], stage4[:, :]).then_inc(x4_staged, 1)
                dve.tensor_scalar(vareps4[:, at_tile(t, TB)], stage4[:, :].rearrange("p (j m) -> p j m", m=2)[:, :, 1],
                                  EPS, None, ALU.add).then_inc(x4_var, 1)

            def last_norm(t, par):
                dve.wait_ge(x4_rstd, t + 1)
                if not isinstance(t, int) or t >= 2:
                    dve.wait_ge(x4_turned, t - 1)
                xt = blocks(t)
                mt, rt = moments4[:, at_tile(t, 2 * TB)], rstd4[:, at_tile(t, TB)]
                for j in range(TB):
                    dve.tensor_scalar(xn[:, par, j, :], xt[:, j, :], mt[:, 2 * j:2 * j + 1], rt[:, j:j + 1],
                                      ALU.subtract, ALU.mult).then_inc(x4_ready, 1)

            def low_part(t, par):
                dve.wait_ge(g_hi, t + 1)
                at = at_tile(t, TILE)
                dve.tensor_tensor(xl[:, at], ps[:, par, :], xh[:, at].bitcast(F32), ALU.subtract).then_inc(g_lo, 1)

            def phase3(s, par):
                for u in range(8):
                    k = (s - 1) * 8 + u
                    if live(s - 2) and u in (2, 4, 6):
                        block_stats(s - 2, u // 2 - 1)
                    if u == 1 and live(s):
                        dve.wait_ge(a_x, s + 1)
                        if not isinstance(s, int) or s >= 2:
                            dve.wait_ge(a_proj, (s - 1) * 8)
                            dve.wait_ge(a_vdone, s - 1)
                        dve.tensor_tensor(axl[:, par, :], ps[:, 0, :], axh[:, par, :].bitcast(F32), ALU.subtract).then_inc(axl_ready, 1)
                    if live(s - 1):
                        clip(k, 0)
                        clip(k, 1)
                    if u < 2:
                        if live(s - 1) and not (isinstance(s, int) and s == 1 and u == 0):
                            project_done(s - 1, 1 - par, 6 + u)
                    elif live(s):
                        project_done(s, par, u - 2)
                    if u == 0 and live(s) and not (isinstance(s, int) and s == 0):
                        norm_apply(dve, norms[2], s, par)
                    if live(s - 1):
                        clip(k, 2)
                    if live(s - 2):
                        if u % 2 == 0:
                            normalise(s - 2, u // 2)
                        else:
                            add_block(s - 2, u // 2)
                    if isinstance(s, int) and s == NT + 1 and u % 2 == 0:
                        last_norm(u // 2, u // 2 % 2)
                        if u:
                            low_part(u // 2 - 1, (u // 2 - 1) % 2)
                    if u == (1 if isinstance(s, int) and s == 0 else 5):
                        norm_stats(dve, norms[2], s + 1, 1 - par, [])
                if isinstance(s, int) and s == 0:
                    project_done(0, 0, 6)
                if live(s - 2):
                    block_stats(s - 2, TB - 1)
                    keep_moments(s - 2)

            tile_steps(dve, phase3, 2)

            with dve.Fori(EARLY // 2, NT // 2) as i:
                for par in range(2):
                    last_norm(2 * i + par, par)
                    low_part(2 * i + par - 1, 1 - par)
            low_part(NT - 1, 1)

            steps = [0]

            def link(ins):
                ins.then_inc(s_steps, 1)
                steps[0] += 1
                dve.wait_ge(s_steps, steps[0])

            part, cand, base, take = (small[:, 3 * i:3 * i + 3] for i in range(4))
            sgn, limit, taken, kth, m_hi_bits, m_lo_bits = (small[:, i:i + 1] for i in range(12, 18))
            z, zl, zs = (gy[:, i * (PAIRS // P):(i + 1) * (PAIRS // P)] for i in range(3))
            half = PAIRS // P // 2
            upper16, lower16, *below = (acc[:, i * half:(i + 1) * half].bitcast(I16) for i in range(5))
            low_zero = float(-(1 << (LOW - 1)))
            rise = cst[:, C_STEP:C_STEP + 3]
            dve.wait_ge(g_placed, NT)
            dve.tensor_copy(lg, ps[:, 4, 0:PAIRS // P]).then_inc(g_loaded, 1)
            dve.wait_ge(g_loaded, 1)
            dve.tensor_scalar(zs, lg, 0.0, None, ALU.is_lt, ALU.add, accum_out=part[:, 0:1]).then_inc(s_parts, 1)
            dve.wait_ge(s_counted, 1)
            link(dve.tensor_scalar(taken, ps[:, 7, 0:1], float(KTH), None, ALU.is_ge))
            link(dve.tensor_scalar(sgn, taken, -2.0, 1.0, ALU.mult, ALU.add))
            link(dve.tensor_scalar(limit, taken, float(PAIRS - KTH - (KTH - 1)), float(KTH - 1), ALU.mult, ALU.add))
            link(dve.tensor_scalar(z, lg, sgn, None, ALU.mult))
            link(dve.tensor_scalar(zs.bitcast(I32), z.bitcast(I32), (1 << LOW) - 1, None, ALU.bitwise_and))
            link(dve.tensor_scalar(zl, zs.bitcast(I32), low_zero, None, ALU.add))
            link(dve.tensor_scalar(zs.bitcast(I32), z.bitcast(I32), LOW, None, ALU.arith_shift_right))
            link(dve.tensor_copy(upper16, zs.bitcast(I32)))
            for stage, values in enumerate((upper16, lower16)):
                if stage:
                    link(dve.tensor_scalar(zs, upper16, cand[:, 0:1], float(1 << LOW), ALU.subtract, ALU.mult))
                    link(dve.tensor_copy(m_hi_bits.bitcast(I32), cand[:, 0:1]))
                    link(dve.tensor_tensor(zl, zl, zs, ALU.add))
                    link(dve.tensor_scalar(lower16, zl, -low_zero - 1.0, low_zero, ALU.min, ALU.max))
                link(dve.tensor_scalar(cand, rise, float(4 ** (ROUNDS - 1)), low_zero if stage else 0.0, ALU.mult, ALU.add))
                for rnd in range(ROUNDS):
                    unit = 4.0 ** (ROUNDS - 1 - rnd)
                    for j in range(3):
                        dve.tensor_scalar(below[j], values, cand[:, j:j + 1], None, ALU.is_lt, ALU.add,
                                          accum_out=part[:, j:j + 1]).then_inc(s_parts, 1)
                    less = unit if rnd == ROUNDS - 1 else 0.75 * unit
                    link(dve.scalar_tensor_tensor(base, rise, -less, cand, ALU.mult, ALU.add))
                    dve.wait_ge(s_counted, 2 + stage * ROUNDS + rnd)
                    link(dve.tensor_scalar(take, ps[:, 7, 0:3], limit, None, ALU.is_le, ALU.add, accum_out=taken))
                    link(dve.scalar_tensor_tensor(cand, taken.broadcast_to([P, 3]), unit, base, ALU.mult, ALU.add))
            link(dve.tensor_scalar(m_lo_bits.bitcast(I32), cand[:, 0:1], -low_zero, None, ALU.add))
            link(dve.tensor_scalar(m_hi_bits.bitcast(I32), m_hi_bits.bitcast(I32), LOW, None, ALU.logical_shift_left))
            link(dve.tensor_tensor(taken.bitcast(I32), m_hi_bits.bitcast(I32), m_lo_bits.bitcast(I32), ALU.bitwise_or))
            link(dve.tensor_scalar(kth, taken, sgn, None, ALU.mult))
            dve.scalar_tensor_tensor(zs, lg, kth, lg, ALU.is_ge, ALU.mult).then_inc(g_masked, 1)
            dve.wait_ge(g_turned, 1)
            dve.tensor_copy(gT, ps[:, 7, 0:PAIRS // P]).then_inc(gates_ready, 1)

            def finish(tt):
                if not isinstance(tt, int) or tt >= 1:
                    dve.wait_ge(stored, tt * 16)
                for half in range(2):
                    dve.wait_ge(m_turn, tt * 2 + half + 1)
                    at = bass.ds(tt * 8 + 4 * half, 4) if not isinstance(tt, int) else slice(tt * 8 + 4 * half, tt * 8 + 4 * half + 4)
                    ins = dve.tensor_tensor(yout[:, 4 * half:4 * half + 4, :], ps[:, 6 + half, :].rearrange("p (n c) -> p n c", n=4),
                                            x[:, at, :], ALU.add)
                    if half:
                        ins.then_inc(m_out, 1)
                    else:
                        ins.then_inc(m_half, 1)
                dve.wait_ge(m_half, tt + 1)
                dve.wait_ge(m_out, tt + 1)

            def experts(tt):
                for c in range(CHUNKS):
                    k = tt * CHUNKS + c
                    par = c % 2
                    if not (isinstance(tt, int) and tt == 0 and c < AHEAD):
                        dve.wait_ge(m_hi, k + 1)
                        dve.wait_ge(m_w2, k - 3)
                        if isinstance(tt, int) and c == AHEAD:
                            dve.wait_ge(m_lo, AHEAD)
                        dve.tensor_tensor(hl[:, c % 4, :], h32[:, par, :], hh[:, c % 4, :].bitcast(F32), ALU.subtract).then_inc(m_lo, 1)
                    if c % EC == 2 and c > EC:
                        gate(tt, c // EC - 1)
                    if not (isinstance(tt, int) and tt == 0):
                        if c == 1:
                            gate(tt - 1, EXPERTS - 1)
                        if c == 4:
                            finish(tt - 1)

            def gate(tt, e):
                n = tt * EXPERTS + e
                dve.wait_ge(m_w2, tt * CHUNKS + (e + 1) * EC)
                dve.wait_ge(gb_in[e % 2], (tt * (EXPERTS // 2) + e // 2 + 1) * 16)
                dst = acc if e == 0 else gy
                y = ps[:, 4 + 2 * (e % 2):6 + 2 * (e % 2), :].rearrange("p a t -> p (a t)")
                if e == 0 and not (isinstance(tt, int) and tt == 0):
                    dve.wait_ge(m_turn, tt * 2)
                if not (isinstance(tt, int) and tt == 0 and e == 0):
                    dve.wait_ge(m_acc, n)
                ins = dve.scalar_tensor_tensor(dst, y, vec[:, V_B2 + e:V_B2 + e + 1], gbc[:, e % 2, :], ALU.add, ALU.mult)
                ins.then_inc(m_gy, 1)
                dve.wait_ge(m_gy, n + 1)
                if e == 0:
                    dve.sem_inc(m_acc, 1)
                else:
                    dve.tensor_tensor(acc, acc, gy, ALU.add).then_inc(m_acc, 1)

            experts(0)
            with dve.Fori(1, NMT) as tt:
                experts(tt)
            gate(NMT - 1, EXPERTS - 1)
            finish(NMT - 1)

        @block.tensor
        def _(pe):
            pe.wait_ge(weights_in, 48)
            pe.wait_ge(consts_in, 16)
            pe.matmul(ps[:, 7, :], lat[:, L_DQ:L_DQ + P], lat[:, L_UQ:L_UQ + 512], start=True, stop=True).then_inc(comb, 1)
            pe.matmul(ps[:, 6, :], lat[:, L_DKV:L_DKV + P], lat[:, L_UK:L_UK + 512], start=True, stop=True).then_inc(comb, 1)
            pe.matmul(ps[:, 5, 0:P], lat[:, L_DKV:L_DKV + P], lat[:, L_UV:L_UV + P], start=True, stop=True).then_inc(comb, 1)
            pe.wait_ge(mix_steps, 8)

            def mixed(s, par, m):
                if m == 1 and (not isinstance(s, int) or s >= 1):
                    pe.wait_ge(c_kv, 2 * s)
                dst = ps[:, 1 + m, :].rearrange("p (b t) -> p b t", b=SEQS)
                pe.matmul(dst, wmix[:, m, 0, :], xT[:, par, :, 1:T + 1], start=True, stop=False)
                pe.matmul(dst, wmix[:, m, 1, :], xT[:, par, :, 0:T], start=False, stop=True).then_inc(proj_done, 1)

            def gate_up(t, par, j):
                for i in range(2):
                    w = wgu[:, (i * FJ + j) * P:(i * FJ + j + 1) * P]
                    pe.matmul(ps[:, 1 + 2 * j + i, :], w, fxh[:, par, :], start=True, stop=False)
                    mm = pe.matmul(ps[:, 1 + 2 * j + i, :], w, fxl[:, par, :], start=False, stop=True)
                mm.then_inc(fg_done, 1)

            def phase1(s, par):
                t = s - 1
                if isinstance(s, int) and s == NT:
                    pe.wait_ge(f_lo, 1)
                    pe.wait_ge(act1, NT * 3)
                    pe.wait_ge(c_kv, NT * 2)
                    gate_up(0, 0, 0)
                    pe.wait_ge(c_den, NT * 3 - 1)
                    gate_up(0, 0, 1)
                if live(s):
                    pe.wait_ge(xT_ready, s + 1)
                    if not isinstance(s, int) or s >= 1:
                        pe.wait_ge(act1, s * 3)
                    mixed(s, par, 0)
                    mixed(s, par, 1)
                if live(t):
                    pe.wait_ge(c_den, t * 3 + 3)
                    if isinstance(t, int) and t == 0:
                        pe.wait_ge(comb_copied, 3)
                    else:
                        pe.wait_ge(c_wkv, t)
                    for b in range(SEQS):
                        mm = pe.matmul(ps[:, 5, b * T:(b + 1) * T], cst[:, C_SPREAD + b * P:C_SPREAD + (b + 1) * P], rec,
                                       start=True, stop=True)
                    mm.then_inc(c_spread, 1)
                if live(s):
                    mixed(s, par, 2)
                    for i, e in enumerate((ek, eu)):
                        pe.wait_ge(act1, s * 3 + 1 + i)
                        if not isinstance(s, int) or s >= 1:
                            pe.wait_ge(c_den, s * 3 - 1)
                        for b in range(SEQS):
                            mm = pe.matmul(ps[:, 4, i * T:(i + 1) * T], cst[:, C_SUM + b * P:C_SUM + (b + 1) * P],
                                           e[:, par, b * T:(b + 1) * T], start=(b == 0), stop=(b == SEQS - 1))
                        mm.then_inc(sums_done, 1)
                    norm_turn(pe, norms[1 if isinstance(s, int) and s == NT - 1 else 0],
                              0 if isinstance(s, int) and s == NT - 1 else s + 1, 1 - par, 0)
                if live(t):
                    pe.wait_ge(c_gated, t + 1)
                    if not isinstance(t, int) or t >= 1:
                        pe.wait_ge(resid1, t)
                    for j in range(TB):
                        mm = pe.matmul(ps[:, 6, j * P:(j + 1) * P], gated[:, 1 - par, j * P:(j + 1) * P],
                                       wts[:, W_O0:W_O0 + P], start=True, stop=True)
                    mm.then_inc(o_done, 1)

            norm_turn(pe, norms[0], 0, 0, 0)
            tile_steps(pe, phase1, 2, NT - 2)

            def phase2(s, par):
                t = s - 1
                if isinstance(t, int) and t == 0:
                    pe.wait_ge(resid1, NT)
                    gate_up(0, 0, FJ - 1)
                elif live(t):
                    pe.wait_ge(f_lo, t + 1)
                    for j in range(FJ):
                        pe.wait_ge(f_h, (t - 1) * FJ + j + 1)
                        gate_up(t, 1 - par, j)
                if not isinstance(s, int) or 1 <= s < NT:
                    norm_turn(pe, norms[1], s, par, 0)
                t = s - 2
                if live(t):
                    pe.wait_ge(f_h, (t + 1) * FJ)
                    if not isinstance(t, int) or t >= 1:
                        pe.wait_ge(resid2, t)
                    for b in range(TB):
                        for j in range(FJ):
                            mm = pe.matmul(ps[:, 7, b * P:(b + 1) * P], fh[:, par, j, b * P:(b + 1) * P],
                                           wdn[:, j * P:(j + 1) * P], start=(j == 0), stop=(j == FJ - 1))
                    mm.then_inc(f_down, 1)
                if isinstance(s, int) and s == NT + 1:
                    norm_turn(pe, norms[2], 0, 0, 0)

            tile_steps(pe, phase2, 2)
            pe.wait_ge(f_h, NT * FJ)

            def project(t, par, piece):
                if not (isinstance(t, int) and t == 0 and piece < 7):
                    pe.wait_ge(a_qk, t * 8 + piece)
                elif piece >= 3:
                    pe.wait_ge(a_qk, piece - 2)
                o = (GROUPS * (1 - piece % 2) + piece // 2) * P
                for i, (w, xs) in enumerate(((wqkv_hi, axh), (wqkv_lo, axh), (wqkv_hi, axl))):
                    if i == 2 and piece == 0:
                        pe.wait_ge(axl_ready, t + 1)
                    mm = pe.matmul(ps[:, piece_bank(t, piece), :], w[:, o:o + P], xs[:, par, :], start=(i == 0), stop=(i == 2))
                mm.then_inc(a_proj, 1)

            def values(t, par):
                pe.wait_ge(a_x, t + 1)
                pe.wait_ge(axl_ready, t + 1)
                o = 2 * GROUPS * P
                for n in range(TB):
                    toks = slice(n * P, (n + 1) * P)
                    for i, (xs, w) in enumerate(((axh, wqkv_hi), (axl, wqkv_hi), (axh, wqkv_lo))):
                        mm = pe.matmul(ps[:, 0, toks], xs[:, par, toks], w[:, o:o + P], start=(i == 0), stop=(i == 2))
                mm.then_inc(a_vdone, 1)

            def scores(t, par, u, part):
                k = t * 8 + u
                b, g = u // 4, u % 4
                if part == 0:
                    if b == 0:
                        pe.wait_ge(a_qk, 7 if isinstance(t, int) and t == 0 and g < 3 else t * 8 + 2 * g + 2)
                    pe.wait_ge(a_kb, 4 * k + 4)
                if not (isinstance(t, int) and t == 0 and u == 0):
                    pe.wait_ge(a_cl, 3 * k - 2 + part)
                for pair in ((0,), (1,), (0, 1))[part]:
                    for j in ((0, 1), (2, 3))[part // 2]:
                        n = T - j * KB
                        at = S_AT[j] if part < 2 else pair * ZC + S_AT[j]
                        mm = pe.matmul(ps[:, 2 + part, at:at + n],
                                       kbd[:, u % 2, pair, j, :, :].rearrange("p i k -> p (i k)"),
                                       qs[:, par, g, b * T + j * KB:(b + 1) * T], start=True, stop=True)
                mm.then_inc(a_s, 1)

            def weigh(t, par, w):
                b = w // 2
                pe.wait_ge(a_p, 3 * (t * 8 + 2 * w) + 6)
                if not (isinstance(t, int) and t == 0 and w < 2):
                    pe.wait_ge(a_ot, t * 4 + w - 1)
                for j in range(4):
                    n = T - j * KB
                    for q in range(4):
                        slot = (2 * w + q // 2) % 4
                        probs = (prxy, prz)[j // 2][:, slot, q % 2, S_AT[j]:S_AT[j] + n]
                        mm = pe.matmul(ps[SLOT * q:SLOT * q + SLOT, 5 + w % 2, T - n:T],
                                       vx[:, par, 4 * b + j, 4 * (w % 2) + q, :, :].rearrange("p i s -> p (i s)"),
                                       probs, start=(j == 0), stop=(j == 3))
                mm.then_inc(a_av, 1)

            def turn_out(t, par, q):
                if not (isinstance(t, int) and t == 0 and q == 0):
                    pe.wait_ge(resid3, t * 4 + q)
                b, half = q // 2, q % 2
                pe.wait_ge(a_ot, t * 4 + 2 * b + 2)
                for w in range(2):
                    mm = pe.transpose(ps[:, 7, w * P:(w + 1) * P], ot[:, par, b, w, half * P:(half + 1) * P], ident)
                mm.then_inc(a_f1, 1)

            def turn_back(t, q):
                pe.wait_ge(a_ftok, t * 4 + q + 1)
                pe.transpose(ps[:, 7, 256:384], otok.rearrange("p h d -> p (h d)"), ident).then_inc(a_f2, 1)

            def out_project(t, q):
                pe.wait_ge(a_oT, t * 4 + q + 1)
                pe.matmul(ps[:, 7, 384:512], oT, wts[:, W_O1:W_O1 + P], start=True, stop=True).then_inc(a_wo, 1)

            def turn_last(t, par):
                pe.wait_ge(x4_ready, t * TB + TB)
                if not isinstance(t, int) or t >= 2:
                    pe.wait_ge(g_lo, t - 1)
                for j in range(TB):
                    mm = pe.transpose(ps[:, par, j * P:(j + 1) * P], xn[:, par, j, :], ident)
                mm.then_inc(x4_turned, 1)

            def logits(t, par):
                pe.wait_ge(g_lo, t + 1)
                if not isinstance(t, int) or t >= 2:
                    pe.wait_ge(g_copied, t - 1)
                at = at_tile(t, TILE)
                dst = ps[0:EXPERTS, 2 + par, :]
                pe.matmul(dst, gate_hi[:, :], xh[:, at], start=True, stop=False)
                pe.matmul(dst, gate_hi[:, :], xl[:, at], start=False, stop=False)
                pe.matmul(dst, gate_lo[:, :], xh[:, at], start=False, stop=True).then_inc(g_mm, 1)

            def place(t, par):
                pe.wait_ge(g_copied, t + 1)
                for j in range(TB):
                    o = t * TB * EXPERTS + j * EXPERTS
                    mm = pe.transpose(ps[:, 4, o:o + EXPERTS], lgT[0:EXPERTS, par, j * P:(j + 1) * P], ident[0:EXPERTS, 0:EXPERTS])
                mm.then_inc(g_placed, 1)

            def phase3(s, par):
                if isinstance(s, int) and s == 1:
                    pe.wait_ge(resid2, NT)
                    pe.wait_ge(v_setup, 6)
                for u in range(8):
                    if live(s - 1):
                        scores(s - 1, 1 - par, u, 0)
                        scores(s - 1, 1 - par, u, 1)
                    if u == 0 and live(s - 2):
                        weigh(s - 2, par, 3)
                    if live(s - 1) and u in (2, 4, 6):
                        if u == 2:
                            pe.wait_ge(a_vready, s * 4)
                        weigh(s - 1, 1 - par, u // 2 - 1)
                    if live(s - 2):
                        if u % 2 == 0:
                            turn_out(s - 2, par, u // 2)
                        else:
                            turn_back(s - 2, u // 2)
                    if live(s - 1):
                        scores(s - 1, 1 - par, u, 2)
                    early = isinstance(s, int) and s == NT + 1 and u % 2
                    if early:
                        turn_last(u // 2, u // 2 % 2)
                    if live(s - 2) and u % 2:
                        out_project(s - 2, u // 2)
                    if early and u > 1:
                        pe.wait_ge(w_gw, 2)
                        logits(u // 2 - 1, (u // 2 - 1) % 2)
                        if u > 3:
                            place(u // 2 - 2, u // 2 % 2)
                    if u == 0:
                        if live(s):
                            if not isinstance(s, int) or s >= 1:
                                pe.wait_ge(a_vready, s * 4)
                                norm_turn(pe, norms[2], s, par, 0)
                        if live(s - 1):
                            project(s - 1, 1 - par, 7)
                    elif live(s):
                        if u == 1:
                            values(s, par)
                        project(s, par, u - 1)

            tile_steps(pe, phase3, 2)
            for t in range(EARLY, NT):
                turn_last(t, t % 2)
                logits(t - 1, 1 - t % 2)
                place(t - 2, t % 2)
            logits(NT - 1, 1)
            place(NT - 2, 0)
            place(NT - 1, 1)
            pe.wait_ge(w_split, 4 * NT)

            def first(tt, c):
                k = tt * CHUNKS + c
                par = c % 2
                if not (isinstance(tt, int) and tt == 0 and c < 2):
                    pe.wait_ge(m_gelu, k - 1)
                w = slice(c * P, (c + 1) * P)
                for i, (wt, xs) in enumerate(((w1h, xh), (w1h, xl), (w1l, xh))):
                    for half in range(2):
                        o = tt * MT + half * 512
                        at = bass.ds(o, 512) if not isinstance(tt, int) else slice(o, o + 512)
                        mm = pe.matmul(ps[:, 2 * par + half, :], wt[:, w], xs[:, at], start=(i == 0), stop=(i == 2))
                mm.then_inc(m_w1, 1)

            def second(tt, c):
                k = tt * CHUNKS + c
                e, j = c // EC, c % EC
                if j == 0:
                    if not (isinstance(tt, int) and tt == 0 and e < 2):
                        pe.wait_ge(m_gy, tt * EXPERTS + e - 1)
                    if e == 1 and not (isinstance(tt, int) and tt == 0):
                        pe.wait_ge(m_out, tt)
                w = slice(c * P, (c + 1) * P)
                pe.wait_ge(m_hi, k + 1)
                for i, (wt, hs) in enumerate(((w2h, hh), (w2l, hh), (w2h, hl))):
                    if i == 2:
                        pe.wait_ge(m_lo, k + 1)
                    for half in range(2):
                        mm = pe.matmul(ps[:, 4 + 2 * (e % 2) + half, :], wt[:, w], hs[:, c % 4, half * 512:half * 512 + 512],
                                       start=(j == 0 and i == 0), stop=(j == EC - 1 and i == 2))
                mm.then_inc(m_w2, 1)

            def turn_sum(tt):
                pe.wait_ge(m_acc, (tt + 1) * EXPERTS)
                for half in range(2):
                    for j in range(4):
                        mm = pe.transpose(ps[:, 6 + half, j * P:(j + 1) * P],
                                          acc[:, half * 512 + j * P:half * 512 + (j + 1) * P], ident)
                    mm.then_inc(m_turn, 1)

            def steps_of(c):
                ops = [(first, c)] if c < CHUNKS else []
                return ops + ([(second, c - 2)] if c >= 2 else [])

            def experts(tt, start):
                for c in range(start, CHUNKS):
                    first(tt, c)
                    if c == 4 and not (isinstance(tt, int) and tt == 0):
                        turn_sum(tt - 1)
                    if c >= 2:
                        second(tt, c - 2)
                    elif not (isinstance(tt, int) and tt == 0):
                        second(tt - 1, CHUNKS - 2 + c)

            early = [op for c in range(6) for op in steps_of(c)] + [(first, c) for c in range(6, AHEAD)]
            first(0, 0)
            for i in range(2 * ROUNDS + 1):
                pe.wait_ge(s_parts, 1 + 3 * i)
                cols = 3 if i else 1
                pe.matmul(ps[:, 7, 0:cols], ones, small[:, 0:cols], start=True, stop=True).then_inc(s_counted, 1)
                if 1 + i < len(early):
                    op, c = early[1 + i]
                    op(0, c)
            pe.wait_ge(g_masked, 1)
            for half in range(2):
                mm = pe.transpose(ps[:, 7, half * P:(half + 1) * P], gy[:, GATES_AT + half * P:GATES_AT + (half + 1) * P], ident)
            mm.then_inc(g_turned, 1)
            first(0, AHEAD)
            pe.wait_ge(gates_ready, 1)
            for c in range(4, AHEAD - 1):
                second(0, c)
            experts(0, AHEAD + 1)
            with pe.Fori(1, NMT) as tt:
                experts(tt, 0)
            second(NMT - 1, CHUNKS - 2)
            second(NMT - 1, CHUNKS - 1)
            turn_sum(NMT - 1)


def kernel(**inputs):
    import concourse.bacc as _bacc
    from concourse.bass_utils import run_bass_kernel_spmd as _run

    a = {k: np.ascontiguousarray(v) for k, v in inputs.items()}
    f = np.float32
    weights = np.zeros((P, W_COLS), f)
    for at, name in ((W_K, "Wk"), (W_V, "Wv"), (W_R, "Wr"), (W_O0, "Wo")):
        weights[:, at:at + P] = a["L0_attn_" + name].T
    weights[:, W_O1:W_O1 + P] = a["L1_attn_W_O"]
    latent = np.zeros((32, L_COLS), f)
    latent[:, L_DQ:L_DQ + P] = a["L1_attn_W_DQ"].T
    latent[:, L_DKV:L_DKV + P] = a["L1_attn_W_DKV"].T
    latent[:, L_UV:L_UV + P] = a["L1_attn_W_UV"]
    for h in range(HEADS):
        o = h * SLOT
        latent[:, L_UQ + o:L_UQ + o + DH] = a["L1_attn_W_UQ"][:, h * DH:(h + 1) * DH]
        latent[:, L_UK + o:L_UK + o + DH] = a["L1_attn_W_UK"][:, h * DH:(h + 1) * DH]
        for p in range(DR // 2):
            for k in range(ROPE):
                col = o + DH + ROPE * p + k
                latent[:, L_UQ + col] = a["L1_attn_W_QR"][:, h * DR + 2 * p + Q_DIM[k]]
                weights[:, W_KROPE + col] = a["L1_attn_W_KR"][:, 2 * p + K_DIM[k]]
    vectors = np.zeros((P, V_COLS), f)
    for at, name in ((V_MK, "mix_k"), (V_MV, "mix_v"), (V_MR, "mix_r")):
        vectors[:, at] = a["L0_attn_" + name].reshape(C)
    vectors[:, V_DECAY] = np.repeat(a["L0_attn_time_decay"], DH)
    vectors[:SEQS * HEADS, V_HDECAY] = np.tile(a["L0_attn_time_decay"], SEQS)
    vectors[:, V_FIRST] = np.repeat(a["L0_attn_time_first"], DH)
    vectors[:, V_GATE:V_GATE + EXPERTS] = a["L1_ffn_gate_weight"].T
    vectors[:, V_B1:V_B1 + CHUNKS] = a["L1_ffn_b1"].reshape(CHUNKS, P).T
    vectors[:, V_B2:V_B2 + EXPERTS] = a["L1_ffn_b2"].T
    ints = np.concatenate([a["L0_ffn_w_gate"].T, a["L0_ffn_w_up"].T,
                           a["L0_ffn_w_down"].T.reshape(FJ, P, C).transpose(1, 0, 2).reshape(P, HIDDEN)], 1)
    w1 = a["L1_ffn_w1"].reshape(EXPERTS * HE, C).T
    w2 = a["L1_ffn_w2"].transpose(0, 2, 1).reshape(CHUNKS, P, C).transpose(1, 0, 2).reshape(P, CHUNKS * C)
    arrays = {"x_in": a["L0_attn_x"].reshape(N, C), "weights_in_dram": weights, "vectors_dram": vectors,
              "latent_dram": latent, "ints_dram": ints, "w1_dram": w1, "w2_dram": w2, "consts_dram": rope_tables()}
    arrays = {k: np.ascontiguousarray(v) for k, v in arrays.items()}
    nc = _bacc.Bacc("TRN2", target_bir_lowering=False, num_devices=1)
    args = [nc.dram_tensor(k, v.shape, mybir.dt.from_np(v.dtype), kind="ExternalInput").ap() for k, v in arrays.items()]
    args.append(nc.dram_tensor("out_dram", (N, C), F32, kind="ExternalOutput").ap())
    build(nc, *args)
    r = _run(nc, [arrays], core_ids=[0])
    return r.results[0]["out_dram"].reshape(BATCH, T, C)
```
